# Optimizing a Trainium2 kernel written in Bass

```python
import numpy as np
import jax
import jax.numpy as jnp

def _softmax(x, axis=-1):
    return jax.nn.softmax(x, axis=axis)

def _gelu(x):
    return jax.nn.gelu(x, approximate=True)

def _silu(x):
    return jax.nn.silu(x)

def _sigmoid(x):
    return jax.nn.sigmoid(x)

def _layernorm(x, axis=-1, eps=1e-05):
    m = jnp.mean(x, axis=axis, keepdims=True)
    v = jnp.var(x, axis=axis, keepdims=True)
    return (x - m) / jnp.sqrt(v + eps)

def _scatter_add(tgt, idx, src, axis=0):
    return tgt.at[idx].add(src)

def _segment_sum(src, seg, n):
    return jax.ops.segment_sum(src, seg, n)
kernel_name = 'mk_decoder_postln_d1_seqx_r4_7a6b06'

def setup_inputs(seed: int=0):
    np.random.seed(seed)
    _w = jnp.asarray

    def _rec_inputs():
        import jax
        import jax.numpy as jnp
        _rk = jax.random.key(seed)
        x = 7.22e-05 + 1 * jax.random.normal(jax.random.fold_in(_rk, 1), (16, 256, 512), jnp.float32)
        _lenS = 256 - jax.random.randint(jax.random.fold_in(_rk, 7), (16,), 0, max(1, 256 // 4) + 1, jnp.int32)
        _lenS2 = 256 - jax.random.randint(jax.random.fold_in(_rk, 8), (16,), 0, max(1, 256 // 4) + 1, jnp.int32)
        _ctx_2048P = jax.random.normal(jax.random.fold_in(_rk, 11), (16, 16, 512), jnp.float32)
        _ctx_2048c = jax.random.dirichlet(jax.random.fold_in(_rk, 511), 0.3 * jnp.ones((16,), jnp.float32), (16, 256))
        _ctx_2048t = jnp.einsum('bsk,bkd->bsd', _ctx_2048c, _ctx_2048P)
        _ctx_2048t = _ctx_2048t * jax.lax.rsqrt(jnp.mean(jnp.square(_ctx_2048t)) + 1e-12) * 0.953939
        ctx_2048 = 4.13588e-05 + 0.999923 * (_ctx_2048t + 0.3 * jax.random.normal(jax.random.fold_in(_rk, 611), (16, 256, 512), jnp.float32))
        return (x, ctx_2048)
    x, ctx_2048 = _rec_inputs()

    def _L0_attn_setup():
        import jax, jax.numpy as jnp
        import numpy as np
        EMBED_DIM = 512
        NUM_HEADS = 16
        HEAD_DIM = EMBED_DIM // NUM_HEADS // 2
        DEPTH = 12
        LAMBDA_INIT = 0.8 - 0.6 * float(np.exp(-0.3 * DEPTH))
        EPS = 1e-05
        key = jax.random.key(seed)
        ks = jax.random.split(key, 9)
        B, T, E = (2, 512, EMBED_DIM)
        s = 0.02
        return {'x': jax.random.normal(ks[0], (B, T, E), jnp.float32), 'Wq': jax.random.normal(ks[1], (E, E), jnp.float32) * s, 'Wk': jax.random.normal(ks[2], (E, E), jnp.float32) * s, 'Wv': jax.random.normal(ks[3], (E, E), jnp.float32) * s, 'Wo': jax.random.normal(ks[4], (E, E), jnp.float32) * s, 'lambda_q1': jax.random.normal(ks[5], (HEAD_DIM,), jnp.float32) * 0.1, 'lambda_k1': jax.random.normal(ks[6], (HEAD_DIM,), jnp.float32) * 0.1, 'lambda_q2': jax.random.normal(ks[7], (HEAD_DIM,), jnp.float32) * 0.1, 'lambda_k2': jax.random.normal(ks[8], (HEAD_DIM,), jnp.float32) * 0.1, 'subln_weight': jnp.ones((2 * HEAD_DIM,), jnp.float32)}
    _L0_attn_all = _L0_attn_setup()
    _L0_attn_in = {k: v for k, v in _L0_attn_all.items() if k in ('Wq', 'Wk', 'Wv', 'Wo', 'lambda_q1', 'lambda_k1', 'lambda_q2', 'lambda_k2', 'subln_weight')}
    del _L0_attn_all

    def _L0_xattn_setup():
        import jax, jax.numpy as jnp
        import numpy as np
        N_HEADS = 16
        K_CH = 256 // N_HEADS
        SCALE = 1.0 / np.sqrt(K_CH)
        key = jax.random.key(seed)
        ks = jax.random.split(key, 10)
        B, C, T = (4, 256, 512)
        Cout = 256
        xavier = lambda k, o, i: jax.random.uniform(k, (o, i), jnp.float32, -1.0, 1.0) * np.sqrt(6.0 / (o + i))
        return {'x': jax.random.normal(ks[0], (B, C, T), jnp.float32), 'c': jax.random.normal(ks[1], (B, C, T), jnp.float32), 'Wq': xavier(ks[2], C, C), 'bq': jnp.zeros((C,), jnp.float32), 'Wk': xavier(ks[3], C, C), 'bk': jnp.zeros((C,), jnp.float32), 'Wv': xavier(ks[4], C, C), 'bv': jnp.zeros((C,), jnp.float32), 'Wo': xavier(ks[5], Cout, C), 'bo': jnp.zeros((Cout,), jnp.float32)}
    _L0_xattn_all = _L0_xattn_setup()
    _L0_xattn_in = {k: v for k, v in _L0_xattn_all.items() if k in ('Wq', 'bq', 'Wk', 'bk', 'Wv', 'bv', 'Wo', 'bo')}
    del _L0_xattn_all

    def _L0_ffn_setup():
        import jax, jax.numpy as jnp
        import numpy as np
        D_MODEL = 512
        D_EXPERT = 2048
        EPS = 1e-08

        def ternary_quant(w):
            scale = jnp.mean(jnp.abs(w)) + EPS
            q = jnp.clip(jnp.round(w / scale), -1.0, 1.0) * scale
            return w + jax.lax.stop_gradient(q - w)
        key = jax.random.key(seed)
        k_x, k_up, k_gate, k_down = jax.random.split(key, 4)
        std_in = 1.0 / np.sqrt(D_MODEL)
        std_exp = 1.0 / np.sqrt(D_EXPERT)
        return {'x': jax.random.normal(k_x, (4, 512, D_MODEL), dtype=jnp.float32), 'W_up': jax.random.normal(k_up, (D_EXPERT, D_MODEL), dtype=jnp.float32) * std_in, 'W_gate': jax.random.normal(k_gate, (D_EXPERT, D_MODEL), dtype=jnp.float32) * std_in, 'W_down': jax.random.normal(k_down, (D_MODEL, D_EXPERT), dtype=jnp.float32) * std_exp}
    _L0_ffn_all = _L0_ffn_setup()
    _L0_ffn_in = {k: v for k, v in _L0_ffn_all.items() if k in ('W_up', 'W_gate', 'W_down')}
    del _L0_ffn_all
    return {'x': x, 'ctx_2048': ctx_2048, 'L0_attn_Wq': _L0_attn_in['Wq'], 'L0_attn_Wk': _L0_attn_in['Wk'], 'L0_attn_Wv': _L0_attn_in['Wv'], 'L0_attn_Wo': _L0_attn_in['Wo'], 'L0_attn_lambda_q1': _L0_attn_in['lambda_q1'], 'L0_attn_lambda_k1': _L0_attn_in['lambda_k1'], 'L0_attn_lambda_q2': _L0_attn_in['lambda_q2'], 'L0_attn_lambda_k2': _L0_attn_in['lambda_k2'], 'L0_attn_subln_weight': _L0_attn_in['subln_weight'], 'L0_xattn_Wq': _L0_xattn_in['Wq'], 'L0_xattn_bq': _L0_xattn_in['bq'], 'L0_xattn_Wk': _L0_xattn_in['Wk'], 'L0_xattn_bk': _L0_xattn_in['bk'], 'L0_xattn_Wv': _L0_xattn_in['Wv'], 'L0_xattn_bv': _L0_xattn_in['bv'], 'L0_xattn_Wo': _L0_xattn_in['Wo'], 'L0_xattn_bo': _L0_xattn_in['bo'], 'L0_ffn_W_up': _L0_ffn_in['W_up'], 'L0_ffn_W_gate': _L0_ffn_in['W_gate'], 'L0_ffn_W_down': _L0_ffn_in['W_down']}

def reference(x, ctx_2048, L0_attn_Wq, L0_attn_Wk, L0_attn_Wv, L0_attn_Wo, L0_attn_lambda_q1, L0_attn_lambda_k1, L0_attn_lambda_q2, L0_attn_lambda_k2, L0_attn_subln_weight, L0_xattn_Wq, L0_xattn_bq, L0_xattn_Wk, L0_xattn_bk, L0_xattn_Wv, L0_xattn_bv, L0_xattn_Wo, L0_xattn_bo, L0_ffn_W_up, L0_ffn_W_gate, L0_ffn_W_down):
    import jax
    import jax.numpy as jnp

    def _L0_attn_ref(x, Wq, Wk, Wv, Wo, lambda_q1, lambda_k1, lambda_q2, lambda_k2, subln_weight):
        import jax, jax.numpy as jnp
        import numpy as np
        EMBED_DIM = 512
        NUM_HEADS = 16
        HEAD_DIM = EMBED_DIM // NUM_HEADS // 2
        DEPTH = 12
        LAMBDA_INIT = 0.8 - 0.6 * float(np.exp(-0.3 * DEPTH))
        EPS = 1e-05
        B, T, E = x.shape
        H, hd = (NUM_HEADS, HEAD_DIM)
        scaling = hd ** (-0.5)
        q = (x @ Wq.T).reshape(B, T, H, 2, hd)
        k = (x @ Wk.T).reshape(B, T, H, 2, hd)
        v = (x @ Wv.T).reshape(B, T, H, 2 * hd)
        q1, q2 = (q[:, :, :, 0], q[:, :, :, 1])
        k1, k2 = (k[:, :, :, 0], k[:, :, :, 1])
        p1 = jax.nn.softmax(jnp.einsum('bthd,bshd->bhts', q1, k1) * scaling, axis=-1)
        p2 = jax.nn.softmax(jnp.einsum('bthd,bshd->bhts', q2, k2) * scaling, axis=-1)
        attn1 = jnp.einsum('bhts,bshe->bthe', p1, v)
        attn2 = jnp.einsum('bhts,bshe->bthe', p2, v)
        lambda_1 = jnp.exp(jnp.sum(lambda_q1 * lambda_k1))
        lambda_2 = jnp.exp(jnp.sum(lambda_q2 * lambda_k2))
        lambda_full = lambda_1 - lambda_2 + LAMBDA_INIT
        attn = attn1 - lambda_full * attn2
        rms = jax.lax.rsqrt(jnp.mean(attn * attn, axis=-1, keepdims=True) + EPS)
        attn = attn * rms * subln_weight
        attn = attn * (1.0 - LAMBDA_INIT)
        attn = attn.reshape(B, T, H * 2 * hd)
        return attn @ Wo.T

    def _L0_xattn_ref(x, c, Wq, bq, Wk, bk, Wv, bv, Wo, bo):
        import jax, jax.numpy as jnp
        import numpy as np
        N_HEADS = 16
        K_CH = 256 // N_HEADS
        SCALE = 1.0 / np.sqrt(K_CH)
        B, C, T = x.shape
        H, K = (N_HEADS, K_CH)
        q = jnp.einsum('oc,bct->bot', Wq, x) + bq[None, :, None]
        k = jnp.einsum('oc,bct->bot', Wk, c) + bk[None, :, None]
        v = jnp.einsum('oc,bct->bot', Wv, c) + bv[None, :, None]
        q = q.reshape(B, H, K, T)
        k = k.reshape(B, H, K, -1)
        v = v.reshape(B, H, K, -1)
        scores = jnp.einsum('bhkt,bhks->bhts', q, k) * SCALE
        p = jax.nn.softmax(scores, axis=-1)
        out = jnp.einsum('bhts,bhks->bhkt', p, v)
        out = out.reshape(B, H * K, T)
        return jnp.einsum('oc,bct->bot', Wo, out) + bo[None, :, None]

    def _L0_ffn_ref(x, W_up, W_gate, W_down):
        import jax, jax.numpy as jnp
        import numpy as np
        D_MODEL = 512
        D_EXPERT = 2048
        EPS = 1e-08

        def ternary_quant(w):
            scale = jnp.mean(jnp.abs(w)) + EPS
            q = jnp.clip(jnp.round(w / scale), -1.0, 1.0) * scale
            return w + jax.lax.stop_gradient(q - w)
        wu = ternary_quant(W_up)
        wg = ternary_quant(W_gate)
        wd = ternary_quant(W_down)
        up = jnp.einsum('bsd,ed->bse', x, wu)
        gate = jnp.einsum('bsd,ed->bse', x, wg)
        hidden = jax.nn.silu(up) * gate
        return jnp.einsum('bse,de->bsd', hidden, wd)
    x = _layernorm(x + _L0_attn_ref(x, L0_attn_Wq, L0_attn_Wk, L0_attn_Wv, L0_attn_Wo, L0_attn_lambda_q1, L0_attn_lambda_k1, L0_attn_lambda_q2, L0_attn_lambda_k2, L0_attn_subln_weight), axis=-1)
    x = _layernorm(x + _L0_xattn_ref(x, ctx_2048, L0_xattn_Wq, L0_xattn_bq, L0_xattn_Wk, L0_xattn_bk, L0_xattn_Wv, L0_xattn_bv, L0_xattn_Wo, L0_xattn_bo), axis=-1)
    x = _layernorm(x + _L0_ffn_ref(x, L0_ffn_W_up, L0_ffn_W_gate, L0_ffn_W_down), axis=-1)
    return x

_drawn_inputs = setup_inputs


def setup_inputs(seed=0):
    import zlib

    import numpy as np

    out = dict(_drawn_inputs(seed))
    spreads = {'L0_attn_subln_weight': (1.0, 0.6),
     'L0_xattn_bq': (0.0, 0.8),
     'L0_xattn_bk': (0.0, 2.0),
     'L0_xattn_bv': (0.0, 2.0),
     'L0_xattn_bo': (0.0, 2.0)}
    factors = {'L0_attn_lambda_q1': 30.727, 'L0_attn_lambda_q2': 200.0, 'L0_attn_lambda_k2': 7.664}
    for name, (base, spread) in spreads.items():
        noise = np.random.default_rng([zlib.crc32(name.encode()), seed]).standard_normal(out[name].shape)
        drawn = base * np.exp(spread * noise) if base else spread * noise
        out[name] = jnp.asarray(drawn.astype(out[name].dtype))
    for name, factor in factors.items():
        out[name] = (out[name] * factor).astype(out[name].dtype)
    return out
```

```python
from contextlib import ExitStack

import concourse.bass as bass
from concourse import mybir

f32, f16, f8 = mybir.dt.float32, mybir.dt.float16, mybir.dt.float8e4
ALU, ACT, AX = mybir.AluOpType, mybir.ActivationFunctionType, mybir.AxisListType

P = 128
NB, T, D = 16, 256, 512
TB, KB = T // P, D // P
HEADS = 16
HD = D // HEADS // 2
NM = 2 * HEADS
CH = T
HC = CH // HEADS
E = 2048
EB = E // P
EPS = 1e-5
Q_EPS = 1e-8
LAMBDA_INIT = 0.8 - 0.6 * 2.718281828459045 ** (-0.3 * 12)
SCALE = HD ** -0.5
W_UP = 256.0
P_SHIFT = 32.0
ROWS_A = 96
ROWS_B = 98
GROUPS = 8
GCOLS = 1024
CHUNK = 1024
A_ITEMS = {1: NM // GROUPS, 2: HEADS * KB // GROUPS}
CHUNKS = {1: NM // 2, 2: HEADS * 2}
PER_GROUP = {s: CHUNKS[s] // GROUPS for s in (1, 2)}
LOOK = {1: 3, 2: 2}
NG = 4
N32, NPH = 4, 4
AV_LAG = 3
D_PARTS = 4


def ffn_steps():
    steps = [("FT", 0), ("FT", 1)]
    for e in range(EB):
        steps.append(("UG", e))
        if e >= 1:
            steps.append(("UL", e - 1))
    steps.append(("UL", EB - 1))
    for tb in range(TB):
        for p in range(D_PARTS):
            steps.append(("DN", tb, p))
            if tb == 1 and p == 1:
                steps.append(("FN", 0))
        steps.append(("FV", tb))
    steps.append(("FN", 1))
    return steps


FFN = ffn_steps()


def units(steps):
    out = []
    for s in steps:
        if s[0] in ("FT", "UG", "DN"):
            out.append([])
        out[-1].append(s)
    return out


def batch_order():
    o, left = [], units(FFN)

    def fill(n):
        for _ in range(min(n, len(left))):
            o.extend(left.pop(0))

    def maxima(st, g):
        o.extend(("A", st, g * A_ITEMS[st] + i) for i in range(A_ITEMS[st]))
        o.append(("TM", st, g))
        o.append(("T", st, g))

    def attention(st, before, each):
        for g in range(LOOK[st]):
            maxima(st, g)
            fill(before)
        n, per = CHUNKS[st], PER_GROUP[st]
        share = A_ITEMS[st] // per
        for c in range(n + AV_LAG + 1):
            g = c // per + LOOK[st]
            if c < n:
                o.append(("S", st, c))
                if g < GROUPS:
                    at = g * A_ITEMS[st] + (c % per) * share
                    o.extend(("A", st, at + i) for i in range(share))
                o.append(("CAST", st, c))
                o.append(("SUB", st, c))
                if g < GROUPS and c % per == per - 1:
                    o.append(("TM", st, g))
                    o.append(("T", st, g))
            if each and c % each == each - 1:
                fill(1)
            if 0 <= c - AV_LAG < n:
                o.append(("AV", st, c - AV_LAG))
            done = c - AV_LAG - 1
            if 0 <= done < n:
                if st == 1:
                    o.append(("AVE", 1, done))
                    if done % 4 == 3:
                        o.append(("R1", done // 4))
                    if done % 4 == 0 and done >= 4:
                        o.append(("R1N", done // 4 - 1))
                elif done % 4 == 3:
                    o.append(("AVE", 2, done // 4))
                    if done % 16 == 15:
                        o.append(("R2", done // 16))
        if st == 1:
            fill(1)
            o.append(("R1N", 3))

    o.append(("LOAD",))
    o.append(("XS",))
    o.append(("CS",))
    fill(3)
    o.append(("QK", 0))
    o.append(("QK", 1))
    o.append(("VV",))
    o.append(("V2",))
    o.append(("K2",))
    attention(1, 1, 8)
    o.append(("AT",))
    fill(1)
    o.append(("OP",))
    o.append(("LN1",))
    fill(2)
    o.append(("X1",))
    o.append(("Q2",))
    fill(2)
    attention(2, 1, 3)
    o.append(("OT",))
    fill(1)
    o.append(("OP2",))
    fill(2)
    fill(len(left))
    o.append(("LN2",))
    return o


ORDER = batch_order()
FFN_KINDS = {s[0] for s in FFN}
B_ITEMS = [s for s in ORDER if s[0] in ("QK", "VV", "V2", "K2", "S", "AT", "OP", "Q2", "OT", "OP2")]
A_RING = [s for s in ORDER if s[0] in ("A", "T")]
AV_RING = [s for s in ORDER if s[0] == "AVE"]
F_RING = [s for s in FFN if s[0] in ("FT", "UG") or (s[0] == "DN" and s[2] == D_PARTS - 1)]
assert len(B_ITEMS) % 2 == 0 and len(A_RING) % 2 == 0
LINKS = {"TM": 1, "R1": 6, "R2": 1, "LN1": 2, "LN2": 2, "UG": 1, "FV": 2}


def cast_on_act(c):
    return c % 2 == 0


def sub_on_pool(c):
    return c % 4 != 3


def last_chunk(ave):
    _, st, i = ave
    return ("AV", st, i if st == 1 else 4 * i + 3)


class Signal:

    def __init__(self, sem, keys, step=1):
        self.sem, self.step, self.keys = sem, step, list(keys)
        self.place = {k: n + 1 for n, k in enumerate(self.keys)}
        assert len(self.place) == len(self.keys)

    def at(self, batch, key):
        return batch * (len(self.keys) * self.step) + self.place[key] * self.step


def decoder_kernel(nc, xT, x, ctx_in, wa, wx, w_ffn, sub_w, lam_in, b_qk, b_v, b_o, out):
    ctx = ExitStack()
    with ctx:
        def sb(name, shape, dt):
            return ctx.enter_context(nc.sbuf_tensor(name, shape, dt))

        def sem(name):
            return ctx.enter_context(nc.semaphore(name))

        area_ops = sb("area_ops", [P, 8192], f32)
        area_prob = sb("area_prob", [P, 8192], f32)
        area_act = sb("area_act", [P, 8192], f32)
        ops = area_ops[:, :].bitcast(f16)
        q_op, k_op = ops[:, 0:8192], ops[:, 8192:16384]
        prob32 = [area_prob[:, i * CHUNK:(i + 1) * CHUNK] for i in range(N32)]
        halves = area_prob[:, N32 * CHUNK:8192].bitcast(f16)
        prob_hi = [halves[:, 2 * i * CHUNK:(2 * i + 1) * CHUNK] for i in range(NPH)]
        prob_lo = [halves[:, (2 * i + 1) * CHUNK:(2 * i + 2) * CHUNK] for i in range(NPH)]
        hid_h = area_act[:, 0:2048].bitcast(f16)
        hid_l = area_act[:, 2048:4096].bitcast(f16)
        xr = area_act[:, 4096:5120].rearrange("p (b n) -> p b n", b=TB)
        x2 = area_act[:, 5120:6144].rearrange("p (b n) -> p b n", b=TB)
        attn = area_act[:, 6144:7168]
        work = area_act[:, 7168:8192]
        raw = [area_ops[:, :], area_prob[:, :], area_act[:, :]]

        w8 = sb("w8", [P, 3, 8192], f8)
        wa_h = sb("wa_h", [P, 4, KB, D], f16)
        wa_l = sb("wa_l", [P, 4, KB, D], f16)
        wx_h = sb("wx_h", [P, 4, TB, CH], f16)
        wx_l = sb("wx_l", [P, 4, TB, CH], f16)
        act_h = sb("act_h", [P, 1024], f16)
        act_l = sb("act_l", [P, 1024], f16)
        ctx_h = sb("ctx_h", [P, 1024], f16)
        ctx_l = sb("ctx_l", [P, 1024], f16)
        qk_h = sb("qk_h", [P, 2048], f16)
        qk_l = sb("qk_l", [P, 2048], f16)
        av1 = sb("av1", [P, TB, NM, 33], f32)
        av2 = av1[:, :, :, :].rearrange("p a b c -> p (a b c)")[:, 0:KB * HEADS * 17]\
            .rearrange("p (a b c) -> p a b c", a=KB, b=HEADS)
        v1 = sb("v1", [P, TB * HEADS, 65], f16)
        v2 = sb("v2", [P, KB * HEADS, 33], f16)
        fx_h = sb("fx_h", [P, 1024], f16)
        fx_l = sb("fx_l", [P, 1024], f16)
        tanh_b = sb("tanh_b", [P, 2, 256], f32)
        silu_b = sb("silu_b", [P, 256], f32)
        hid32 = sb("hid32", [P, 2, 256], f32)
        tmp1 = sb("tmp1", [P, 4, 33], f32)
        tmp2 = sb("tmp2", [P, 8, 17], f32)
        ident = sb("ident", [P, P], f32)
        ident16 = sb("ident16", [P, P], f16)
        bv_row = sb("bv_row", [P, CH], f32)
        mcol = sb("mcol", [P, NG, 8], f32)
        mhl = sb("mhl", [P, NG, 16], f16)
        mrow = sb("mrow", [16, NG, P], f16)
        rec = sb("rec", [P, 32], f32)
        msq = sb("msq", [P, 8], f32)
        rrms = sb("rrms", [P, 2, 8], f32)
        stats = sb("stats", [P, 2, TB, 6], f32)
        mv = sb("mv", [P, 2, TB, 2], f32)
        var = sb("var", [P, 2, TB], f32)
        rstd = sb("rstd", [P, 2, TB], f32)
        small = sb("small", [P, 32], f32)
        neg_half = small[:, 0:8]
        b_qk_sb = small[:, 8:12]
        b_o_sb = small[:, 12:14]
        sub_sb = small[:, 14:15]
        w_sc = small[:, 15:18]
        half_sc = small[:, 18:21]
        nhalf_sc = small[:, 21:24]
        asum = small[:, 24:27]
        nlam = small[:, 27:28]
        down_sc = small[:, 28:29]
        lam2 = small[:, 29:31]
        sub_s = small[:, 31:32]
        wait_col = sb("wait_col", [P, 2], f32)
        lam_sb = sb("lam_sb", [P, 64], f32)

        ps_a = ctx.enter_context(nc.psum_tensor("ps_a", [P, 2, 512], f32))
        ps_b = ctx.enter_context(nc.psum_tensor("ps_b", [P, 2, 1024], f32))
        ps_v = ctx.enter_context(nc.psum_tensor("ps_v", [P, 512], f32))
        ps_f = ctx.enter_context(nc.psum_tensor("ps_f", [P, 512], f32))
        slot_a = {s: n % 2 for n, s in enumerate(A_RING)}
        slot_b = {s: n % 2 for n, s in enumerate(B_ITEMS)}

        def bank_a(s):
            return ps_a[:, slot_a[s], :]

        def bank_b(s):
            return ps_b[:, slot_b[s], :]

        def keys(*kinds):
            return [s for s in ORDER if s[0] in kinds]

        chunks = keys("S")
        s_w = [sem(f"s_weights{i}") for i in range(4)]
        s_const = sem("s_const")
        s_set = sem("s_set")
        s_set_act = sem("s_set_act")
        s_set_pe = sem("s_set_pe")
        s_asum = sem("s_asum")
        s_chain = sem("s_chain")
        s_set_pool = sem("s_set_pool")
        xt_in = Signal(sem("xt_in"), ["x"], 16)
        ctx_loaded = Signal(sem("ctx_loaded"), ["x"], 16)
        x_in = Signal(sem("x_in"), ["x"], 16)
        ops1_in = [Signal(sem(f"ops1_in{i}"), ["x"], 128) for i in range(2)]
        ops2_in = Signal(sem("ops2_in"), ["x"], 128)
        max_in = [Signal(sem(f"max_in{i}"), [(st, g) for st in (1, 2) for g in range(i, GROUPS, NG)], 16)
                  for i in range(NG)]
        stored = Signal(sem("stored"), [0, 1], 16)
        a_full = Signal(sem("a_full"), A_RING)
        a_free = Signal(sem("a_free"), A_RING)
        b_full = Signal(sem("b_full"), B_ITEMS)
        exp_done = Signal(sem("exp_done"), chunks)
        av_full = Signal(sem("av_full"), keys("AV"))
        av_tmp = Signal(sem("av_tmp"), AV_RING)
        av_free = Signal(sem("av_free"), AV_RING)
        hi_done = Signal(sem("hi_done"), keys("XS", "CS", "QK", "VV", "V2", "K2", "AT", "X1", "Q2", "OT"))
        lo_done = Signal(sem("lo_done"), keys("XS", "CS", "QK", "VV", "V2", "K2", "AT", "X1", "Q2", "OT"))
        full_done = Signal(sem("full_done"), keys("V2", "K2", "Q2"))
        y_done = Signal(sem("y_done"), keys("LN1", "LN2"))
        cast_act = Signal(sem("cast_act"), [s for s in keys("CAST") if cast_on_act(s[2])])
        cast_dve = Signal(sem("cast_dve"), [s for s in keys("CAST") if not cast_on_act(s[2])])
        sub_pool = Signal(sem("sub_pool"), [s for s in keys("SUB") if sub_on_pool(s[2])])
        sub_dve = Signal(sem("sub_dve"), [s for s in keys("SUB") if not sub_on_pool(s[2])])
        max_split = Signal(sem("max_split"), keys("TM"))
        ms_done = Signal(sem("ms_done"), keys("R1"))
        rms_done = Signal(sem("rms_done"), keys("R1"))
        attn_done = Signal(sem("attn_done"), keys("R1N", "R2"))
        var_done = Signal(sem("var_done"), keys("LN1", "LN2"))
        rstd_done = Signal(sem("rstd_done"), keys("LN1", "LN2"))
        norm_done = Signal(sem("norm_done"), keys("LN1", "LN2"))
        link = Signal(sem("link"), [(s, k) for s in ORDER if s[0] not in FFN_KINDS for k in range(LINKS.get(s[0], 0))])

        f_full = Signal(sem("f_full"), F_RING)
        fx_hi = Signal(sem("fx_hi"), [s for s in FFN if s[0] == "FT"])
        fx_lo = Signal(sem("fx_lo"), [s for s in FFN if s[0] == "FT"])
        tanh_done = Signal(sem("tanh_done"), range(EB))
        hid_done = Signal(sem("hid_done"), range(EB))
        hid_hi = Signal(sem("hid_hi"), range(EB))
        hid_lo = Signal(sem("hid_lo"), range(EB))
        fy_done = Signal(sem("fy_done"), range(TB))
        fvar_done = Signal(sem("fvar_done"), range(TB))
        frstd_done = Signal(sem("frstd_done"), range(TB))
        f_out = Signal(sem("f_out"), range(TB))
        flink = Signal(sem("flink"), [(s, k) for s in FFN for k in range(LINKS.get(s[0], 0))])

        def cast_of(st, c):
            return (cast_act if cast_on_act(c) else cast_dve), ("CAST", st, c)

        def sub_of(st, c):
            return (sub_pool if sub_on_pool(c) else sub_dve), ("SUB", st, c)

        def b_release(s):
            if s[0] == "S":
                return exp_done, s
            if s[0] in ("V2", "K2", "Q2"):
                return full_done, s
            if s[0] in ("OP", "OP2"):
                return y_done, ("LN1",) if s[0] == "OP" else ("LN2",)
            return lo_done, s

        def f_release(s):
            return {"FT": (fx_lo, s), "UG": (hid_done, s[1]), "DN": (fy_done, s[1])}[s[0]]

        def wait_last(eng, signal, batch, key):
            if not isinstance(batch, int) or batch > 0:
                eng.wait_ge(signal.sem, signal.at(batch - 1, key))

        def chunk_index(st, c):
            return c if st == 1 else CHUNKS[1] + c

        def chunk_before(st, c, n):
            i = chunk_index(st, c) - n
            if i < 0:
                i += len(chunks)
                return (chunks[i][1], chunks[i][2]), False
            return (chunks[i][1], chunks[i][2]), True

        block = ctx.enter_context(nc.Block())

        def run(eng, attention, feed_forward):
            for s in ORDER:
                if s[0] not in FFN_KINDS:
                    attention(0, s)
            with eng.Fori(1, NB) as b:
                for s in ORDER:
                    if s[0] in FFN_KINDS:
                        feed_forward(b - 1, s)
                    else:
                        attention(b, s)
            for s in FFN:
                feed_forward(NB - 1, s)

        @block.sync
        def _(sp):
            sp.dma_start(raw[0], wa).then_inc(s_w[0], 16)
            sp.dma_start(raw[1][:, 0:2048], wx).then_inc(s_w[0], 16)
            sp.dma_start(sub_sb, sub_w).then_inc(s_const, 16)
            sp.dma_start(b_qk_sb, b_qk).then_inc(s_const, 16)
            sp.dma_start(b_o_sb, b_o).then_inc(s_const, 16)
            sp.dma_start(bv_row[:, :], b_v.partition_broadcast(P)).then_inc(s_const, 16)
            sp.dma_start(lam_sb[:, :], lam_in.partition_broadcast(P)).then_inc(s_const, 16)
            sp.dma_start(raw[2], w_ffn[2]).then_inc(s_w[3], 16)
            sp.wait_ge(s_set, 1)
            sp.dma_start(raw[0], w_ffn[0]).then_inc(s_w[1], 16)
            sp.wait_ge(s_set, 2)
            sp.dma_start(raw[1], w_ffn[1]).then_inc(s_w[2], 16)
            sp.wait_ge(s_set, 5)

            def attention(b, s):
                if s[0] == "LOAD":
                    wait_last(sp, b_full, b, ("OT",))
                    sp.dma_start(attn.rearrange("p (k t) -> p k t", k=KB), xT[b, :, :, :]).then_inc(xt_in.sem, 16)
                    sp.dma_start(work.rearrange("p (k t) -> p k t", k=TB),
                                 ctx_in[b, :, :].rearrange("(k p) t -> p k t", p=P)).then_inc(ctx_loaded.sem, 16)
                    wait_last(sp, norm_done, b, ("LN2",))
                    sp.dma_start(xr, x[b, :, :].rearrange("(k p) t -> p k t", p=P)).then_inc(x_in.sem, 16)
                elif s[0] == "QK":
                    i = s[1]
                    if i == 0:
                        wait_last(sp, b_full, b, ("S", 2, CHUNKS[2] - 1))
                        if isinstance(b, int):
                            sp.wait_ge(s_set_pool, 7)
                    sp.wait_ge(hi_done.sem, hi_done.at(b, s))
                    sp.wait_ge(lo_done.sem, lo_done.at(b, s))
                    for which, op in ((0, q_op), (1, k_op)):
                        for r, half in enumerate((qk_h, qk_l, qk_h, qk_l) if which == 0 else (qk_h, qk_l, qk_l, qk_h)):
                            src = half[:, i * 1024:(i + 1) * 1024].rearrange("p (c w t) -> p c w t", c=2, w=2)
                            sp.dma_start(op[16 * r:16 * r + 16, i * 4096:(i + 1) * 4096], src[:, :, which, :])\
                                .then_inc(ops1_in[i].sem, 16)
                elif s[0] in ("K2", "Q2"):
                    sp.wait_ge(hi_done.sem, hi_done.at(b, s))
                    sp.wait_ge(lo_done.sem, lo_done.at(b, s))
                    if s[0] == "Q2":
                        hi, lo, op = qk_h, qk_l, q_op
                        for r, half in enumerate((hi, lo, hi, lo)):
                            sp.dma_start(op[16 * r:16 * r + 16, :], half[:, 0:1024].rearrange("p (c t) -> p c t", c=2))\
                                .then_inc(ops2_in.sem, 16)
                elif s[0] == "AT":
                    sp.wait_ge(b_full.sem, b_full.at(b, ("S", 1, CHUNKS[1] - 1)))
                    for r, half in enumerate((ctx_h, ctx_l, ctx_l, ctx_h)):
                        sp.dma_start(k_op[16 * r:16 * r + 16, :], half[:, :].rearrange("p (c t) -> p c t", c=2))\
                            .then_inc(ops2_in.sem, 16)
                elif s[0] == "T":
                    st, g = s[1], s[2]
                    sp.wait_ge(a_free.sem, a_free.at(b, s))
                    sp.dma_start(q_op[96:98, g * GCOLS:(g + 1) * GCOLS], mrow[:, g % NG, :])\
                        .then_inc(max_in[g % NG].sem, 16)

            def feed_forward(b, s):
                if s[0] == "FN":
                    tb = s[1]
                    sp.wait_ge(f_out.sem, f_out.at(b, tb))
                    sp.dma_start(out[b, tb * P:(tb + 1) * P, :], x2[:, tb, :]).then_inc(stored.sem, 16)

            run(sp, attention, feed_forward)
            sp.wait_ge(stored.sem, NB * 2 * 16)

        @block.tensor
        def _(pe):
            pe.wait_ge(s_set_pool, 3)
            for i, w in enumerate((2, 0, 1)):
                pe.wait_ge(s_asum, i + 1)
                pe.matmul(ps_a[:, 0, i:i + 1], silu_b[:, 0:P], asum[:, w:w + 1], start=True, stop=True)\
                    .then_inc(s_set_pe, 1)

            def product(dst, lhs, rhs, n):
                for k in range(n):
                    (lh, ll), (rh, rl) = lhs(k), rhs(k)
                    for j, (a, c) in enumerate(((lh, rh), (lh, rl), (ll, rh))):
                        last = pe.matmul(dst, a, c, start=k == 0 and j == 0, stop=k == n - 1 and j == 2)
                return last

            def b_slot(b, s):
                n = B_ITEMS.index(s)
                signal, key = b_release(B_ITEMS[n - 2])
                if n >= 2:
                    pe.wait_ge(signal.sem, signal.at(b, key))
                else:
                    wait_last(pe, signal, b, key)

            def a_slot(b, s):
                n = A_RING.index(s)
                if n >= 2:
                    pe.wait_ge(a_free.sem, a_free.at(b, A_RING[n - 2]))
                else:
                    wait_last(pe, a_free, b, A_RING[n - 2])

            def attention(b, s):
                kind = s[0]
                if kind in ("QK", "VV", "V2", "K2", "AT", "OP", "Q2", "OT", "OP2", "S"):
                    b_slot(b, s)
                    dst = bank_b(s)
                if kind == "QK":
                    pe.wait_ge(lo_done.sem, lo_done.at(b, ("XS",)))
                    pe.wait_ge(hi_done.sem, hi_done.at(b, ("XS",)))
                    for c in range(2):
                        cb = 2 * s[1] + c
                        for w in range(2):
                            last = product(dst[:, c * 512 + w * 256:c * 512 + w * 256 + 256],
                                           lambda k: (wa_h[:, w, k, cb * P:(cb + 1) * P], wa_l[:, w, k, cb * P:(cb + 1) * P]),
                                           lambda k: (act_h[:, k * T:(k + 1) * T], act_l[:, k * T:(k + 1) * T]), KB)
                    last.then_inc(b_full.sem, 1)
                elif kind == "VV":
                    for tb in range(TB):
                        last = product(dst[:, tb * 512:(tb + 1) * 512],
                                       lambda k: (act_h[:, k * T + tb * P:k * T + tb * P + P], act_l[:, k * T + tb * P:k * T + tb * P + P]),
                                       lambda k: (wa_h[:, 2, k, :], wa_l[:, 2, k, :]), KB)
                    last.then_inc(b_full.sem, 1)
                elif kind == "V2":
                    pe.wait_ge(lo_done.sem, lo_done.at(b, ("CS",)))
                    pe.wait_ge(hi_done.sem, hi_done.at(b, ("CS",)))
                    for tb in range(KB):
                        last = product(dst[:, tb * 256:(tb + 1) * 256],
                                       lambda k: (ctx_h[:, k * D + tb * P:k * D + tb * P + P], ctx_l[:, k * D + tb * P:k * D + tb * P + P]),
                                       lambda k: (wx_h[:, 2, k, :], wx_l[:, 2, k, :]), TB)
                    last.then_inc(b_full.sem, 1)
                elif kind in ("K2", "Q2", "OP2"):
                    w, hi, lo = {"K2": (1, ctx_h, ctx_l), "Q2": (0, act_h, act_l), "OP2": (3, act_h, act_l)}[kind]
                    if kind != "K2":
                        src = ("X1",) if kind == "Q2" else ("OT",)
                        pe.wait_ge(lo_done.sem, lo_done.at(b, src))
                        pe.wait_ge(hi_done.sem, hi_done.at(b, src))
                    for ob in range(TB):
                        last = product(dst[:, ob * 512:(ob + 1) * 512],
                                       lambda k: (wx_h[:, w, k, ob * P:(ob + 1) * P], wx_l[:, w, k, ob * P:(ob + 1) * P]),
                                       lambda k: (hi[:, k * D:(k + 1) * D], lo[:, k * D:(k + 1) * D]), TB)
                    last.then_inc(b_full.sem, 1)
                elif kind == "A":
                    st, i = s[1], s[2]
                    a_slot(b, s)
                    if st == 1 and i % 16 == 0:
                        pe.wait_ge(ops1_in[i // 16].sem, ops1_in[i // 16].at(b, "x"))
                    if st == 2 and i == 0:
                        pe.wait_ge(ops2_in.sem, ops2_in.at(b, "x"))
                    bank = bank_a(s)
                    if st == 1:
                        for tb in range(TB):
                            last = pe.matmul(bank[:, tb * T:(tb + 1) * T],
                                             q_op[0:ROWS_A, i * T + tb * P:i * T + tb * P + P],
                                             k_op[0:ROWS_A, i * T:(i + 1) * T], start=True, stop=True)
                    else:
                        h = i // KB
                        last = pe.matmul(bank, q_op[0:ROWS_A, i * P:(i + 1) * P],
                                         k_op[0:ROWS_A, h * D:(h + 1) * D], start=True, stop=True)
                    last.then_inc(a_full.sem, 1)
                elif kind == "T":
                    st, g = s[1], s[2]
                    a_slot(b, s)
                    pe.wait_ge(max_split.sem, max_split.at(b, ("TM", st, g)))
                    pe.transpose(bank_a(s).bitcast(f16)[0:16, 0:P], mhl[:, g % NG, :], ident16[:, :])\
                        .then_inc(a_full.sem, 1)
                elif kind == "S":
                    st, c = s[1], s[2]
                    g = c // PER_GROUP[st]
                    if c % PER_GROUP[st] == 0:
                        pe.wait_ge(max_in[g % NG].sem, max_in[g % NG].at(b, (st, g)))
                    for j in range(2):
                        if st == 1:
                            m = 2 * c + j
                            for kb in range(TB):
                                last = pe.matmul(dst[:, j * 512 + kb * T:j * 512 + (kb + 1) * T],
                                                 k_op[0:ROWS_B, m * T + kb * P:m * T + kb * P + P],
                                                 q_op[0:ROWS_B, m * T:(m + 1) * T], start=True, stop=True)
                        else:
                            h, kb = c // 2, 2 * (c % 2) + j
                            last = pe.matmul(dst[:, j * 512:(j + 1) * 512],
                                             k_op[0:ROWS_B, h * D + kb * P:h * D + kb * P + P],
                                             q_op[0:ROWS_B, h * D:(h + 1) * D], start=True, stop=True)
                    last.then_inc(b_full.sem, 1)
                elif kind == "AV":
                    st, c = s[1], s[2]
                    first = st == 1 or c % 4 == 0
                    if first:
                        n = AV_RING.index(("AVE", st, c if st == 1 else c // 4))
                        if n >= 1:
                            pe.wait_ge(av_free.sem, av_free.at(b, AV_RING[n - 1]))
                        else:
                            wait_last(pe, av_free, b, AV_RING[-1])
                    if c == 0:
                        need = ("VV",) if st == 1 else ("V2",)
                        pe.wait_ge(hi_done.sem, hi_done.at(b, need))
                        pe.wait_ge(lo_done.sem, lo_done.at(b, need))
                    signal, key = cast_of(st, c)
                    pe.wait_ge(signal.sem, signal.at(b, key))
                    signal, key = sub_of(st, c)
                    pe.wait_ge(signal.sem, signal.at(b, key))
                    buf = chunk_index(st, c) % NPH
                    start = first
                    for j in range(2):
                        for tb in range(TB if st == 1 else KB):
                            for kb in range(TB if st == 1 else 1):
                                for part in (prob_hi, prob_lo):
                                    if st == 1:
                                        col, r = j * 512 + kb * T + tb * P, j * TB + tb
                                        rhs, width = v1[:, kb * HEADS + c, :], 65
                                    else:
                                        col, r = j * 512 + tb * P, ((c // 2) % 2) * KB + tb
                                        rhs, width = v2[:, (2 * (c % 2) + j) * HEADS + c // 2, :], 33
                                    last = pe.matmul(ps_v[:, r * width:(r + 1) * width], part[buf][:, col:col + P],
                                                     rhs, start=start, stop=True, skip_group_check=True)
                                    start = False
                    last.then_inc(av_full.sem, 1)
                elif kind == "AT":
                    pe.wait_ge(attn_done.sem, attn_done.at(b, ("R1N", 3)))
                    for cb in range(KB):
                        for tb in range(TB):
                            last = pe.transpose(dst[:, cb * T + tb * P:cb * T + tb * P + P],
                                                attn[:, tb * D + cb * P:tb * D + cb * P + P], ident[:, :])
                    last.then_inc(b_full.sem, 1)
                elif kind == "OP":
                    pe.wait_ge(lo_done.sem, lo_done.at(b, ("AT",)))
                    pe.wait_ge(hi_done.sem, hi_done.at(b, ("AT",)))
                    for tb in range(TB):
                        last = product(dst[:, tb * 512:(tb + 1) * 512],
                                       lambda k: (act_h[:, k * T + tb * P:k * T + tb * P + P], act_l[:, k * T + tb * P:k * T + tb * P + P]),
                                       lambda k: (wa_h[:, 3, k, :], wa_l[:, 3, k, :]), KB)
                    last.then_inc(b_full.sem, 1)
                elif kind == "OT":
                    pe.wait_ge(attn_done.sem, attn_done.at(b, ("R2", 1)))
                    for cb in range(TB):
                        for tb in range(KB):
                            last = pe.transpose(dst[:, cb * D + tb * P:cb * D + tb * P + P],
                                                attn[:, tb * CH + cb * P:tb * CH + cb * P + P], ident[:, :])
                    last.then_inc(b_full.sem, 1)

            def f_slot(b, s):
                n = F_RING.index(s)
                signal, key = f_release(F_RING[n - 1])
                if n >= 1:
                    pe.wait_ge(signal.sem, signal.at(b, key))

            def take_wait():
                pe.matmul(ps_f[:, 0:1], ident16[:, :], ident16[:, 0:1], start=True, stop=True)

            def feed_forward(b, s):
                kind = s[0]
                if kind == "FT":
                    i = s[1]
                    f_slot(b, s)
                    if i == 0:
                        pe.wait_ge(norm_done.sem, norm_done.at(b, ("LN2",)))
                    for k in range(2):
                        for tb in range(TB):
                            last = pe.transpose(ps_f[:, k * T + tb * P:k * T + tb * P + P],
                                                x2[:, tb, (2 * i + k) * P:(2 * i + k + 1) * P], ident[:, :])
                    last.then_inc(f_full.sem, 1)
                elif kind == "UG":
                    e = s[1]
                    f_slot(b, s)
                    if e == 0:
                        pe.wait_ge(fx_hi.sem, fx_hi.at(b, ("FT", 1)))
                    take_wait()
                    for w in range(2):
                        for k in range(KB):
                            for half in (fx_h, fx_l):
                                last = pe.matmul(ps_f[:, w * T:(w + 1) * T], w8[:, w, k * E + e * P:k * E + e * P + P],
                                                 half[:, k * T:(k + 1) * T],
                                                 start=k == 0 and half is fx_h, stop=k == KB - 1 and half is fx_l)
                    last.then_inc(f_full.sem, 1)
                elif kind == "DN":
                    tb, p = s[1], s[2]
                    n = EB // D_PARTS
                    if p == 0:
                        f_slot(b, ("DN", tb, D_PARTS - 1))
                        if tb == 0:
                            pe.wait_ge(hid_hi.sem, hid_hi.at(b, EB - 1))
                            pe.wait_ge(hid_lo.sem, hid_lo.at(b, EB - 1))
                        take_wait()
                    for e in range(p * n, (p + 1) * n):
                        for half in (hid_h, hid_l):
                            last = pe.matmul(ps_f[:, :], half[:, e * T + tb * P:e * T + tb * P + P],
                                             w8[:, 2, e * D:(e + 1) * D], start=e == 0 and half is hid_h,
                                             stop=e == EB - 1 and half is hid_l)
                    if p == D_PARTS - 1:
                        last.then_inc(f_full.sem, 1)

            run(pe, attention, feed_forward)

        @block.scalar
        def _(act):
            act.wait_ge(s_w[0], 32)
            act.wait_ge(s_const, 80)
            for w in range(4):
                src = raw[0][:, w * 2048:(w + 1) * 2048]
                dst = wa_h[:, w, :, :].rearrange("p k n -> p (k n)")
                if w == 3:
                    act.wait_ge(s_set_pool, 4)
                act.activation(dst, src, ACT.Copy, scale=sub_s if w == 3 else W_UP)
            act.activation(wx_h[:, :, :, :].rearrange("p w k n -> p (w k n)"), raw[1][:, 0:2048], ACT.Copy, scale=W_UP)\
                .then_inc(s_set_act, 1)
            act.wait_ge(s_set, 3)
            act.activation(lam2, lam2, ACT.Exp).then_inc(s_set_act, 1)

            def attention(b, s):
                kind = s[0]
                if kind in ("XS", "CS"):
                    if kind == "XS":
                        wait_last(act, b_full, b, ("OP2",))
                        act.wait_ge(xt_in.sem, xt_in.at(b, "x"))
                        dst, src = act_h, attn
                    else:
                        wait_last(act, ops2_in, b, "x")
                        act.wait_ge(ctx_loaded.sem, ctx_loaded.at(b, "x"))
                        dst, src = ctx_h, work
                    act.activation(dst[:, :], src, ACT.Copy).then_inc(hi_done.sem, 1)
                elif kind == "QK":
                    act.wait_ge(b_full.sem, b_full.at(b, s))
                    act.activation(qk_h[:, s[1] * 1024:(s[1] + 1) * 1024], bank_b(s), ACT.Copy, scale=1 / W_UP)\
                        .then_inc(hi_done.sem, 1)
                elif kind == "VV":
                    act.wait_ge(b_full.sem, b_full.at(b, s))
                    act.activation(v1[:, :, 32:64], bank_b(s).rearrange("p (h e) -> p h e", e=32), ACT.Copy,
                                   scale=1 / W_UP).then_inc(hi_done.sem, 1)
                elif kind == "V2":
                    act.wait_ge(full_done.sem, full_done.at(b, s))
                    act.activation(v2[:, :, 16:32], work.rearrange("p (h e) -> p h e", e=16), ACT.Copy)\
                        .then_inc(hi_done.sem, 1)
                elif kind in ("K2", "Q2"):
                    act.wait_ge(full_done.sem, full_done.at(b, s))
                    dst = ctx_h[:, :] if kind == "K2" else qk_h[:, 0:1024]
                    act.activation(dst, work, ACT.Copy).then_inc(hi_done.sem, 1)
                elif kind in ("AT", "OT"):
                    act.wait_ge(b_full.sem, b_full.at(b, s))
                    act.activation(act_h[:, :], bank_b(s), ACT.Copy).then_inc(hi_done.sem, 1)
                elif kind == "X1":
                    act.wait_ge(norm_done.sem, norm_done.at(b, ("LN1",)))
                    act.activation(act_h[:, :], xr.rearrange("p b n -> p (b n)"), ACT.Copy).then_inc(hi_done.sem, 1)
                elif kind == "S":
                    st, c = s[1], s[2]
                    act.wait_ge(b_full.sem, b_full.at(b, s))
                    before, same = chunk_before(st, c, N32)
                    signal, key = sub_of(*before)
                    if same:
                        act.wait_ge(signal.sem, signal.at(b, key))
                    else:
                        wait_last(act, signal, b, key)
                    act.activation(prob32[chunk_index(st, c) % N32], bank_b(s), ACT.Exp, scale=SCALE)\
                        .then_inc(exp_done.sem, 1)
                elif kind == "CAST" and cast_on_act(s[2]):
                    st, c = s[1], s[2]
                    cast_chunk(act, b, st, c).then_inc(cast_act.sem, 1)
                elif kind == "AVE":
                    act.wait_ge(av_full.sem, av_full.at(b, last_chunk(s)))
                    n = AV_RING.index(s)
                    if n >= 1:
                        act.wait_ge(av_free.sem, av_free.at(b, AV_RING[n - 1]))
                    else:
                        wait_last(act, av_free, b, AV_RING[-1])
                    if s[1] == 1:
                        act.activation(tmp1[:, :, 0:32], ps_v[:, 0:260].rearrange("p (r e) -> p r e", e=65)[:, :, 0:32],
                                       ACT.Copy).then_inc(av_tmp.sem, 1)
                    else:
                        act.activation(tmp2[:, :, 0:16], ps_v[:, 0:264].rearrange("p (r e) -> p r e", e=33)[:, :, 0:16],
                                       ACT.Copy).then_inc(av_tmp.sem, 1)

            def cast_chunk(eng, b, st, c):
                eng.wait_ge(exp_done.sem, exp_done.at(b, ("S", st, c)))
                before, same = chunk_before(st, c, NPH)
                if same:
                    eng.wait_ge(av_full.sem, av_full.at(b, ("AV", *before)))
                else:
                    wait_last(eng, av_full, b, ("AV", *before))
                i = chunk_index(st, c)
                return eng.activation(prob_hi[i % NPH], prob32[i % N32], ACT.Copy)

            def feed_forward(b, s):
                if s[0] == "FT":
                    act.wait_ge(f_full.sem, f_full.at(b, s))
                    act.activation(fx_h[:, s[1] * 512:(s[1] + 1) * 512], ps_f[:, :], ACT.Copy).then_inc(fx_hi.sem, 1)
                elif s[0] == "UG":
                    e = s[1]
                    act.wait_ge(f_full.sem, f_full.at(b, s))
                    if e >= 2:
                        act.wait_ge(hid_done.sem, hid_done.at(b, e - 2))
                    act.activation(tanh_b[:, e % 2, :], ps_f[:, 0:T], ACT.Tanh, scale=half_sc[:, 0:1])\
                        .then_inc(tanh_done.sem, 1)
                elif s[0] == "UL":
                    e = s[1]
                    act.wait_ge(hid_done.sem, hid_done.at(b, e))
                    act.activation(hid_h[:, e * T:(e + 1) * T], hid32[:, e % 2, :], ACT.Copy).then_inc(hid_hi.sem, 1)

            run(act, attention, feed_forward)

        @block.gpsimd
        def _(pool):
            pool.memset(small[:, 0:8], -0.5)
            pool.memset(silu_b[:, 0:P], 1.0)
            pool.memset(tmp1[:, :, :], 0.0)
            pool.memset(tmp2[:, :, :], 0.0)
            pool.memset(v1[:, :, 64:65], 1.0)
            pool.memset(v2[:, :, 32:33], 1.0)
            pool.memset(ident[:, :], 0.0)
            pool.memset(ident16[:, :], 0.0).then_inc(s_set_pool, 1)
            pool.wait_ge(s_set_pool, 1)
            for m in (ident, ident16):
                pool.affine_select(out=m[:, :], in_=m[:, :], compare_op=ALU.not_equal, fill=1.0, base=0,
                                   pattern=[[-1, P]], channel_multiplier=1).then_inc(s_set_pool, 1)
            pool.wait_ge(s_const, 80)
            pool.tensor_scalar(sub_s, sub_sb, W_UP * (1.0 - LAMBDA_INIT), None, ALU.mult).then_inc(s_set_pool, 1)
            pool.wait_ge(s_set, 5)
            pool.memset(q_op[64:96, :], 0.0).then_inc(s_set_pool, 1)
            pool.memset(k_op[64:96, :], 0.0).then_inc(s_set_pool, 1)
            pool.memset(k_op[96:98, :], -1.0).then_inc(s_set_pool, 1)

            def attention(b, s):
                if s[0] == "SUB" and sub_on_pool(s[2]):
                    st, c = s[1], s[2]
                    signal, key = cast_of(st, c)
                    pool.wait_ge(signal.sem, signal.at(b, key))
                    i = chunk_index(st, c)
                    pool.tensor_tensor(prob_lo[i % NPH], prob32[i % N32], prob_hi[i % NPH], ALU.subtract)\
                        .then_inc(sub_pool.sem, 1)
                elif s[0] == "R1":
                    pool.wait_ge(ms_done.sem, ms_done.at(b, s))
                    pool.tensor_tensor(rrms[:, s[1] % 2, :], msq[:, :], neg_half, ALU.pow).then_inc(rms_done.sem, 1)
                elif s[0] in ("LN1", "LN2"):
                    pool.wait_ge(var_done.sem, var_done.at(b, s))
                    pool.tensor_tensor(rstd[:, 0, :], var[:, 0, :], neg_half[:, 0:2], ALU.pow).then_inc(rstd_done.sem, 1)

            def feed_forward(b, s):
                if s[0] == "FV":
                    tb = s[1]
                    pool.wait_ge(fvar_done.sem, fvar_done.at(b, tb))
                    pool.tensor_tensor(rstd[:, 1, tb:tb + 1], var[:, 1, tb:tb + 1], neg_half[:, 0:1], ALU.pow)\
                        .then_inc(frstd_done.sem, 1)

            run(pool, attention, feed_forward)

        @block.vector
        def _(dve):
            steps = [0]

            def setup_step(ins):
                steps[0] += 1
                ins.then_inc(s_set, 1)
                dve.wait_ge(s_set, steps[0])

            dve.wait_ge(s_set_act, 1)
            for w in range(4):
                src = raw[0][:, w * 2048:(w + 1) * 2048]
                hi = wa_h[:, w, :, :].rearrange("p k n -> p (k n)")
                lo = wa_l[:, w, :, :].rearrange("p k n -> p (k n)")
                last = dve.scalar_tensor_tensor(out=lo, in0=src, scalar=sub_s if w == 3 else W_UP, in1=hi,
                                                op0=ALU.mult, op1=ALU.subtract)
            setup_step(last)
            setup_step(dve.scalar_tensor_tensor(
                out=wx_l[:, :, :, :].rearrange("p w k n -> p (w k n)"), in0=raw[1][:, 0:2048], scalar=W_UP,
                in1=wx_h[:, :, :, :].rearrange("p w k n -> p (w k n)"), op0=ALU.mult, op1=ALU.subtract))
            dve.wait_ge(s_const, 80)
            lam = lam_sb[:, :].rearrange("p (s b d) -> p s b d", s=2, b=2)
            chain = [0]

            def chained(ins):
                chain[0] += 1
                ins.then_inc(s_chain, 1)
                dve.wait_ge(s_chain, chain[0])

            chained(dve.tensor_tensor(lam[:, 0, :, :], lam[:, 0, :, :], lam[:, 1, :, :], ALU.mult))
            setup_step(dve.tensor_reduce(lam2, lam[:, 0, :, :], AX.X, ALU.add))
            dve.wait_ge(s_set_act, 2)
            chained(dve.tensor_scalar(nlam, lam2[:, 1:2], LAMBDA_INIT, None, ALU.subtract))
            chained(dve.tensor_tensor(nlam, nlam, lam2[:, 0:1], ALU.subtract))
            for n, w in enumerate((2, 0, 1)):
                dve.wait_ge(s_w[1 + w], 16)
                dve.tensor_reduce(asum[:, w:w + 1], raw[w], AX.X, ALU.add, apply_absolute_value=True)\
                    .then_inc(s_asum, 1)
                dve.wait_ge(s_set_pe, 1 + n)
                chained(dve.tensor_scalar(w_sc[:, w:w + 1], ps_a[:, 0, n:n + 1], 1.0 / (D * E), Q_EPS, ALU.mult, ALU.add))
                chained(dve.tensor_scalar(half_sc[:, w:w + 1], w_sc[:, w:w + 1], 0.5, None, ALU.mult))
                chained(dve.tensor_scalar(nhalf_sc[:, w:w + 1], w_sc[:, w:w + 1], -0.5, None, ALU.mult))
                chained(dve.tensor_scalar(w8[:, w, :], raw[w], nhalf_sc[:, w:w + 1], None, ALU.is_lt, saturate=False))
                last = dve.scalar_tensor_tensor(out=w8[:, w, :], in0=raw[w], scalar=half_sc[:, w:w + 1],
                                                in1=w8[:, w, :], op0=ALU.is_gt, op1=ALU.subtract, saturate=False)
                chained(last)
            chained(dve.tensor_tensor(down_sc, w_sc[:, 0:1], w_sc[:, 1:2], ALU.mult))
            chained(dve.tensor_tensor(down_sc, down_sc, w_sc[:, 2:3], ALU.mult))
            setup_step(dve.tensor_scalar(down_sc, down_sc, 8.0, None, ALU.mult))
            setup_step(dve.memset(msq[:, :], 1.0))

            def linked(b, s, k, ins, signal=None):
                signal = signal or link
                ins.then_inc(signal.sem, 1)
                dve.wait_ge(signal.sem, signal.at(b, (s, k)))

            def layer_norm(b, s, k0, src, part, blocks, signal, ready):
                for tb in blocks:
                    last = dve.bn_stats(stats[:, part, tb, :], src[:, tb, :])
                linked(b, s, k0, last, signal)
                dve.memset(wait_col[:, part:part + 1], 0.0)
                for tb in blocks:
                    last = dve.bn_aggr(mv[:, part, tb, :], stats[:, part, tb, :])
                linked(b, s, k0 + 1, last, signal)
                dve.tensor_scalar(var[:, part, blocks[0]:blocks[-1] + 1], mv[:, part, blocks[0]:blocks[-1] + 1, 1],
                                  EPS, None, ALU.add).then_inc(ready.sem, 1)

            def attention(b, s):
                kind = s[0]
                if kind in ("XS", "CS", "AT", "OT", "X1", "K2", "Q2", "V2", "QK", "VV"):
                    n = lo_done.keys.index(s)
                    if n >= 1:
                        dve.wait_ge(lo_done.sem, lo_done.at(b, lo_done.keys[n - 1]))
                    else:
                        wait_last(dve, lo_done, b, lo_done.keys[-1])
                    if kind in ("K2", "Q2"):
                        dve.wait_ge(b_full.sem, b_full.at(b, s))
                        for ob in range(TB):
                            i = ob + (TB if kind == "K2" else 0)
                            last = dve.tensor_scalar(work[:, ob * 512:(ob + 1) * 512], bank_b(s)[:, ob * 512:(ob + 1) * 512],
                                                     1 / W_UP, b_qk_sb[:, i:i + 1], ALU.mult, ALU.add)
                        last.then_inc(full_done.sem, 1)
                    elif kind == "V2":
                        dve.wait_ge(b_full.sem, b_full.at(b, s))
                        dve.scalar_tensor_tensor(
                            out=work.rearrange("p (k n) -> p k n", k=KB), in0=bank_b(s).rearrange("p (k n) -> p k n", k=KB),
                            scalar=1 / W_UP, in1=bv_row[:, :].unsqueeze(1).to_broadcast([P, KB, CH]),
                            op0=ALU.mult, op1=ALU.add).then_inc(full_done.sem, 1)
                    dve.wait_ge(hi_done.sem, hi_done.at(b, s))
                    if kind == "XS":
                        ins = dve.tensor_tensor(act_l[:, :], attn, act_h[:, :], ALU.subtract)
                    elif kind == "CS":
                        ins = dve.tensor_tensor(ctx_l[:, :], work, ctx_h[:, :], ALU.subtract)
                    elif kind == "QK":
                        cols = slice(s[1] * 1024, (s[1] + 1) * 1024)
                        ins = dve.scalar_tensor_tensor(out=qk_l[:, cols], in0=bank_b(s), scalar=1 / W_UP,
                                                       in1=qk_h[:, cols], op0=ALU.mult, op1=ALU.subtract)
                    elif kind == "VV":
                        ins = dve.scalar_tensor_tensor(out=v1[:, :, 0:32], in0=bank_b(s).rearrange("p (h e) -> p h e", e=32),
                                                       scalar=1 / W_UP, in1=v1[:, :, 32:64], op0=ALU.mult, op1=ALU.subtract)
                    elif kind == "V2":
                        ins = dve.tensor_tensor(v2[:, :, 0:16], work.rearrange("p (h e) -> p h e", e=16), v2[:, :, 16:32],
                                                ALU.subtract)
                    elif kind == "K2":
                        ins = dve.tensor_tensor(ctx_l[:, :], work, ctx_h[:, :], ALU.subtract)
                    elif kind == "Q2":
                        ins = dve.tensor_tensor(qk_l[:, 0:1024], work, qk_h[:, 0:1024], ALU.subtract)
                    elif kind in ("AT", "OT"):
                        ins = dve.tensor_tensor(act_l[:, :], bank_b(s), act_h[:, :], ALU.subtract)
                    else:
                        ins = dve.tensor_tensor(act_l[:, :], xr.rearrange("p b n -> p (b n)"), act_h[:, :], ALU.subtract)
                    ins.then_inc(lo_done.sem, 1)
                    if kind == "X1":
                        dve.wait_ge(lo_done.sem, lo_done.at(b, s))
                        for tb in range(TB):
                            dve.tensor_scalar(xr[:, tb, :], xr[:, tb, :], b_o_sb[:, tb:tb + 1], None, ALU.add)
                elif kind == "A":
                    st, i = s[1], s[2]
                    g, n = divmod(i, A_ITEMS[st])
                    dve.wait_ge(a_full.sem, a_full.at(b, s))
                    if st == 1:
                        dve.tensor_reduce(mcol[:, g % NG, 2 * n:2 * n + 2], bank_a(s).rearrange("p (t k) -> p t k", t=TB),
                                          AX.X, ALU.max).then_inc(a_free.sem, 1)
                    else:
                        dve.tensor_reduce(mcol[:, g % NG, n:n + 1], bank_a(s), AX.X, ALU.max).then_inc(a_free.sem, 1)
                elif kind == "TM":
                    st, g = s[1], s[2]
                    dve.wait_ge(a_free.sem, a_free.at(b, ("A", st, (g + 1) * A_ITEMS[st] - 1)))
                    linked(b, s, 0, dve.tensor_scalar(mhl[:, g % NG, 0:8], mcol[:, g % NG, :], -P_SHIFT, None, ALU.add))
                    dve.scalar_tensor_tensor(out=mhl[:, g % NG, 8:16], in0=mcol[:, g % NG, :], scalar=-P_SHIFT,
                                             in1=mhl[:, g % NG, 0:8], op0=ALU.add, op1=ALU.subtract)\
                        .then_inc(max_split.sem, 1)
                elif kind == "T":
                    st, g = s[1], s[2]
                    dve.wait_ge(a_full.sem, a_full.at(b, s))
                    dve.tensor_copy(mrow[:, g % NG, :], bank_a(s).bitcast(f16)[0:16, 0:P]).then_inc(a_free.sem, 1)
                elif kind == "CAST" and not cast_on_act(s[2]):
                    st, c = s[1], s[2]
                    dve.wait_ge(exp_done.sem, exp_done.at(b, ("S", st, c)))
                    before, same = chunk_before(st, c, NPH)
                    if same:
                        dve.wait_ge(av_full.sem, av_full.at(b, ("AV", *before)))
                    else:
                        wait_last(dve, av_full, b, ("AV", *before))
                    i = chunk_index(st, c)
                    dve.tensor_copy(prob_hi[i % NPH], prob32[i % N32]).then_inc(cast_dve.sem, 1)
                elif kind == "SUB" and not sub_on_pool(s[2]):
                    st, c = s[1], s[2]
                    signal, key = cast_of(st, c)
                    dve.wait_ge(signal.sem, signal.at(b, key))
                    i = chunk_index(st, c)
                    dve.tensor_tensor(prob_lo[i % NPH], prob32[i % N32], prob_hi[i % NPH], ALU.subtract)\
                        .then_inc(sub_dve.sem, 1)
                elif kind == "AVE":
                    dve.wait_ge(av_tmp.sem, av_tmp.at(b, s))
                    if s[1] == 1:
                        c = s[2]
                        dst = av1[:, :, 2 * c:2 * c + 2, :].rearrange("p t m e -> p m t e")
                        src = ps_v[:, 0:260].rearrange("p (m t e) -> p m t e", m=2, t=TB)[:, :, :, 32:65]
                        tmp = tmp1[:, :, :].rearrange("p (m t) e -> p m t e", m=2)
                    else:
                        g = s[2]
                        dst = av2[:, :, 2 * g:2 * g + 2, :].rearrange("p t m e -> p m t e")
                        src = ps_v[:, 0:264].rearrange("p (m t e) -> p m t e", m=2, t=KB)[:, :, :, 16:33]
                        tmp = tmp2[:, :, :].rearrange("p (m t) e -> p m t e", m=2)
                    dve.tensor_tensor(dst, src, tmp, ALU.add).then_inc(av_free.sem, 1)
                elif kind == "R1":
                    q = s[1]
                    dve.wait_ge(av_free.sem, av_free.at(b, ("AVE", 1, 4 * q + 3)))
                    av = av1[:, :, 8 * q:8 * q + 8, :]
                    r = rec[:, 0:16].rearrange("p (t m) -> p t m", t=TB)
                    odd = rec[:, 0:16].rearrange("p (t h two) -> p t h two", t=TB, two=2)[:, :, :, 1]
                    linked(b, s, 0, dve.reciprocal(r, av[:, :, :, 32]))
                    linked(b, s, 1, dve.tensor_scalar(odd, odd, nlam, None, ALU.mult))
                    linked(b, s, 2, dve.tensor_tensor(av[:, :, :, 0:32], av[:, :, :, 0:32],
                                                      r.unsqueeze(3).to_broadcast([P, TB, 8, 32]), ALU.mult))
                    pair = av.rearrange("p t (h two) e -> p t h two e", two=2)
                    dst = attn_heads(q)
                    linked(b, s, 3, dve.tensor_tensor(dst, pair[:, :, :, 0, 0:32], pair[:, :, :, 1, 0:32], ALU.add))
                    sq = work[:, 0:256].rearrange("p (t h e) -> p t h e", t=TB, h=4)
                    linked(b, s, 4, dve.tensor_tensor(sq, dst, dst, ALU.mult))
                    linked(b, s, 5, dve.tensor_reduce(msq[:, :].rearrange("p (t h) -> p t h", t=TB), sq, AX.X, ALU.add))
                    dve.tensor_scalar(msq[:, :], msq[:, :], 1.0 / 32, EPS, ALU.mult, ALU.add).then_inc(ms_done.sem, 1)
                elif kind == "R1N":
                    q = s[1]
                    dve.wait_ge(rms_done.sem, rms_done.at(b, ("R1", q)))
                    dst = attn_heads(q)
                    dve.tensor_tensor(dst, dst, rrms[:, q % 2, :].rearrange("p (t h) -> p t h", t=TB).unsqueeze(3)
                                      .to_broadcast([P, TB, 4, 32]), ALU.mult).then_inc(attn_done.sem, 1)
                elif kind == "R2":
                    half = s[1]
                    dve.wait_ge(av_free.sem, av_free.at(b, ("AVE", 2, 4 * half + 3)))
                    av = av2[:, :, 8 * half:8 * half + 8, :]
                    r = rec[:, :].rearrange("p (t h) -> p t h", t=KB)
                    linked(b, s, 0, dve.reciprocal(r, av[:, :, :, 16]))
                    dst = attn.rearrange("p (t h e) -> p t h e", t=KB, h=HEADS)[:, :, 8 * half:8 * half + 8, :]
                    dve.tensor_tensor(dst, av[:, :, :, 0:16], r.unsqueeze(3).to_broadcast([P, KB, 8, 16]), ALU.mult)\
                        .then_inc(attn_done.sem, 1)
                elif kind in ("LN1", "LN2"):
                    item = ("OP",) if kind == "LN1" else ("OP2",)
                    dve.wait_ge(b_full.sem, b_full.at(b, item))
                    if kind == "LN1":
                        dve.wait_ge(x_in.sem, x_in.at(b, "x"))
                    for tb in range(TB):
                        last = dve.scalar_tensor_tensor(out=xr[:, tb, :], in0=bank_b(item)[:, tb * 512:(tb + 1) * 512],
                                                        scalar=1 / W_UP, in1=xr[:, tb, :], op0=ALU.mult, op1=ALU.add)
                    last.then_inc(y_done.sem, 1)
                    dve.wait_ge(y_done.sem, y_done.at(b, s))
                    layer_norm(b, s, 0, xr, 0, (0, 1), link, var_done)
                    dve.wait_ge(rstd_done.sem, rstd_done.at(b, s))
                    if kind == "LN2":
                        wait_last(dve, stored, b, 1)
                    dst = xr if kind == "LN1" else x2
                    for tb in range(TB):
                        last = dve.tensor_scalar(dst[:, tb, :], xr[:, tb, :], mv[:, 0, tb, 0:1], rstd[:, 0, tb:tb + 1],
                                                 ALU.subtract, ALU.mult)
                    last.then_inc(norm_done.sem, 1)

            def attn_heads(q):
                return attn.rearrange("p (t h e) -> p t h e", t=TB, h=HEADS)[:, :, 4 * q:4 * q + 4, :]

            def feed_forward(b, s):
                kind = s[0]
                if kind == "FT":
                    cols = slice(s[1] * 512, (s[1] + 1) * 512)
                    dve.wait_ge(fx_hi.sem, fx_hi.at(b, s))
                    dve.tensor_tensor(fx_l[:, cols], ps_f[:, :], fx_h[:, cols], ALU.subtract).then_inc(fx_lo.sem, 1)
                elif kind == "UG":
                    e = s[1]
                    dve.wait_ge(tanh_done.sem, tanh_done.at(b, e))
                    linked(b, s, 0, dve.scalar_tensor_tensor(out=silu_b[:, :], in0=tanh_b[:, e % 2, :], scalar=1.0,
                                                             in1=ps_f[:, 0:T], op0=ALU.add, op1=ALU.mult), flink)
                    if e >= 2:
                        dve.wait_ge(hid_hi.sem, hid_hi.at(b, e - 2))
                    dve.scalar_tensor_tensor(out=hid32[:, e % 2, :], in0=ps_f[:, T:2 * T], scalar=1.0 / 16,
                                             in1=silu_b[:, :], op0=ALU.mult, op1=ALU.mult).then_inc(hid_done.sem, 1)
                elif kind == "UL":
                    e = s[1]
                    dve.wait_ge(hid_hi.sem, hid_hi.at(b, e))
                    dve.tensor_tensor(hid_l[:, e * T:(e + 1) * T], hid32[:, e % 2, :], hid_h[:, e * T:(e + 1) * T],
                                      ALU.subtract).then_inc(hid_lo.sem, 1)
                elif kind == "FV":
                    tb = s[1]
                    dve.wait_ge(f_full.sem, f_full.at(b, ("DN", tb, D_PARTS - 1)))
                    dve.scalar_tensor_tensor(out=x2[:, tb, :], in0=ps_f[:, :], scalar=down_sc, in1=x2[:, tb, :],
                                             op0=ALU.mult, op1=ALU.add).then_inc(fy_done.sem, 1)
                    dve.wait_ge(fy_done.sem, fy_done.at(b, tb))
                    layer_norm(b, s, 0, x2, 1, (tb,), flink, fvar_done)
                elif kind == "FN":
                    tb = s[1]
                    dve.wait_ge(frstd_done.sem, frstd_done.at(b, tb))
                    dve.tensor_scalar(x2[:, tb, :], x2[:, tb, :], mv[:, 1, tb, 0:1], rstd[:, 1, tb:tb + 1],
                                      ALU.subtract, ALU.mult).then_inc(f_out.sem, 1)

            run(dve, attention, feed_forward)


def kernel(**inputs):
    import numpy as np
    import concourse.bacc as bacc
    from concourse.bass_utils import run_bass_kernel_spmd

    a = {k: np.asarray(v) for k, v in inputs.items()}

    def rows_first(w):
        wt = w.T
        n = wt.shape[0] // P
        return np.ascontiguousarray(wt.reshape(n, P, wt.shape[1]).transpose(1, 0, 2)).reshape(P, -1)

    def channel_order(matrices):
        order = np.empty((matrices // 8, HD, 8), np.int64)
        for cb in range(matrices // 8):
            for j in range(8):
                m = (cb // 2) * 16 + j * 2 + cb % 2
                order[cb, :, j] = m * HD + np.arange(HD)
        return order.reshape(-1)

    c1, c2 = channel_order(NM), channel_order(HEADS)
    L, X = "L0_attn_", "L0_xattn_"
    arrays = {
        "xT": np.ascontiguousarray(a["x"].transpose(0, 2, 1).reshape(NB, KB, P, T).transpose(0, 2, 1, 3)),
        "x": a["x"],
        "ctx_in": a["ctx_2048"],
        "wa": np.concatenate([rows_first(a[L + "Wq"][c1]), rows_first(a[L + "Wk"][c1]), rows_first(a[L + "Wv"]),
                              rows_first(a[L + "Wo"])], axis=1),
        "wx": np.concatenate([rows_first(a[X + "Wq"][c2]), rows_first(a[X + "Wk"][c2]), rows_first(a[X + "Wv"]),
                              rows_first(a[X + "Wo"])], axis=1),
        "w_ffn": np.stack([rows_first(a["L0_ffn_W_up"]), rows_first(a["L0_ffn_W_gate"]),
                           rows_first(a["L0_ffn_W_down"])]),
        "sub_w": np.tile(a[L + "subln_weight"], P // 32).reshape(P, 1),
        "lam_in": np.concatenate([a[L + "lambda_q1"], a[L + "lambda_q2"], a[L + "lambda_k1"], a[L + "lambda_k2"]]),
        "b_qk": np.ascontiguousarray(np.concatenate([a[X + "bq"][c2].reshape(TB, P).T, a[X + "bk"][c2].reshape(TB, P).T], axis=1)),
        "b_v": a[X + "bv"],
        "b_o": np.ascontiguousarray(a[X + "bo"].reshape(TB, P).T),
    }
    nc = bacc.Bacc("TRN2", target_bir_lowering=False, num_devices=1)
    args = [nc.dram_tensor(f"in_{k}", v.shape, f32, kind="ExternalInput").ap() for k, v in arrays.items()]
    args.append(nc.dram_tensor("out_0", (NB, T, D), f32, kind="ExternalOutput").ap())
    decoder_kernel(nc, *args)
    r = run_bass_kernel_spmd(nc, [{f"in_{k}": v for k, v in arrays.items()}], core_ids=[0])
    return r.results[0]["out_0"]
```

```python
from contextlib import ExitStack

import concourse.bass as bass
from concourse import mybir

f32, f16, f8 = mybir.dt.float32, mybir.dt.float16, mybir.dt.float8e4
ALU, ACT, AX = mybir.AluOpType, mybir.ActivationFunctionType, mybir.AxisListType

P = 128
NB, T, D = 16, 256, 512
TB, KB = T // P, D // P
HEADS = 16
HD = D // HEADS // 2
NM = 2 * HEADS
CH = T
HC = CH // HEADS
E = 2048
EB = E // P
EPS = 1e-5
Q_EPS = 1e-8
LAMBDA_INIT = 0.8 - 0.6 * 2.718281828459045 ** (-0.3 * 12)
SCALE = HD ** -0.5
W_UP = 256.0
P_SHIFT = 32.0
ROWS_A = 96
ROWS_B = 98
GROUPS = 8
GCOLS = 1024
CHUNK = 1024
A_ITEMS = {1: NM // GROUPS, 2: HEADS * KB // GROUPS}
CHUNKS = {1: NM // 2, 2: HEADS * 2}
PER_GROUP = {s: CHUNKS[s] // GROUPS for s in (1, 2)}
LOOK = {1: 3, 2: 2}
NG = 4
N32, NPH = 4, 4
AV_LAG = 3
D_PARTS = 4


def ffn_steps():
    steps = [("LN2",), ("FT",)]
    for e in range(EB // 2):
        steps.append(("UG", e))
        if e >= 1:
            steps.append(("UL", e - 1))
    steps.append(("UL", EB // 2 - 1))
    for tb in range(TB):
        for p in range(D_PARTS):
            steps.append(("DN", tb, p))
            if tb == 1 and p == 1:
                steps.append(("FN", 0))
        steps.append(("FV", tb))
    steps.append(("FN", 1))
    return steps


FFN = ffn_steps()


def units(steps):
    out = []
    for s in steps:
        if s[0] in ("LN2", "FT", "UG", "DN"):
            out.append([])
        out[-1].append(s)
    return out


def batch_order():
    o, left = [], units(FFN)

    def fill(n=1):
        for _ in range(min(n, len(left))):
            o.extend(left.pop(0))

    def attention(st, before, every):
        for g in range(LOOK[st]):
            o.extend(("A", st, g * A_ITEMS[st] + i) for i in range(A_ITEMS[st]))
            o.append(("TM", st, g))
            fill(before[g])
            o.append(("T", st, g))
        n, per = CHUNKS[st], PER_GROUP[st]
        share = A_ITEMS[st] // per
        late = {}
        for c in range(n + AV_LAG + 2):
            g = c // per + LOOK[st]
            if c < n:
                o.append(("S", st, c))
            o.extend(late.pop(c, []))
            if c < n and g < GROUPS:
                at = g * A_ITEMS[st] + (c % per) * share
                o.extend(("A", st, at + i) for i in range(share))
                if c % per == per - 1:
                    o.append(("TM", st, g))
                    late.setdefault(c + 1, []).append(("T", st, g))
            if 1 <= c <= n:
                o.append(("CAST", st, c - 1))
                o.append(("SUB", st, c - 1))
            if c in every:
                fill()
            done = c - AV_LAG
            if 0 <= done < n:
                o.append(("AV", st, done))
                if st == 1:
                    o.append(("AVE", 1, done))
                    if done % 4 == 3:
                        late.setdefault(c + 1, []).append(("R1", done // 4))
                        late.setdefault(c + 2, []).append(("R1N", done // 4))
                elif done % 4 == 3:
                    o.append(("AVE", 2, done // 4))
                    if done % 16 == 15:
                        late.setdefault(c + 1, []).append(("R2", done // 16))
        if late:
            fill()
        for k in sorted(late):
            o.extend(late[k])

    o += [("LOAD",), ("CS",), ("V2",), ("XS",)]
    fill()
    o += [("LOADX",), ("QK", 0), ("K2",), ("QK", 1)]
    fill()
    o += [("VV",)]
    fill(1)
    attention(1, (1, 0, 0), (6, 12))
    o.append(("AT",))
    fill(1)
    o.append(("OP",))
    o.append(("LN1",))
    fill(2)
    o.append(("X1",))
    o.append(("Q2",))
    fill(1)
    attention(2, (1, 0), (4, 8, 12, 16, 20, 24, 28, 31))
    o += [("OT",), ("GAP",), ("OP2",)]
    assert not left, left
    return o


ORDER = batch_order()
FFN_KINDS = {s[0] for s in FFN}
B_ITEMS = [s for s in ORDER if s[0] in ("QK", "VV", "V2", "K2", "S", "AT", "OP", "Q2", "OT", "OP2", "FT", "UG", "GAP")]
A_RING = [s for s in ORDER if s[0] in ("A", "T")]
AV_RING = [s for s in ORDER if s[0] == "AVE"]
SUMS = [("R1", q) for q in range(4)] + [("R2", h) for h in range(2)]
assert len(B_ITEMS) % 2 == 0 and len(A_RING) % 2 == 0 and len(SUMS) % 2 == 0
LAST_IN_SLOT = {n: [s for s in B_ITEMS[n::2] if s[0] != "GAP"][-1] for n in range(2)}
assert all(s[0] not in FFN_KINDS for s in LAST_IN_SLOT.values())
LINKS = {"TM": 1, "R1": 6, "R2": 1, "LN1": 2, "LN2": 2, "UG": 1, "FV": 2}


def cast_on_act(st, c):
    return True


def sub_on_pool(st, c):
    return c % 4 != 3


def sums_item(ave):
    _, st, i = ave
    return ("R1", i // 4) if st == 1 else ("R2", i // 4)


class Signal:

    def __init__(self, sem, keys, step=1, base=0):
        self.sem, self.step, self.keys, self.base = sem, step, list(keys), base
        self.place = {k: n + 1 for n, k in enumerate(self.keys)}
        assert len(self.place) == len(self.keys)

    def at(self, batch, key):
        return batch * (len(self.keys) * self.step) + (self.place[key] * self.step + self.base)


def decoder_kernel(nc, xT, x, ctx_in, wa, wx, w_ffn, sub_w, lam_in, b_qk, b_v, b_o, out):
    ctx = ExitStack()
    with ctx:
        def sb(name, shape, dt):
            return ctx.enter_context(nc.sbuf_tensor(name, shape, dt))

        def sem(name):
            return ctx.enter_context(nc.semaphore(name))

        area_ops = sb("area_ops", [P, 8192], f32)
        area_prob = sb("area_prob", [P, 8192], f32)
        area_act = sb("area_act", [P, 8192], f32)
        ops = area_ops[:, :].bitcast(f16)
        q_op, k_op = ops[:, 0:8192], ops[:, 8192:16384]
        prob32 = [area_prob[:, i * CHUNK:(i + 1) * CHUNK] for i in range(N32)]
        halves = area_prob[:, N32 * CHUNK:8192].bitcast(f16)
        prob_hi = [halves[:, 2 * i * CHUNK:(2 * i + 1) * CHUNK] for i in range(NPH)]
        prob_lo = [halves[:, (2 * i + 1) * CHUNK:(2 * i + 2) * CHUNK] for i in range(NPH)]
        hid_h = area_act[:, 0:2048].bitcast(f16)
        hid_l = area_act[:, 2048:4096].bitcast(f16)
        xr = area_act[:, 4096:5120].rearrange("p (b n) -> p b n", b=TB)
        x2 = area_act[:, 5120:6144].rearrange("p (b n) -> p b n", b=TB)
        attn = area_act[:, 6144:7168]
        work = area_act[:, 7168:8192]
        av = work[:, 512:1024]
        raw = [area_ops[:, :], area_prob[:, :], area_act[:, :]]

        w8 = sb("w8", [P, 3, 8192], f8)
        wa_h = sb("wa_h", [P, 4, KB, D], f16)
        wa_l = sb("wa_l", [P, 4, KB, D], f16)
        wx_h = sb("wx_h", [P, 4, TB, CH], f16)
        wx_l = sb("wx_l", [P, 4, TB, CH], f16)
        act_h = sb("act_h", [P, 1024], f16)
        act_l = sb("act_l", [P, 1024], f16)
        ctx_h = sb("ctx_h", [P, 1024], f16)
        ctx_l = sb("ctx_l", [P, 1024], f16)
        qk_h = sb("qk_h", [P, 2048], f16)
        qk_l = sb("qk_l", [P, 2048], f16)
        sums = sb("sums", [P, 2, 1056], f32)
        v1 = sb("v1", [P, TB * HEADS, 65], f16)
        v2 = sb("v2", [P, KB * HEADS, 33], f16)
        fx_h = sb("fx_h", [P, 1024], f16)
        fx_l = sb("fx_l", [P, 1024], f16)
        tanh_b = sb("tanh_b", [P, 2, 256], f32)
        hid32 = sb("hid32", [P, 2, 2, 256], f32)
        ones = hid32[:, 0, 0, 0:P]
        ident = sb("ident", [P, P], f32)
        ident16 = sb("ident16", [P, P], f16)
        bv_row = sb("bv_row", [P, CH], f32)
        mcol = sb("mcol", [P, NG, 8], f32)
        mhl = sb("mhl", [P, NG, 16], f16)
        mrow = sb("mrow", [16, NG, P], f16)
        rec = sb("rec", [P, 32], f32)
        msq = sb("msq", [P, 8], f32)
        rrms = sb("rrms", [P, 2, 8], f32)
        stats = sb("stats", [P, 2, TB, 6], f32)
        mv = sb("mv", [P, 2, TB, 2], f32)
        var = sb("var", [P, 2, TB], f32)
        rstd = sb("rstd", [P, 2, TB], f32)
        small = sb("small", [P, 32], f32)
        neg_half = small[:, 0:8]
        b_qk_sb = small[:, 8:12]
        b_o_sb = small[:, 12:14]
        sub_sb = small[:, 14:15]
        w_sc = small[:, 15:18]
        half_sc = small[:, 18:21]
        nhalf_sc = small[:, 21:24]
        asum = small[:, 24:27]
        nlam = small[:, 27:28]
        down_sc = small[:, 28:29]
        lam2 = small[:, 29:31]
        sub_s = small[:, 31:32]
        wait_col = sb("wait_col", [P, 2], f32)
        lam_sb = sb("lam_sb", [P, 64], f32)

        ps_a = ctx.enter_context(nc.psum_tensor("ps_a", [P, 2, 512], f32))
        ps_b = ctx.enter_context(nc.psum_tensor("ps_b", [P, 2, 1024], f32))
        ps_v = ctx.enter_context(nc.psum_tensor("ps_v", [P, 512], f32))
        ps_f = ctx.enter_context(nc.psum_tensor("ps_f", [P, 512], f32))
        slot_a = {s: n % 2 for n, s in enumerate(A_RING)}
        slot_b = {s: n % 2 for n, s in enumerate(B_ITEMS)}

        def bank_a(s):
            return ps_a[:, slot_a[s], :]

        def bank_b(s):
            return ps_b[:, slot_b[s], :]

        def keys(*kinds):
            return [s for s in ORDER if s[0] in kinds]

        chunks = keys("S")
        s_w = [sem(f"s_weights{i}") for i in range(4)]
        s_const = sem("s_const")
        s_set = sem("s_set")
        s_set_act = sem("s_set_act")
        s_set_pe = sem("s_set_pe")
        s_asum = sem("s_asum")
        s_chain = sem("s_chain")
        s_set_pool = sem("s_set_pool")
        xt_in = Signal(sem("xt_in"), ["x"], 16)
        ctx_loaded = Signal(sem("ctx_loaded"), ["x"], 16)
        x_in = Signal(sem("x_in"), ["x"], 16)
        ops1_in = [Signal(sem(f"ops1_in{i}"), ["x"], 128) for i in range(2)]
        ops2_in = Signal(sem("ops2_in"), ["x"], 128)
        max_in = [Signal(sem(f"max_in{i}"), [(st, g) for st in (1, 2) for g in range(i, GROUPS, NG)], 16)
                  for i in range(NG)]
        stored = Signal(sem("stored"), [0, 1], 16, base=16)
        a_full = Signal(sem("a_full"), A_RING)
        a_free = Signal(sem("a_free"), A_RING)
        b_full = Signal(sem("b_full"), [s for s in B_ITEMS if s[0] not in FFN_KINDS and s[0] != "GAP"])
        exp_done = Signal(sem("exp_done"), chunks)
        av_full = Signal(sem("av_full"), keys("AV"))
        av_free = Signal(sem("av_free"), AV_RING)
        sums_read = Signal(sem("sums_read"), SUMS)
        hi_done = Signal(sem("hi_done"), keys("XS", "CS", "QK", "VV", "V2", "K2", "AT", "X1", "Q2", "OT"))
        lo_done = Signal(sem("lo_done"), keys("XS", "CS", "QK", "VV", "V2", "K2", "AT", "X1", "Q2", "OT"))
        full_done = Signal(sem("full_done"), keys("V2", "K2", "Q2"))
        y_done = Signal(sem("y_done"), [("LN1",), ("LN2",)])
        cast_act = Signal(sem("cast_act"), [s for s in keys("CAST") if cast_on_act(*s[1:])])
        cast_dve = Signal(sem("cast_dve"), [s for s in keys("CAST") if not cast_on_act(*s[1:])])
        sub_pool = Signal(sem("sub_pool"), [s for s in keys("SUB") if sub_on_pool(*s[1:])])
        sub_dve = Signal(sem("sub_dve"), [s for s in keys("SUB") if not sub_on_pool(*s[1:])])
        max_split = Signal(sem("max_split"), keys("TM"))
        ms_done = Signal(sem("ms_done"), keys("R1"))
        rms_done = Signal(sem("rms_done"), keys("R1"))
        attn_done = Signal(sem("attn_done"), keys("R1N", "R2"))
        var_done = Signal(sem("var_done"), [("LN1",), ("LN2",)])
        rstd_done = Signal(sem("rstd_done"), [("LN1",), ("LN2",)])
        norm_done = Signal(sem("norm_done"), [("LN1",), ("LN2",)])
        link = Signal(sem("link"), [(s, k) for s in ORDER if s[0] not in FFN_KINDS for k in range(LINKS.get(s[0], 0))])

        f_full = Signal(sem("f_full"), [s for s in FFN if s[0] in ("FT", "UG")])
        down_full = Signal(sem("down_full"), range(TB))
        fx_hi = Signal(sem("fx_hi"), [("FT",)])
        fx_lo = Signal(sem("fx_lo"), [("FT",)])
        tanh_done = Signal(sem("tanh_done"), range(EB // 2))
        hid_done = Signal(sem("hid_done"), range(EB // 2))
        hid_hi = Signal(sem("hid_hi"), range(EB // 2))
        hid_lo = Signal(sem("hid_lo"), range(EB // 2))
        fy_done = Signal(sem("fy_done"), range(TB))
        fvar_done = Signal(sem("fvar_done"), range(TB))
        frstd_done = Signal(sem("frstd_done"), range(TB))
        f_out = Signal(sem("f_out"), range(TB))
        flink = Signal(sem("flink"), [(s, k) for s in FFN for k in range(LINKS.get(s[0], 0))])

        def cast_of(st, c):
            return (cast_act if cast_on_act(st, c) else cast_dve), ("CAST", st, c)

        def sub_of(st, c):
            return (sub_pool if sub_on_pool(st, c) else sub_dve), ("SUB", st, c)

        def b_release(s):
            if s[0] == "S":
                return exp_done, s
            if s[0] in ("V2", "K2", "Q2"):
                return full_done, s
            if s[0] in ("OP", "OP2"):
                return y_done, ("LN1",) if s[0] == "OP" else ("LN2",)
            if s[0] == "FT":
                return fx_lo, s
            if s[0] == "UG":
                return hid_done, s[1]
            return lo_done, s

        def wait_last(eng, signal, batch, key):
            if not isinstance(batch, int) or batch > 0:
                eng.wait_ge(signal.sem, signal.at(batch - 1, key))

        def chunk_index(st, c):
            return c if st == 1 else CHUNKS[1] + c

        def chunk_before(st, c, n):
            i = chunk_index(st, c) - n
            if i < 0:
                i += len(chunks)
                return (chunks[i][1], chunks[i][2]), False
            return (chunks[i][1], chunks[i][2]), True

        def up_of(s):
            return bank_b(s).rearrange("p (j w t) -> p j w t", j=2, w=2)[:, :, 0, :]

        def gate_of(s):
            return bank_b(s).rearrange("p (j w t) -> p j w t", j=2, w=2)[:, :, 1, :]

        block = ctx.enter_context(nc.Block())

        def run(eng, attention, feed_forward):
            for s in ORDER:
                if s[0] not in FFN_KINDS:
                    attention(0, s)
            with eng.Fori(1, NB) as b:
                for s in ORDER:
                    if s[0] in FFN_KINDS:
                        feed_forward(b - 1, s)
                    else:
                        attention(b, s)
            for s in FFN:
                feed_forward(NB - 1, s)

        @block.sync
        def _(sp):
            sp.dma_start(raw[0], wa).then_inc(s_w[0], 16)
            sp.dma_start(raw[1][:, 0:2048], wx).then_inc(s_w[0], 16)
            sp.dma_start(sub_sb, sub_w).then_inc(s_const, 16)
            sp.dma_start(b_qk_sb, b_qk).then_inc(s_const, 16)
            sp.dma_start(b_o_sb, b_o).then_inc(s_const, 16)
            sp.dma_start(bv_row[:, :], b_v.partition_broadcast(P)).then_inc(s_const, 16)
            sp.dma_start(lam_sb[:, :], lam_in.partition_broadcast(P)).then_inc(s_const, 16)
            sp.dma_start(raw[2], w_ffn[2]).then_inc(s_w[3], 16)
            sp.wait_ge(s_set, 1)
            sp.dma_start(raw[0], w_ffn[0]).then_inc(s_w[1], 16)
            sp.wait_ge(s_set, 2)
            sp.dma_start(raw[1], w_ffn[1]).then_inc(s_w[2], 16)
            sp.wait_ge(s_set, 5)

            def attention(b, s):
                if s[0] == "LOAD":
                    wait_last(sp, b_full, b, ("OT",))
                    sp.dma_start(attn.rearrange("p (k t) -> p k t", k=KB), xT[b, :, :, :]).then_inc(xt_in.sem, 16)
                    sp.dma_start(work.rearrange("p (k t) -> p k t", k=TB),
                                 ctx_in[b, :, :].rearrange("(k p) t -> p k t", p=P)).then_inc(ctx_loaded.sem, 16)
                elif s[0] == "LOADX":
                    wait_last(sp, norm_done, b, ("LN2",))
                    sp.dma_start(xr, x[b, :, :].rearrange("(k p) t -> p k t", p=P)).then_inc(x_in.sem, 16)
                elif s[0] == "QK":
                    i = s[1]
                    if i == 0:
                        wait_last(sp, b_full, b, ("S", 2, CHUNKS[2] - 1))
                        if isinstance(b, int):
                            sp.wait_ge(s_set_pool, 7)
                    sp.wait_ge(hi_done.sem, hi_done.at(b, s))
                    sp.wait_ge(lo_done.sem, lo_done.at(b, s))
                    for which, op in ((0, q_op), (1, k_op)):
                        for r, half in enumerate((qk_h, qk_l, qk_h, qk_l) if which == 0 else (qk_h, qk_l, qk_l, qk_h)):
                            src = half[:, i * 1024:(i + 1) * 1024].rearrange("p (c w t) -> p c w t", c=2, w=2)
                            sp.dma_start(op[16 * r:16 * r + 16, i * 4096:(i + 1) * 4096], src[:, :, which, :])\
                                .then_inc(ops1_in[i].sem, 16)
                elif s[0] == "Q2":
                    sp.wait_ge(hi_done.sem, hi_done.at(b, s))
                    sp.wait_ge(lo_done.sem, lo_done.at(b, s))
                    for r, half in enumerate((qk_h, qk_l, qk_h, qk_l)):
                        sp.dma_start(q_op[16 * r:16 * r + 16, :], half[:, 0:1024].rearrange("p (c t) -> p c t", c=2))\
                            .then_inc(ops2_in.sem, 16)
                elif s[0] == "AT":
                    sp.wait_ge(b_full.sem, b_full.at(b, ("S", 1, CHUNKS[1] - 1)))
                    for r, half in enumerate((ctx_h, ctx_l, ctx_l, ctx_h)):
                        sp.dma_start(k_op[16 * r:16 * r + 16, :], half[:, :].rearrange("p (c t) -> p c t", c=2))\
                            .then_inc(ops2_in.sem, 16)
                elif s[0] == "T":
                    st, g = s[1], s[2]
                    sp.wait_ge(a_free.sem, a_free.at(b, s))
                    sp.dma_start(q_op[96:98, g * GCOLS:(g + 1) * GCOLS], mrow[:, g % NG, :])\
                        .then_inc(max_in[g % NG].sem, 16)

            def feed_forward(b, s):
                if s[0] == "FN":
                    tb = s[1]
                    sp.wait_ge(f_out.sem, f_out.at(b, tb))
                    sp.dma_start(out[b, tb * P:(tb + 1) * P, :], x2[:, tb, :]).then_inc(stored.sem, 16)

            run(sp, attention, feed_forward)
            sp.wait_ge(stored.sem, stored.at(NB - 1, 1))

        @block.tensor
        def _(pe):
            pe.wait_ge(s_set_pool, 3)
            for i, w in enumerate((2, 0, 1)):
                pe.wait_ge(s_asum, i + 1)
                pe.matmul(ps_a[:, 0, i:i + 1], ones, asum[:, w:w + 1], start=True, stop=True)\
                    .then_inc(s_set_pe, 1)

            def product(dst, lhs, rhs, n):
                for k in range(n):
                    (lh, ll), (rh, rl) = lhs(k), rhs(k)
                    for j, (a, c) in enumerate(((lh, rh), (lh, rl), (ll, rh))):
                        last = pe.matmul(dst, a, c, start=k == 0 and j == 0, stop=k == n - 1 and j == 2)
                return last

            def b_slot(b, s):
                n, peeled, own = B_ITEMS.index(s), isinstance(b, int), s[0] in FFN_KINDS
                before = [t for t in B_ITEMS[n % 2:n:2] if t[0] != "GAP"]
                if peeled:
                    before = [t for t in before if (t[0] in FFN_KINDS) == own]
                if before:
                    signal, key = b_release(before[-1])
                    shift = (before[-1][0] not in FFN_KINDS) - (not own)
                    pe.wait_ge(signal.sem, signal.at(b + shift, key))
                elif own:
                    signal, key = b_release(LAST_IN_SLOT[n % 2])
                    pe.wait_ge(signal.sem, signal.at(b, key))
                else:
                    signal, key = b_release(LAST_IN_SLOT[n % 2])
                    wait_last(pe, signal, b, key)

            def a_slot(b, s):
                n = A_RING.index(s)
                if n >= 2:
                    pe.wait_ge(a_free.sem, a_free.at(b, A_RING[n - 2]))
                else:
                    wait_last(pe, a_free, b, A_RING[n - 2])

            def attention(b, s):
                kind = s[0]
                if kind in ("QK", "VV", "V2", "K2", "AT", "OP", "Q2", "OT", "OP2", "S"):
                    b_slot(b, s)
                    dst = bank_b(s)
                if kind == "QK":
                    pe.wait_ge(lo_done.sem, lo_done.at(b, ("XS",)))
                    pe.wait_ge(hi_done.sem, hi_done.at(b, ("XS",)))
                    for c in range(2):
                        cb = 2 * s[1] + c
                        for w in range(2):
                            last = product(dst[:, c * 512 + w * 256:c * 512 + w * 256 + 256],
                                           lambda k: (wa_h[:, w, k, cb * P:(cb + 1) * P], wa_l[:, w, k, cb * P:(cb + 1) * P]),
                                           lambda k: (act_h[:, k * T:(k + 1) * T], act_l[:, k * T:(k + 1) * T]), KB)
                    last.then_inc(b_full.sem, 1)
                elif kind == "VV":
                    for tb in range(TB):
                        last = product(dst[:, tb * 512:(tb + 1) * 512],
                                       lambda k: (act_h[:, k * T + tb * P:k * T + tb * P + P], act_l[:, k * T + tb * P:k * T + tb * P + P]),
                                       lambda k: (wa_h[:, 2, k, :], wa_l[:, 2, k, :]), KB)
                    last.then_inc(b_full.sem, 1)
                elif kind == "V2":
                    pe.wait_ge(lo_done.sem, lo_done.at(b, ("CS",)))
                    pe.wait_ge(hi_done.sem, hi_done.at(b, ("CS",)))
                    for tb in range(KB):
                        last = product(dst[:, tb * 256:(tb + 1) * 256],
                                       lambda k: (ctx_h[:, k * D + tb * P:k * D + tb * P + P], ctx_l[:, k * D + tb * P:k * D + tb * P + P]),
                                       lambda k: (wx_h[:, 2, k, :], wx_l[:, 2, k, :]), TB)
                    last.then_inc(b_full.sem, 1)
                elif kind in ("K2", "Q2", "OP2"):
                    w, hi, lo = {"K2": (1, ctx_h, ctx_l), "Q2": (0, act_h, act_l), "OP2": (3, act_h, act_l)}[kind]
                    if kind != "K2":
                        src = ("X1",) if kind == "Q2" else ("OT",)
                        pe.wait_ge(lo_done.sem, lo_done.at(b, src))
                        pe.wait_ge(hi_done.sem, hi_done.at(b, src))
                    for ob in range(TB):
                        last = product(dst[:, ob * 512:(ob + 1) * 512],
                                       lambda k: (wx_h[:, w, k, ob * P:(ob + 1) * P], wx_l[:, w, k, ob * P:(ob + 1) * P]),
                                       lambda k: (hi[:, k * D:(k + 1) * D], lo[:, k * D:(k + 1) * D]), TB)
                    last.then_inc(b_full.sem, 1)
                elif kind == "A":
                    st, i = s[1], s[2]
                    a_slot(b, s)
                    if st == 1 and i % 16 == 0:
                        pe.wait_ge(ops1_in[i // 16].sem, ops1_in[i // 16].at(b, "x"))
                    if st == 2 and i == 0:
                        pe.wait_ge(ops2_in.sem, ops2_in.at(b, "x"))
                    bank = bank_a(s)
                    if st == 1:
                        for tb in range(TB):
                            last = pe.matmul(bank[:, tb * T:(tb + 1) * T],
                                             q_op[0:ROWS_A, i * T + tb * P:i * T + tb * P + P],
                                             k_op[0:ROWS_A, i * T:(i + 1) * T], start=True, stop=True)
                    else:
                        h = i // KB
                        last = pe.matmul(bank, q_op[0:ROWS_A, i * P:(i + 1) * P],
                                         k_op[0:ROWS_A, h * D:(h + 1) * D], start=True, stop=True)
                    last.then_inc(a_full.sem, 1)
                elif kind == "T":
                    st, g = s[1], s[2]
                    a_slot(b, s)
                    pe.wait_ge(max_split.sem, max_split.at(b, ("TM", st, g)))
                    pe.transpose(bank_a(s).bitcast(f16)[0:16, 0:P], mhl[:, g % NG, :], ident16[:, :])\
                        .then_inc(a_full.sem, 1)
                elif kind == "S":
                    st, c = s[1], s[2]
                    g = c // PER_GROUP[st]
                    if c % PER_GROUP[st] == 0:
                        pe.wait_ge(max_in[g % NG].sem, max_in[g % NG].at(b, (st, g)))
                    for j in range(2):
                        if st == 1:
                            m = 2 * c + j
                            for kb in range(TB):
                                last = pe.matmul(dst[:, j * 512 + kb * T:j * 512 + (kb + 1) * T],
                                                 k_op[0:ROWS_B, m * T + kb * P:m * T + kb * P + P],
                                                 q_op[0:ROWS_B, m * T:(m + 1) * T], start=True, stop=True)
                        else:
                            h, kb = c // 2, 2 * (c % 2) + j
                            last = pe.matmul(dst[:, j * 512:(j + 1) * 512],
                                             k_op[0:ROWS_B, h * D + kb * P:h * D + kb * P + P],
                                             q_op[0:ROWS_B, h * D:(h + 1) * D], start=True, stop=True)
                    last.then_inc(b_full.sem, 1)
                elif kind == "AV":
                    st, c = s[1], s[2]
                    first = st == 1 or c % 4 == 0
                    if first:
                        n = AV_RING.index(("AVE", st, c if st == 1 else c // 4))
                        if n >= 1:
                            pe.wait_ge(av_free.sem, av_free.at(b, AV_RING[n - 1]))
                        else:
                            wait_last(pe, av_free, b, AV_RING[-1])
                    if c == 0:
                        need = ("VV",) if st == 1 else ("V2",)
                        pe.wait_ge(hi_done.sem, hi_done.at(b, need))
                        pe.wait_ge(lo_done.sem, lo_done.at(b, need))
                    signal, key = cast_of(st, c)
                    pe.wait_ge(signal.sem, signal.at(b, key))
                    signal, key = sub_of(st, c)
                    pe.wait_ge(signal.sem, signal.at(b, key))
                    buf = chunk_index(st, c) % NPH
                    start = first
                    for j in range(2):
                        for tb in range(TB if st == 1 else KB):
                            for kb in range(TB if st == 1 else 1):
                                for part in (prob_hi, prob_lo):
                                    if st == 1:
                                        col, r = j * 512 + kb * T + tb * P, j * TB + tb
                                        rhs, width = v1[:, kb * HEADS + c, :], 65
                                    else:
                                        col, r = j * 512 + tb * P, ((c // 2) % 2) * KB + tb
                                        rhs, width = v2[:, (2 * (c % 2) + j) * HEADS + c // 2, :], 33
                                    last = pe.matmul(ps_v[:, r * width:(r + 1) * width], part[buf][:, col:col + P],
                                                     rhs, start=start, stop=True, skip_group_check=True)
                                    start = False
                    last.then_inc(av_full.sem, 1)
                elif kind == "AT":
                    pe.wait_ge(attn_done.sem, attn_done.at(b, ("R1N", 3)))
                    for cb in range(KB):
                        for tb in range(TB):
                            last = pe.transpose(dst[:, cb * T + tb * P:cb * T + tb * P + P],
                                                attn[:, tb * D + cb * P:tb * D + cb * P + P], ident[:, :])
                    last.then_inc(b_full.sem, 1)
                elif kind == "OP":
                    pe.wait_ge(lo_done.sem, lo_done.at(b, ("AT",)))
                    pe.wait_ge(hi_done.sem, hi_done.at(b, ("AT",)))
                    for tb in range(TB):
                        last = product(dst[:, tb * 512:(tb + 1) * 512],
                                       lambda k: (act_h[:, k * T + tb * P:k * T + tb * P + P], act_l[:, k * T + tb * P:k * T + tb * P + P]),
                                       lambda k: (wa_h[:, 3, k, :], wa_l[:, 3, k, :]), KB)
                    last.then_inc(b_full.sem, 1)
                elif kind == "OT":
                    pe.wait_ge(attn_done.sem, attn_done.at(b, ("R2", 1)))
                    for cb in range(TB):
                        for tb in range(KB):
                            last = pe.transpose(dst[:, cb * D + tb * P:cb * D + tb * P + P],
                                                attn[:, tb * CH + cb * P:tb * CH + cb * P + P], ident[:, :])
                    last.then_inc(b_full.sem, 1)

            def take_wait(dst):
                pe.matmul(dst, ident16[:, :], ident16[:, 0:1], start=True, stop=True)

            def feed_forward(b, s):
                kind = s[0]
                if kind == "FT":
                    b_slot(b, s)
                    pe.wait_ge(norm_done.sem, norm_done.at(b, ("LN2",)))
                    dst = bank_b(s)
                    for k in range(KB):
                        for tb in range(TB):
                            last = pe.transpose(dst[:, k * T + tb * P:k * T + tb * P + P],
                                                x2[:, tb, k * P:(k + 1) * P], ident[:, :])
                    last.then_inc(f_full.sem, 1)
                elif kind == "UG":
                    b_slot(b, s)
                    if s[1] == 0:
                        pe.wait_ge(fx_lo.sem, fx_lo.at(b, ("FT",)))
                        pe.wait_ge(fx_hi.sem, fx_hi.at(b, ("FT",)))
                    dst = bank_b(s)
                    take_wait(dst[:, 0:1])
                    for j in range(2):
                        e = 2 * s[1] + j
                        for w in range(2):
                            for k in range(KB):
                                for half in (fx_h, fx_l):
                                    last = pe.matmul(dst[:, (2 * j + w) * T:(2 * j + w + 1) * T],
                                                     w8[:, w, k * E + e * P:k * E + e * P + P],
                                                     half[:, k * T:(k + 1) * T],
                                                     start=k == 0 and half is fx_h, stop=k == KB - 1 and half is fx_l)
                    last.then_inc(f_full.sem, 1)
                elif kind == "DN":
                    tb, p = s[1], s[2]
                    n = EB // D_PARTS
                    if p == 0:
                        if tb == 1:
                            pe.wait_ge(fy_done.sem, fy_done.at(b, 0))
                        else:
                            pe.wait_ge(hid_hi.sem, hid_hi.at(b, EB // 2 - 1))
                            pe.wait_ge(hid_lo.sem, hid_lo.at(b, EB // 2 - 1))
                        take_wait(ps_f[:, 0:1])
                    for e in range(p * n, (p + 1) * n):
                        for half in (hid_h, hid_l):
                            last = pe.matmul(ps_f[:, :], half[:, e * T + tb * P:e * T + tb * P + P],
                                             w8[:, 2, e * D:(e + 1) * D], start=e == 0 and half is hid_h,
                                             stop=e == EB - 1 and half is hid_l)
                    if p == D_PARTS - 1:
                        last.then_inc(down_full.sem, 1)

            run(pe, attention, feed_forward)

        @block.scalar
        def _(act):
            act.wait_ge(s_w[0], 32)
            act.wait_ge(s_const, 80)
            for w in range(4):
                src = raw[0][:, w * 2048:(w + 1) * 2048]
                dst = wa_h[:, w, :, :].rearrange("p k n -> p (k n)")
                if w == 3:
                    act.wait_ge(s_set_pool, 4)
                act.activation(dst, src, ACT.Copy, scale=sub_s if w == 3 else W_UP)
            act.activation(wx_h[:, :, :, :].rearrange("p w k n -> p (w k n)"), raw[1][:, 0:2048], ACT.Copy, scale=W_UP)\
                .then_inc(s_set_act, 1)
            act.wait_ge(s_set, 3)
            act.activation(lam2, lam2, ACT.Exp).then_inc(s_set_act, 1)

            def attention(b, s):
                kind = s[0]
                if kind in ("XS", "CS"):
                    if kind == "XS":
                        wait_last(act, b_full, b, ("OP2",))
                        act.wait_ge(xt_in.sem, xt_in.at(b, "x"))
                        dst, src = act_h, attn
                    else:
                        wait_last(act, ops2_in, b, "x")
                        act.wait_ge(ctx_loaded.sem, ctx_loaded.at(b, "x"))
                        dst, src = ctx_h, work
                    act.activation(dst[:, :], src, ACT.Copy).then_inc(hi_done.sem, 1)
                elif kind == "QK":
                    act.wait_ge(b_full.sem, b_full.at(b, s))
                    act.activation(qk_h[:, s[1] * 1024:(s[1] + 1) * 1024], bank_b(s), ACT.Copy, scale=1 / W_UP)\
                        .then_inc(hi_done.sem, 1)
                elif kind == "VV":
                    act.wait_ge(b_full.sem, b_full.at(b, s))
                    act.activation(v1[:, :, 32:64], bank_b(s).rearrange("p (h e) -> p h e", e=32), ACT.Copy,
                                   scale=1 / W_UP).then_inc(hi_done.sem, 1)
                elif kind == "V2":
                    act.wait_ge(full_done.sem, full_done.at(b, s))
                    act.activation(v2[:, :, 16:32], work.rearrange("p (h e) -> p h e", e=16), ACT.Copy)\
                        .then_inc(hi_done.sem, 1)
                elif kind in ("K2", "Q2"):
                    act.wait_ge(full_done.sem, full_done.at(b, s))
                    dst = ctx_h[:, :] if kind == "K2" else qk_h[:, 0:1024]
                    act.activation(dst, work, ACT.Copy).then_inc(hi_done.sem, 1)
                elif kind in ("AT", "OT"):
                    act.wait_ge(b_full.sem, b_full.at(b, s))
                    act.activation(act_h[:, :], bank_b(s), ACT.Copy).then_inc(hi_done.sem, 1)
                elif kind == "X1":
                    act.wait_ge(norm_done.sem, norm_done.at(b, ("LN1",)))
                    act.activation(act_h[:, :], xr.rearrange("p b n -> p (b n)"), ACT.Copy).then_inc(hi_done.sem, 1)
                elif kind == "S":
                    st, c = s[1], s[2]
                    act.wait_ge(b_full.sem, b_full.at(b, s))
                    before, same = chunk_before(st, c, N32)
                    signal, key = sub_of(*before)
                    if same:
                        act.wait_ge(signal.sem, signal.at(b, key))
                    else:
                        wait_last(act, signal, b, key)
                    act.activation(prob32[chunk_index(st, c) % N32], bank_b(s), ACT.Exp, scale=SCALE)\
                        .then_inc(exp_done.sem, 1)
                elif kind == "CAST" and cast_on_act(*s[1:]):
                    st, c = s[1], s[2]
                    cast_chunk(act, b, st, c).then_inc(cast_act.sem, 1)
                elif kind == "AVE":
                    st, i = s[1], s[2]
                    act.wait_ge(av_full.sem, av_full.at(b, ("AV", st, i if st == 1 else 4 * i + 3)))
                    n = SUMS.index(sums_item(s))
                    if i % 4 == 0:
                        if n >= 2:
                            act.wait_ge(sums_read.sem, sums_read.at(b, SUMS[n - 2]))
                        else:
                            wait_last(act, sums_read, b, SUMS[n - 2])
                    width = 260 if st == 1 else 264
                    act.activation(sums[:, n % 2, (i % 4) * width:(i % 4 + 1) * width], ps_v[:, 0:width],
                                   ACT.Copy).then_inc(av_free.sem, 1)

            def cast_chunk(eng, b, st, c):
                eng.wait_ge(exp_done.sem, exp_done.at(b, ("S", st, c)))
                before, same = chunk_before(st, c, NPH)
                if same:
                    eng.wait_ge(av_full.sem, av_full.at(b, ("AV", *before)))
                else:
                    wait_last(eng, av_full, b, ("AV", *before))
                i = chunk_index(st, c)
                return eng.activation(prob_hi[i % NPH], prob32[i % N32], ACT.Copy)

            def feed_forward(b, s):
                if s[0] == "FT":
                    act.wait_ge(f_full.sem, f_full.at(b, s))
                    act.activation(fx_h[:, :], bank_b(s), ACT.Copy).then_inc(fx_hi.sem, 1)
                elif s[0] == "UG":
                    e = s[1]
                    act.wait_ge(f_full.sem, f_full.at(b, s))
                    if e >= 1:
                        act.wait_ge(hid_done.sem, hid_done.at(b, e - 1))
                    act.activation(tanh_b[:, :, :], up_of(s), ACT.Tanh, scale=half_sc[:, 0:1]).then_inc(tanh_done.sem, 1)
                elif s[0] == "UL":
                    e = s[1]
                    act.wait_ge(hid_done.sem, hid_done.at(b, e))
                    act.activation(hid_h[:, e * 512:(e + 1) * 512], hid32[:, e % 2, :, :].rearrange("p j t -> p (j t)"),
                                   ACT.Copy).then_inc(hid_hi.sem, 1)

            run(act, attention, feed_forward)

        @block.gpsimd
        def _(pool):
            pool.memset(small[:, 0:8], -0.5)
            pool.memset(ones, 1.0)
            pool.memset(v1[:, :, 64:65], 1.0).then_inc(stored.sem, 16)
            pool.memset(v2[:, :, 32:33], 1.0)
            pool.memset(ident[:, :], 0.0)
            pool.memset(ident16[:, :], 0.0).then_inc(s_set_pool, 1)
            pool.wait_ge(s_set_pool, 1)
            for m in (ident, ident16):
                pool.affine_select(out=m[:, :], in_=m[:, :], compare_op=ALU.not_equal, fill=1.0, base=0,
                                   pattern=[[-1, P]], channel_multiplier=1).then_inc(s_set_pool, 1)
            pool.wait_ge(s_const, 80)
            pool.tensor_scalar(sub_s, sub_sb, W_UP * (1.0 - LAMBDA_INIT), None, ALU.mult).then_inc(s_set_pool, 1)
            pool.wait_ge(s_set, 5)
            pool.memset(q_op[64:96, :], 0.0).then_inc(s_set_pool, 1)
            pool.memset(k_op[64:96, :], 0.0).then_inc(s_set_pool, 1)
            pool.memset(k_op[96:98, :], -1.0).then_inc(s_set_pool, 1)

            def attention(b, s):
                if s[0] == "SUB" and sub_on_pool(*s[1:]):
                    st, c = s[1], s[2]
                    signal, key = cast_of(st, c)
                    pool.wait_ge(signal.sem, signal.at(b, key))
                    i = chunk_index(st, c)
                    pool.tensor_tensor(prob_lo[i % NPH], prob32[i % N32], prob_hi[i % NPH], ALU.subtract)\
                        .then_inc(sub_pool.sem, 1)
                elif s[0] == "R1":
                    pool.wait_ge(ms_done.sem, ms_done.at(b, s))
                    pool.tensor_tensor(rrms[:, s[1] % 2, :], msq[:, :], neg_half, ALU.pow).then_inc(rms_done.sem, 1)
                elif s[0] == "LN1":
                    layer_power(b, s)

            def layer_power(b, s):
                pool.wait_ge(var_done.sem, var_done.at(b, s))
                pool.tensor_tensor(rstd[:, 0, :], var[:, 0, :], neg_half[:, 0:2], ALU.pow).then_inc(rstd_done.sem, 1)

            def feed_forward(b, s):
                if s[0] == "LN2":
                    layer_power(b, s)
                elif s[0] == "FV":
                    tb = s[1]
                    pool.wait_ge(fvar_done.sem, fvar_done.at(b, tb))
                    pool.tensor_tensor(rstd[:, 1, tb:tb + 1], var[:, 1, tb:tb + 1], neg_half[:, 0:1], ALU.pow)\
                        .then_inc(frstd_done.sem, 1)

            run(pool, attention, feed_forward)

        @block.vector
        def _(dve):
            steps = [0]

            def setup_step(ins):
                steps[0] += 1
                ins.then_inc(s_set, 1)
                dve.wait_ge(s_set, steps[0])

            dve.wait_ge(s_set_act, 1)
            for w in range(4):
                src = raw[0][:, w * 2048:(w + 1) * 2048]
                hi = wa_h[:, w, :, :].rearrange("p k n -> p (k n)")
                lo = wa_l[:, w, :, :].rearrange("p k n -> p (k n)")
                last = dve.scalar_tensor_tensor(out=lo, in0=src, scalar=sub_s if w == 3 else W_UP, in1=hi,
                                                op0=ALU.mult, op1=ALU.subtract)
            setup_step(last)
            setup_step(dve.scalar_tensor_tensor(
                out=wx_l[:, :, :, :].rearrange("p w k n -> p (w k n)"), in0=raw[1][:, 0:2048], scalar=W_UP,
                in1=wx_h[:, :, :, :].rearrange("p w k n -> p (w k n)"), op0=ALU.mult, op1=ALU.subtract))
            dve.wait_ge(s_const, 80)
            lam = lam_sb[:, :].rearrange("p (s b d) -> p s b d", s=2, b=2)
            chain = [0]

            def chained(ins):
                chain[0] += 1
                ins.then_inc(s_chain, 1)
                dve.wait_ge(s_chain, chain[0])

            chained(dve.tensor_tensor(lam[:, 0, :, :], lam[:, 0, :, :], lam[:, 1, :, :], ALU.mult))
            setup_step(dve.tensor_reduce(lam2, lam[:, 0, :, :], AX.X, ALU.add))
            dve.wait_ge(s_set_act, 2)
            chained(dve.tensor_scalar(nlam, lam2[:, 1:2], LAMBDA_INIT, None, ALU.subtract))
            chained(dve.tensor_tensor(nlam, nlam, lam2[:, 0:1], ALU.subtract))
            for n, w in enumerate((2, 0, 1)):
                dve.wait_ge(s_w[1 + w], 16)
                dve.tensor_reduce(asum[:, w:w + 1], raw[w], AX.X, ALU.add, apply_absolute_value=True)\
                    .then_inc(s_asum, 1)
                dve.wait_ge(s_set_pe, 1 + n)
                chained(dve.tensor_scalar(w_sc[:, w:w + 1], ps_a[:, 0, n:n + 1], 1.0 / (D * E), Q_EPS, ALU.mult, ALU.add))
                chained(dve.tensor_scalar(half_sc[:, w:w + 1], w_sc[:, w:w + 1], 0.5, None, ALU.mult))
                chained(dve.tensor_scalar(nhalf_sc[:, w:w + 1], w_sc[:, w:w + 1], -0.5, None, ALU.mult))
                chained(dve.tensor_scalar(w8[:, w, :], raw[w], nhalf_sc[:, w:w + 1], None, ALU.is_lt, saturate=False))
                last = dve.scalar_tensor_tensor(out=w8[:, w, :], in0=raw[w], scalar=half_sc[:, w:w + 1],
                                                in1=w8[:, w, :], op0=ALU.is_gt, op1=ALU.subtract, saturate=False)
                chained(last)
            chained(dve.tensor_tensor(down_sc, w_sc[:, 0:1], w_sc[:, 1:2], ALU.mult))
            chained(dve.tensor_tensor(down_sc, down_sc, w_sc[:, 2:3], ALU.mult))
            setup_step(dve.tensor_scalar(down_sc, down_sc, 8.0, None, ALU.mult))
            setup_step(dve.memset(msq[:, :], 1.0))

            def linked(b, s, k, ins, signal=None):
                signal = signal or link
                ins.then_inc(signal.sem, 1)
                dve.wait_ge(signal.sem, signal.at(b, (s, k)))

            def layer_norm(b, s, k0, src, part, blocks, signal, ready):
                for tb in blocks:
                    last = dve.bn_stats(stats[:, part, tb, :], src[:, tb, :])
                linked(b, s, k0, last, signal)
                dve.memset(wait_col[:, part:part + 1], 0.0)
                for tb in blocks:
                    last = dve.bn_aggr(mv[:, part, tb, :], stats[:, part, tb, :])
                linked(b, s, k0 + 1, last, signal)
                dve.tensor_scalar(var[:, part, blocks[0]:blocks[-1] + 1], mv[:, part, blocks[0]:blocks[-1] + 1, 1],
                                  EPS, None, ALU.add).then_inc(ready.sem, 1)

            def attention(b, s):
                kind = s[0]
                if kind in ("XS", "CS", "AT", "OT", "X1", "K2", "Q2", "V2", "QK", "VV"):
                    n = lo_done.keys.index(s)
                    if n >= 1:
                        dve.wait_ge(lo_done.sem, lo_done.at(b, lo_done.keys[n - 1]))
                    else:
                        wait_last(dve, lo_done, b, lo_done.keys[-1])
                    if kind in ("K2", "Q2"):
                        dve.wait_ge(b_full.sem, b_full.at(b, s))
                        for ob in range(TB):
                            i = ob + (TB if kind == "K2" else 0)
                            last = dve.tensor_scalar(work[:, ob * 512:(ob + 1) * 512], bank_b(s)[:, ob * 512:(ob + 1) * 512],
                                                     1 / W_UP, b_qk_sb[:, i:i + 1], ALU.mult, ALU.add)
                        last.then_inc(full_done.sem, 1)
                    elif kind == "V2":
                        dve.wait_ge(b_full.sem, b_full.at(b, s))
                        dve.scalar_tensor_tensor(
                            out=work.rearrange("p (k n) -> p k n", k=KB), in0=bank_b(s).rearrange("p (k n) -> p k n", k=KB),
                            scalar=1 / W_UP, in1=bv_row[:, :].unsqueeze(1).to_broadcast([P, KB, CH]),
                            op0=ALU.mult, op1=ALU.add).then_inc(full_done.sem, 1)
                    dve.wait_ge(hi_done.sem, hi_done.at(b, s))
                    if kind == "XS":
                        ins = dve.tensor_tensor(act_l[:, :], attn, act_h[:, :], ALU.subtract)
                    elif kind == "CS":
                        ins = dve.tensor_tensor(ctx_l[:, :], work, ctx_h[:, :], ALU.subtract)
                    elif kind == "QK":
                        cols = slice(s[1] * 1024, (s[1] + 1) * 1024)
                        ins = dve.scalar_tensor_tensor(out=qk_l[:, cols], in0=bank_b(s), scalar=1 / W_UP,
                                                       in1=qk_h[:, cols], op0=ALU.mult, op1=ALU.subtract)
                    elif kind == "VV":
                        ins = dve.scalar_tensor_tensor(out=v1[:, :, 0:32], in0=bank_b(s).rearrange("p (h e) -> p h e", e=32),
                                                       scalar=1 / W_UP, in1=v1[:, :, 32:64], op0=ALU.mult, op1=ALU.subtract)
                    elif kind == "V2":
                        ins = dve.tensor_tensor(v2[:, :, 0:16], work.rearrange("p (h e) -> p h e", e=16), v2[:, :, 16:32],
                                                ALU.subtract)
                    elif kind == "K2":
                        ins = dve.tensor_tensor(ctx_l[:, :], work, ctx_h[:, :], ALU.subtract)
                    elif kind == "Q2":
                        ins = dve.tensor_tensor(qk_l[:, 0:1024], work, qk_h[:, 0:1024], ALU.subtract)
                    elif kind in ("AT", "OT"):
                        ins = dve.tensor_tensor(act_l[:, :], bank_b(s), act_h[:, :], ALU.subtract)
                    else:
                        ins = dve.tensor_tensor(act_l[:, :], xr.rearrange("p b n -> p (b n)"), act_h[:, :], ALU.subtract)
                    ins.then_inc(lo_done.sem, 1)
                    if kind == "X1":
                        dve.wait_ge(lo_done.sem, lo_done.at(b, s))
                        for tb in range(TB):
                            dve.tensor_scalar(xr[:, tb, :], xr[:, tb, :], b_o_sb[:, tb:tb + 1], None, ALU.add)
                elif kind == "A":
                    st, i = s[1], s[2]
                    g, n = divmod(i, A_ITEMS[st])
                    dve.wait_ge(a_full.sem, a_full.at(b, s))
                    if st == 1:
                        dve.tensor_reduce(mcol[:, g % NG, 2 * n:2 * n + 2], bank_a(s).rearrange("p (t k) -> p t k", t=TB),
                                          AX.X, ALU.max).then_inc(a_free.sem, 1)
                    else:
                        dve.tensor_reduce(mcol[:, g % NG, n:n + 1], bank_a(s), AX.X, ALU.max).then_inc(a_free.sem, 1)
                elif kind == "TM":
                    st, g = s[1], s[2]
                    dve.wait_ge(a_free.sem, a_free.at(b, ("A", st, (g + 1) * A_ITEMS[st] - 1)))
                    linked(b, s, 0, dve.tensor_scalar(mhl[:, g % NG, 0:8], mcol[:, g % NG, :], -P_SHIFT, None, ALU.add))
                    dve.scalar_tensor_tensor(out=mhl[:, g % NG, 8:16], in0=mcol[:, g % NG, :], scalar=-P_SHIFT,
                                             in1=mhl[:, g % NG, 0:8], op0=ALU.add, op1=ALU.subtract)\
                        .then_inc(max_split.sem, 1)
                elif kind == "T":
                    st, g = s[1], s[2]
                    dve.wait_ge(a_full.sem, a_full.at(b, s))
                    dve.tensor_copy(mrow[:, g % NG, :], bank_a(s).bitcast(f16)[0:16, 0:P]).then_inc(a_free.sem, 1)
                elif kind == "CAST" and not cast_on_act(*s[1:]):
                    st, c = s[1], s[2]
                    dve.wait_ge(exp_done.sem, exp_done.at(b, ("S", st, c)))
                    before, same = chunk_before(st, c, NPH)
                    if same:
                        dve.wait_ge(av_full.sem, av_full.at(b, ("AV", *before)))
                    else:
                        wait_last(dve, av_full, b, ("AV", *before))
                    i = chunk_index(st, c)
                    dve.tensor_copy(prob_hi[i % NPH], prob32[i % N32]).then_inc(cast_dve.sem, 1)
                elif kind == "SUB" and not sub_on_pool(*s[1:]):
                    st, c = s[1], s[2]
                    signal, key = cast_of(st, c)
                    dve.wait_ge(signal.sem, signal.at(b, key))
                    i = chunk_index(st, c)
                    dve.tensor_tensor(prob_lo[i % NPH], prob32[i % N32], prob_hi[i % NPH], ALU.subtract)\
                        .then_inc(sub_dve.sem, 1)
                elif kind == "R1":
                    q = s[1]
                    if q == 0:
                        dve.wait_ge(lo_done.sem, lo_done.at(b, ("K2",)))
                    dve.wait_ge(av_free.sem, av_free.at(b, ("AVE", 1, 4 * q + 3)))
                    src = sums[:, SUMS.index(s) % 2, 0:1040].rearrange("p (r e) -> p r e", e=65)
                    r = rec[:, 0:16]
                    odd = r.rearrange("p (h two t) -> p h two t", h=4, two=2)[:, :, 1, :]
                    avr = av.rearrange("p (r e) -> p r e", e=32)
                    linked(b, s, 0, dve.reciprocal(r, src[:, :, 64]))
                    linked(b, s, 1, dve.tensor_scalar(odd, odd, nlam, None, ALU.mult))
                    dve.tensor_tensor(avr, src[:, :, 0:32], src[:, :, 32:64], ALU.add).then_inc(sums_read.sem, 1)
                    dve.wait_ge(sums_read.sem, sums_read.at(b, s))
                    linked(b, s, 2, dve.tensor_tensor(avr, avr, r.unsqueeze(2).to_broadcast([P, 16, 32]), ALU.mult))
                    pair = av.rearrange("p (h two t e) -> p t h two e", h=4, two=2, t=TB)
                    dst = attn_heads(q)
                    linked(b, s, 3, dve.tensor_tensor(dst, pair[:, :, :, 0, :], pair[:, :, :, 1, :], ALU.add))
                    sq = work[:, 0:256].rearrange("p (t h e) -> p t h e", t=TB, h=4)
                    linked(b, s, 4, dve.tensor_tensor(sq, dst, dst, ALU.mult))
                    linked(b, s, 5, dve.tensor_reduce(msq[:, :].rearrange("p (t h) -> p t h", t=TB), sq, AX.X, ALU.add))
                    dve.tensor_scalar(msq[:, :], msq[:, :], 1.0 / 32, EPS, ALU.mult, ALU.add).then_inc(ms_done.sem, 1)
                elif kind == "R1N":
                    q = s[1]
                    dve.wait_ge(rms_done.sem, rms_done.at(b, ("R1", q)))
                    dst = attn_heads(q)
                    dve.tensor_tensor(dst, dst, rrms[:, q % 2, :].rearrange("p (t h) -> p t h", t=TB).unsqueeze(3)
                                      .to_broadcast([P, TB, 4, 32]), ALU.mult).then_inc(attn_done.sem, 1)
                elif kind == "R2":
                    half = s[1]
                    if half == 0:
                        dve.wait_ge(lo_done.sem, lo_done.at(b, ("Q2",)))
                    else:
                        dve.wait_ge(attn_done.sem, attn_done.at(b, ("R2", 0)))
                    dve.wait_ge(av_free.sem, av_free.at(b, ("AVE", 2, 4 * half + 3)))
                    src = sums[:, SUMS.index(s) % 2, :].rearrange("p (r e) -> p r e", e=33)
                    r = rec[:, :]
                    linked(b, s, 0, dve.reciprocal(r, src[:, :, 32]))
                    dve.tensor_tensor(av.rearrange("p (r e) -> p r e", e=16), src[:, :, 0:16], src[:, :, 16:32], ALU.add)\
                        .then_inc(sums_read.sem, 1)
                    dve.wait_ge(sums_read.sem, sums_read.at(b, s))
                    dst = attn.rearrange("p (t h e) -> p t h e", t=KB, h=HEADS)[:, :, 8 * half:8 * half + 8, :]
                    dve.tensor_tensor(dst, av.rearrange("p (h t e) -> p t h e", h=8, t=KB),
                                      r.rearrange("p (h t) -> p t h", h=8).unsqueeze(3).to_broadcast([P, KB, 8, 16]),
                                      ALU.mult).then_inc(attn_done.sem, 1)
                elif kind == "LN1":
                    dve.wait_ge(x_in.sem, x_in.at(b, "x"))
                    block_norm(b, s)

            def block_norm(b, s):
                item, signal = (("OP",), link) if s[0] == "LN1" else (("OP2",), flink)
                dve.wait_ge(b_full.sem, b_full.at(b, item))
                for tb in range(TB):
                    last = dve.scalar_tensor_tensor(out=xr[:, tb, :], in0=bank_b(item)[:, tb * 512:(tb + 1) * 512],
                                                    scalar=1 / W_UP, in1=xr[:, tb, :], op0=ALU.mult, op1=ALU.add)
                last.then_inc(y_done.sem, 1)
                dve.wait_ge(y_done.sem, y_done.at(b, s))
                layer_norm(b, s, 0, xr, 0, (0, 1), signal, var_done)
                dve.wait_ge(rstd_done.sem, rstd_done.at(b, s))
                if s[0] == "LN2":
                    wait_last(dve, stored, b, 1)
                dst = xr if s[0] == "LN1" else x2
                for tb in range(TB):
                    last = dve.tensor_scalar(dst[:, tb, :], xr[:, tb, :], mv[:, 0, tb, 0:1], rstd[:, 0, tb:tb + 1],
                                             ALU.subtract, ALU.mult)
                last.then_inc(norm_done.sem, 1)

            def attn_heads(q):
                return attn.rearrange("p (t h e) -> p t h e", t=TB, h=HEADS)[:, :, 4 * q:4 * q + 4, :]

            def feed_forward(b, s):
                kind = s[0]
                if kind == "LN2":
                    block_norm(b, s)
                elif kind == "FT":
                    dve.wait_ge(fx_hi.sem, fx_hi.at(b, s))
                    dve.tensor_tensor(fx_l[:, :], bank_b(s), fx_h[:, :], ALU.subtract).then_inc(fx_lo.sem, 1)
                elif kind == "UG":
                    e = s[1]
                    dve.wait_ge(tanh_done.sem, tanh_done.at(b, e))
                    if e >= 2:
                        dve.wait_ge(hid_lo.sem, hid_lo.at(b, e - 2))
                    linked(b, s, 0, dve.scalar_tensor_tensor(out=hid32[:, e % 2, :, :], in0=tanh_b[:, :, :], scalar=1.0,
                                                             in1=up_of(s), op0=ALU.add, op1=ALU.mult), flink)
                    dve.scalar_tensor_tensor(out=hid32[:, e % 2, :, :], in0=gate_of(s), scalar=1.0 / 16,
                                             in1=hid32[:, e % 2, :, :], op0=ALU.mult, op1=ALU.mult)\
                        .then_inc(hid_done.sem, 1)
                elif kind == "UL":
                    e = s[1]
                    dve.wait_ge(hid_hi.sem, hid_hi.at(b, e))
                    dve.tensor_tensor(hid_l[:, e * 512:(e + 1) * 512], hid32[:, e % 2, :, :].rearrange("p j t -> p (j t)"),
                                      hid_h[:, e * 512:(e + 1) * 512], ALU.subtract).then_inc(hid_lo.sem, 1)
                elif kind == "FV":
                    tb = s[1]
                    dve.wait_ge(down_full.sem, down_full.at(b, tb))
                    dve.scalar_tensor_tensor(out=x2[:, tb, :], in0=ps_f[:, :], scalar=down_sc, in1=x2[:, tb, :],
                                             op0=ALU.mult, op1=ALU.add).then_inc(fy_done.sem, 1)
                    dve.wait_ge(fy_done.sem, fy_done.at(b, tb))
                    layer_norm(b, s, 0, x2, 1, (tb,), flink, fvar_done)
                elif kind == "FN":
                    tb = s[1]
                    dve.wait_ge(frstd_done.sem, frstd_done.at(b, tb))
                    dve.tensor_scalar(x2[:, tb, :], x2[:, tb, :], mv[:, 1, tb, 0:1], rstd[:, 1, tb:tb + 1],
                                      ALU.subtract, ALU.mult).then_inc(f_out.sem, 1)

            run(dve, attention, feed_forward)


def kernel(**inputs):
    import numpy as np
    import concourse.bacc as bacc
    from concourse.bass_utils import run_bass_kernel_spmd

    a = {k: np.asarray(v) for k, v in inputs.items()}

    def rows_first(w):
        wt = w.T
        n = wt.shape[0] // P
        return np.ascontiguousarray(wt.reshape(n, P, wt.shape[1]).transpose(1, 0, 2)).reshape(P, -1)

    def channel_order(matrices):
        order = np.empty((matrices // 8, HD, 8), np.int64)
        for cb in range(matrices // 8):
            for j in range(8):
                m = (cb // 2) * 16 + j * 2 + cb % 2
                order[cb, :, j] = m * HD + np.arange(HD)
        return order.reshape(-1)

    c1, c2 = channel_order(NM), channel_order(HEADS)
    L, X = "L0_attn_", "L0_xattn_"
    arrays = {
        "xT": np.ascontiguousarray(a["x"].transpose(0, 2, 1).reshape(NB, KB, P, T).transpose(0, 2, 1, 3)),
        "x": a["x"],
        "ctx_in": a["ctx_2048"],
        "wa": np.concatenate([rows_first(a[L + "Wq"][c1]), rows_first(a[L + "Wk"][c1]), rows_first(a[L + "Wv"]),
                              rows_first(a[L + "Wo"])], axis=1),
        "wx": np.concatenate([rows_first(a[X + "Wq"][c2]), rows_first(a[X + "Wk"][c2]), rows_first(a[X + "Wv"]),
                              rows_first(a[X + "Wo"])], axis=1),
        "w_ffn": np.stack([rows_first(a["L0_ffn_W_up"]), rows_first(a["L0_ffn_W_gate"]),
                           rows_first(a["L0_ffn_W_down"])]),
        "sub_w": np.tile(a[L + "subln_weight"], P // 32).reshape(P, 1),
        "lam_in": np.concatenate([a[L + "lambda_q1"], a[L + "lambda_q2"], a[L + "lambda_k1"], a[L + "lambda_k2"]]),
        "b_qk": np.ascontiguousarray(np.concatenate([a[X + "bq"][c2].reshape(TB, P).T, a[X + "bk"][c2].reshape(TB, P).T], axis=1)),
        "b_v": a[X + "bv"],
        "b_o": np.ascontiguousarray(a[X + "bo"].reshape(TB, P).T),
    }
    nc = bacc.Bacc("TRN2", target_bir_lowering=False, num_devices=1)
    args = [nc.dram_tensor(f"in_{k}", v.shape, f32, kind="ExternalInput").ap() for k, v in arrays.items()]
    args.append(nc.dram_tensor("out_0", (NB, T, D), f32, kind="ExternalOutput").ap())
    decoder_kernel(nc, *args)
    r = run_bass_kernel_spmd(nc, [{f"in_{k}": v for k, v in arrays.items()}], core_ids=[0])
    return r.results[0]["out_0"]
```

```python
from contextlib import ExitStack

import concourse.bass as bass
from concourse import mybir

f32, f16, f8 = mybir.dt.float32, mybir.dt.float16, mybir.dt.float8e4
ALU, ACT, AX = mybir.AluOpType, mybir.ActivationFunctionType, mybir.AxisListType

P = 128
NB, T, D = 16, 256, 512
TB, KB = T // P, D // P
HEADS = 16
HD = D // HEADS // 2
NM = 2 * HEADS
CH = T
E = 2048
EB = E // P
EPS = 1e-5
Q_EPS = 1e-8
LAMBDA_INIT = 0.8 - 0.6 * 2.718281828459045 ** (-0.3 * 12)
SCALE = HD ** -0.5
W_UP = 256.0
P_SHIFT = 32.0
ROWS_A = 96
ROWS_B = 98
GROUPS = 8
GCOLS = 1024
CHUNK = 1024
A_ITEMS = {1: NM // GROUPS, 2: HEADS * KB // GROUPS}
CHUNKS = {1: NM // 2, 2: HEADS * 2}
PER_GROUP = {s: CHUNKS[s] // GROUPS for s in (1, 2)}
LOOK = {1: 2, 2: 2}
NG = 4
N32, NPH = 4, 4
AV_LAG = 3
D_PARTS = 4


def product_of(s):
    return {"QK": ("QKP", *s[1:], 1), "VV": ("VVP", *s[1:], 1), "OP2": ("OP2P", 0, 1),
            "UG": ("UGP", *s[1:], 1)}.get(s[0], (s[0] + "P", *s[1:]))


def batch_order():
    o, slot_b, state = [], {}, {"last": 1, "held": None, "taken": False}

    def put(shift, *steps):
        for s in steps:
            if s[0] == "S" or s[0] in B_PRODUCTS and s[2:] != (1,):
                if s[0] != "S" and state["taken"]:
                    state["held"] = None
                slot = 1 - (state["last"] if state["held"] is None else state["held"])
                slot_b[s[:2] if s[0] in TWO_PARTS else s] = state["last"] = slot
                if state["taken"]:
                    state["held"], state["taken"] = None, False
                if s[0] in ("OTP", "FTP", *TWO_PARTS):
                    state["held"] = slot
            if s[0] in ("OTL", "FTL", "UG", "LN2"):
                state["taken"] = True
            o.append((shift, s))

    def attention(st, extra):
        n, per = CHUNKS[st], PER_GROUP[st]
        share = A_ITEMS[st] // per
        late = {}
        lag = AV_LAG + 3
        for c in range(n + lag):
            if st == 2 and c == n:
                break
            g = c // per + LOOK[st]
            if c < n:
                put(0, ("S", st, c))
            if st == 1 and c == 0:
                put(-1, ("CAST", 2, CHUNKS[2] - 1), ("SUB", 2, CHUNKS[2] - 1))
            put(0, *late.pop(c, []))
            if c < n and g < GROUPS:
                at = g * A_ITEMS[st] + (c % per) * share
                put(0, *[("A", st, at + i) for i in range(share)])
                if c % per == per - 1:
                    put(0, ("TM", st, g))
                    late.setdefault(c + 1, []).append(("T", st, g))
            if 1 <= c <= n:
                put(0, ("CAST", st, c - 1), ("SUB", st, c - 1))
            if st == 1 and c < AV_LAG:
                put(-1, ("AV", 2, CHUNKS[2] - AV_LAG + c))
                if c == AV_LAG - 1:
                    put(-1, ("AVE", 2, CHUNKS[2] // 4 - 1))
            for shift, step in extra.get(c, []):
                put(shift, step)
            done = c - AV_LAG
            if 0 <= done < n:
                put(0, ("AV", st, done))
                if st == 1:
                    put(0, ("AVE", 1, done))
                    if done % 4 == 3:
                        late.setdefault(c + 1, []).append(("R1", done // 4))
                        late.setdefault(c + 2, []).append(("R1B", done // 4))
                        late.setdefault(c + 3, []).append(("R1N", done // 4))
                elif done % 4 == 3:
                    put(0, ("AVE", 2, done // 4))
                    if done % 16 == 15:
                        late.setdefault(c + 1, []).append(("R2", done // 16))
            for shift, step in extra.get(c + 0.5, []):
                put(shift, step)

    first, second = {}, {}

    def at(table, c, shift, *steps):
        table.setdefault(c, []).extend((shift, s) for s in steps)

    at(first, 0, 0, ("QKD", 1))
    at(first, 2.5, 0, ("V2P", 0))
    at(first, 3, -1, ("R2", 1))
    at(first, 4.5, -1, ("OTP",))
    at(first, 5, -1, ("OT",))
    at(first, 6, -1, ("OTL",))
    for j in range(2):
        at(first, 3 + 2 * j, 0, ("V2", j))
        at(first, 4 + 2 * j, 0, ("V2L", j))
        at(first, 12 + j, 0, ("K2", j))
        at(first, 13 + j, 0, ("K2L", j))
    at(first, 4, 0, ("V2P", 1))
    at(first, 10.5, 0, ("K2P", 0))
    at(first, 7, -1, ("OP2P", 0, 0))
    at(first, 8, -1, ("OP2P", 0, 1))
    at(first, 9, -1, ("LN2",))
    at(first, 10, -1, ("LN2S",))
    at(first, 10.5, -1, ("LN2N",))
    at(first, 10.5, 0, ("LOADX",))
    at(first, 11, -1, ("FTP",))
    at(first, 12.5, 0, ("K2P", 1))
    at(first, 12, -1, ("FT",))
    at(first, 13, -1, ("FTL",))
    at(first, 15.5, -1, ("UGP", 0, 0))
    at(first, 16.5, -1, ("UGP", 0, 1))
    at(first, 18, -1, ("UG", 0))
    at(first, 18.5, -1, ("UGP", 1, 0), ("UGP", 1, 1))
    at(first, 20.5, -1, ("UG", 1), ("UL", 0), ("UGP", 2, 0), ("UGP", 2, 1))

    at(second, 0, 1, ("XT",))
    for p in range(D_PARTS):
        at(second, p, -1, ("DN", 0, p))
        at(second, 18 + p, -1, ("DN", 1, p))
    at(second, 4.5, -1, ("FV", 0))
    at(second, 19, -1, ("FN", 0))
    at(second, 22, -1, ("FV", 1), ("FN", 1))
    at(second, 2.5, 1, ("XS",))
    at(second, 3, 1, ("XSL",), ("XC",))
    at(second, 8.5, 1, ("CS",))
    at(second, 9, 1, ("CSL",))
    for j in range(KB):
        at(second, 6 + 3 * j, 1, ("QKP", j, 0))
        at(second, 7 + 3 * j, 1, ("QKP", j, 1))
        at(second, 7.5 + 3 * j, 1, ("QK", j))
        at(second, 8 + 3 * j, 1, ("QKL", j))
    for tb in range(TB):
        at(second, 23 + 3 * tb, 1, ("VVP", tb, 0))
        at(second, 24 + 3 * tb, 1, ("VVP", tb, 1))
        at(second, 24.5 + 3 * tb, 1, ("VV", tb))
        at(second, 25 + 3 * tb, 1, ("VVL", tb))
    at(second, 17, 1, ("QKD", 0))
    for g in range(LOOK[1]):
        for k in range(2):
            at(second, 24 + 2 * g + k, 1, *[("A", 1, g * A_ITEMS[1] + 2 * k + i) for i in range(2)])
        at(second, 25 + 2 * g, 1, ("TM", 1, g))
        at(second, 26 + 2 * g, 1, ("T", 1, g))

    attention(1, first)
    put(-1, ("UG", 2))
    put(0, ("ATP",), ("AT",))
    put(-1, ("UL", 1))
    put(0, ("ATL",))
    put(-1, ("UGP", 3, 0))
    put(0, ("OPP",))
    put(-1, ("UGP", 3, 1))
    put(0, ("LN1",), ("LN1S",))
    put(-1, ("UGP", 4, 0), ("UGP", 4, 1), ("UL", 2))
    put(0, ("LN1N",))
    put(-1, ("UG", 3))
    put(0, ("X1",), ("X1L",), ("Q2P",))
    put(-1, ("UG", 4), ("UL", 3), ("UGP", 5, 0), ("UGP", 5, 1))
    put(0, ("Q2",))
    put(-1, ("UL", 4))
    put(0, ("Q2L",))
    put(-1, ("UG", 5), ("UGP", 6, 0), ("UGP", 6, 1), ("UL", 5), ("UG", 6), ("UGP", 7, 0))
    put(0, *[("A", 2, i) for i in range(A_ITEMS[2])])
    put(0, ("TM", 2, 0), ("T", 2, 0))
    put(-1, ("UGP", 7, 1), ("UL", 6))
    for g in range(1, LOOK[2]):
        put(0, *[("A", 2, g * A_ITEMS[2] + i) for i in range(A_ITEMS[2])])
        put(0, ("TM", 2, g), ("T", 2, g))
    put(-1, ("UG", 7), ("UL", EB // 2 - 1))
    attention(2, second)
    return o, slot_b


B_PRODUCTS = ("ATP", "OPP", "Q2P", "OTP", "OP2P", "FTP", "UGP")
TWO_PARTS = ("OP2P", "UGP")
WEIGHTS_BEFORE = [("XSL",), ("QKL", 0), ("QKL", 1), ("QKD", 0)]
WEIGHTS = (2, 0, 1)
LOW = ("XSL", "CSL", "QKL", "VVL", "V2L", "K2L", "ATL", "OTL", "X1L", "Q2L", "FTL")
ORDER, SLOT_B = batch_order()
SHIFT = {s: shift for shift, s in ORDER}
assert len(SHIFT) == len(ORDER)
OWN = [s for shift in (1, 0, -1) for sh, s in ORDER if sh == shift]
RING_B = list(SLOT_B)
RING_F = [s for _, s in ORDER if s[0] in ("QKP", "VVP", "DN") and s[2] == 0 or s[0] in ("V2P", "K2P")]
RING_A = [s for s in OWN if s[0] in ("A", "T")]
AV_RING = [s for s in OWN if s[0] == "AVE"]
SUMS = [("R1", q) for q in range(4)] + [("R2", h) for h in range(2)]
assert len(RING_A) % 2 == 0 and len(SUMS) % 2 == 0
LINKS = {"TM": 1, "R1": 6, "R2": 1, "LN1": 2, "LN2": 2, "UG": 1, "FV": 2}


def item_of(s):
    return s[:2] if s[0] in TWO_PARTS else s


def item_before(ring, slots, it, s):
    n, looped = ring.index(s), not isinstance(it, int)

    def shift_of(t):
        return SHIFT[t] if t in SHIFT else SHIFT[(*t, 0)]

    for back in range(3):
        for t in reversed(ring[:n] if back == 0 else ring):
            if slots is not None and slots[t] != slots[s]:
                continue
            if looped:
                assert back == 0 or shift_of(t) >= 0
                return t, it + (shift_of(t) - back)
            if 0 <= it - back + shift_of(t) < NB:
                return t, it - back + shift_of(t)
    return None


def cast_on_act(st, c):
    return st == 1 or c % 8 != 5


def sub_on_pool(st, c):
    return c != 15 if st == 1 else c % 8 != 3


def sums_item(ave):
    _, st, i = ave
    return ("R1", i // 4) if st == 1 else ("R2", i // 4)


class Signal:

    def __init__(self, sem, keys, step=1, base=0):
        self.sem, self.step, self.keys, self.base = sem, step, list(keys), base
        self.place = {k: n + 1 for n, k in enumerate(self.keys)}
        assert len(self.place) == len(self.keys)

    def at(self, batch, key):
        return batch * (len(self.keys) * self.step) + (self.place[key] * self.step + self.base)


def decoder_kernel(nc, xT, x, ctx_in, wa, wx, w_ffn, sub_w, lam_in, b_qk, b_v, b_o, out):
    ctx = ExitStack()
    with ctx:
        def sb(name, shape, dt):
            return ctx.enter_context(nc.sbuf_tensor(name, shape, dt))

        def sem(name):
            return ctx.enter_context(nc.semaphore(name))

        area_ops = sb("area_ops", [P, 8192], f32)
        area_prob = sb("area_prob", [P, 8192], f32)
        area_act = sb("area_act", [P, 8192], f32)
        ops = area_ops[:, :].bitcast(f16)
        q_op, k_op = ops[:, 0:8192], ops[:, 8192:16384]
        prob32 = [area_prob[:, i * CHUNK:(i + 1) * CHUNK] for i in range(N32)]
        halves = area_prob[:, N32 * CHUNK:8192].bitcast(f16)
        prob_hi = [halves[:, 2 * i * CHUNK:(2 * i + 1) * CHUNK] for i in range(NPH)]
        prob_lo = [halves[:, (2 * i + 1) * CHUNK:(2 * i + 2) * CHUNK] for i in range(NPH)]
        hid_h = area_act[:, 0:2048].bitcast(f16)
        hid_l = area_act[:, 2048:4096].bitcast(f16)
        xr = area_act[:, 4096:5120].rearrange("p (b n) -> p b n", b=TB)
        x2 = area_act[:, 5120:6144].rearrange("p (b n) -> p b n", b=TB)
        attn = area_act[:, 6144:7168]
        work = area_act[:, 7168:8192]
        av = work[:, 512:1024]
        raw = [area_ops[:, :], area_prob[:, :], area_act[:, :]]

        w8 = sb("w8", [P, 3, 8192], f8)
        wa_h = sb("wa_h", [P, 4, KB, D], f16)
        wa_l = sb("wa_l", [P, 4, KB, D], f16)
        wx_h = sb("wx_h", [P, 4, TB, CH], f16)
        wx_l = sb("wx_l", [P, 4, TB, CH], f16)
        act_h = sb("act_h", [P, 1024], f16)
        act_l = sb("act_l", [P, 1024], f16)
        ctx_h = sb("ctx_h", [P, 1024], f16)
        ctx_l = sb("ctx_l", [P, 1024], f16)
        qk_h = sb("qk_h", [P, 2048], f16)
        qk_l = sb("qk_l", [P, 2048], f16)
        sums = sb("sums", [P, 2, 1056], f32)
        v1 = sb("v1", [P, TB * HEADS, 65], f16)
        v2 = sb("v2", [P, KB * HEADS, 33], f16)
        fx_h = sb("fx_h", [P, 1024], f16)
        fx_l = sb("fx_l", [P, 1024], f16)
        tanh_b = sb("tanh_b", [P, 2, 256], f32)
        hid32 = sb("hid32", [P, 2, 2, 256], f32)
        ones = act_h[:, 0:2 * P].bitcast(f32)
        stage = hid32[:, :, :, :].rearrange("p a b c -> p (a b c)")
        ident = sb("ident", [P, P], f32)
        ident16 = sb("ident16", [P, P], f16)
        bv_row = sb("bv_row", [P, CH], f32)
        mcol = sb("mcol", [P, NG, 8], f32)
        mhl = sb("mhl", [P, NG, 16], f16)
        mrow = sb("mrow", [16, NG, P], f16)
        rec = sb("rec", [P, 32], f32)
        msq = sb("msq", [P, 8], f32)
        rrms = sb("rrms", [P, 2, 8], f32)
        stats = sb("stats", [P, 2, TB, 6], f32)
        mv = sb("mv", [P, 2, TB, 2], f32)
        var = sb("var", [P, 2, TB], f32)
        rstd = sb("rstd", [P, 2, TB], f32)
        small = sb("small", [P, 32], f32)
        neg_half = small[:, 0:8]
        b_qk_sb = small[:, 8:12]
        b_o_sb = small[:, 12:14]
        sub_sb = small[:, 14:15]
        w_sc = small[:, 15:18]
        half_sc = small[:, 18:21]
        nhalf_sc = small[:, 21:24]
        asum = small[:, 24:27]
        nlam = small[:, 27:28]
        down_sc = small[:, 28:29]
        lam2 = small[:, 29:31]
        sub_s = small[:, 31:32]
        wait_col = sb("wait_col", [P, 2], f32)
        lam_sb = sb("lam_sb", [P, 64], f32)

        ps_a = ctx.enter_context(nc.psum_tensor("ps_a", [P, 2, 512], f32))
        ps_b = ctx.enter_context(nc.psum_tensor("ps_b", [P, 2, 1024], f32))
        ps_v = ctx.enter_context(nc.psum_tensor("ps_v", [P, 512], f32))
        ps_f = ctx.enter_context(nc.psum_tensor("ps_f", [P, 512], f32))
        slot_a = {s: n % 2 for n, s in enumerate(RING_A)}

        def bank_a(s):
            return ps_a[:, slot_a[s], :]

        def bank_b(s):
            return ps_b[:, SLOT_B[item_of(s)], :]

        def keys(*kinds):
            return [s for s in OWN if s[0] in kinds]

        chunks = keys("S")
        s_w = [sem(f"s_weights{i}") for i in range(4)]
        s_const = sem("s_const")
        s_set = sem("s_set")
        s_set_act = sem("s_set_act")
        s_set_pe = sem("s_set_pe")
        s_asum = sem("s_asum")
        s_chain = sem("s_chain")
        s_set_pool = sem("s_set_pool")
        xt_in = Signal(sem("xt_in"), ["x"], 16)
        ctx_loaded = Signal(sem("ctx_loaded"), ["x"], 16)
        x_in = Signal(sem("x_in"), ["x"], 16)
        ops1_in = [Signal(sem(f"ops1_in{i}"), ["x"], 128) for i in range(2)]
        ops2_in = Signal(sem("ops2_in"), ["x"], 128)
        max_in = [Signal(sem(f"max_in{i}"), [(st, g) for st in (1, 2) for g in range(i, GROUPS, NG)], 16)
                  for i in range(NG)]
        stored = Signal(sem("stored"), [0, 1], 16, base=16)
        a_full = Signal(sem("a_full"), RING_A)
        a_free = Signal(sem("a_free"), RING_A)
        scores_full = Signal(sem("scores_full"), chunks)
        b_full = Signal(sem("b_full"), [("ATP",), ("OPP",), ("Q2P",), ("OTP",), ("OP2P", 0, 1)])
        proj_full = Signal(sem("proj_full"), [s for s in keys("QKP", "VVP") if s[2] == 1])
        ctx_full = Signal(sem("ctx_full"), keys("V2P", "K2P"))
        exp_done = Signal(sem("exp_done"), chunks)
        av_full = Signal(sem("av_full"), keys("AV"))
        av_free = Signal(sem("av_free"), AV_RING)
        sums_read = Signal(sem("sums_read"), SUMS)
        hi_done = Signal(sem("hi_done"), keys("AT", "X1", "Q2", "OT"))
        lo_done = Signal(sem("lo_done"), keys("AT", "X1", "Q2", "OT"))
        x_hi = Signal(sem("x_hi"), keys("XS", "CS", "QK", "VV"))
        x_lo = Signal(sem("x_lo"), keys("XS", "CS"))
        vv_lo = Signal(sem("vv_lo"), keys("VV"))
        qk_lo = Signal(sem("qk_lo"), keys("QK"))
        ctx_hi = Signal(sem("ctx_hi"), keys("V2", "K2"))
        ctx_lo = Signal(sem("ctx_lo"), keys("V2", "K2"))
        ctx_value = Signal(sem("ctx_value"), keys("V2", "K2"))
        full_done = Signal(sem("full_done"), keys("Q2"))
        y_done = Signal(sem("y_done"), [("LN1",), ("LN2",)])
        cast_act = Signal(sem("cast_act"), [s for s in keys("CAST") if cast_on_act(*s[1:])])
        cast_dve = Signal(sem("cast_dve"), [s for s in keys("CAST") if not cast_on_act(*s[1:])])
        sub_pool = Signal(sem("sub_pool"), [s for s in keys("SUB") if sub_on_pool(*s[1:])])
        sub_dve = Signal(sem("sub_dve"), [s for s in keys("SUB") if not sub_on_pool(*s[1:])])
        max_split = Signal(sem("max_split"), keys("TM"))
        ms_done = Signal(sem("ms_done"), keys("R1"))
        rms_done = Signal(sem("rms_done"), keys("R1"))
        attn_done = Signal(sem("attn_done"), keys("R1N", "R2"))
        var_done = Signal(sem("var_done"), [("LN1",), ("LN2",)])
        rstd_done = Signal(sem("rstd_done"), [("LN1",), ("LN2",)])
        norm_done = Signal(sem("norm_done"), [("LN1",), ("LN2",)])
        link = Signal(sem("link"), [(s, k) for s in keys("R1", "R2") for k in range(LINKS[s[0]])])
        split_link = Signal(sem("split_link"), [(s, 0) for s in keys("TM")])
        norm_link = Signal(sem("norm_link"), [((n,), k) for n in ("LN1", "LN2") for k in range(2)])

        f_full = Signal(sem("f_full"), [("FTP",)] + [("UGP", e, 1) for e in range(EB // 2)])
        down_full = Signal(sem("down_full"), range(TB))
        fx_hi = Signal(sem("fx_hi"), [("FT",)])
        fx_lo = Signal(sem("fx_lo"), [("FT",)])
        tanh_done = Signal(sem("tanh_done"), range(EB // 2))
        hid_done = Signal(sem("hid_done"), range(EB // 2))
        hid_hi = Signal(sem("hid_hi"), range(EB // 2))
        hid_lo = Signal(sem("hid_lo"), range(EB // 2))
        fy_done = Signal(sem("fy_done"), range(TB))
        fvar_done = Signal(sem("fvar_done"), range(TB))
        frstd_done = Signal(sem("frstd_done"), range(TB))
        f_out = Signal(sem("f_out"), range(TB))
        flink = Signal(sem("flink"), [(s, k) for s in keys("UG", "FV") for k in range(LINKS[s[0]])])

        def cast_of(st, c):
            return (cast_act if cast_on_act(st, c) else cast_dve), ("CAST", st, c)

        def sub_of(st, c):
            return (sub_pool if sub_on_pool(st, c) else sub_dve), ("SUB", st, c)

        def b_release(item):
            taken = (item[0][:-1], *item[1:])
            return {"S": (exp_done, item), "OPP": (y_done, ("LN1",)), "OP2P": (y_done, ("LN2",)),
                    "Q2P": (full_done, taken), "FTP": (fx_lo, taken), "UGP": (hid_done, item[1:2] and item[1])}\
                .get(item[0], (lo_done, taken))

        def f_release(item):
            taken = (item[0][:-1], item[1])
            return {"DN": (fy_done, item[1]), "V2P": (ctx_value, taken), "K2P": (ctx_value, taken), "QKP": (qk_lo, taken)}\
                .get(item[0], (vv_lo, taken))

        def wait_last(eng, signal, batch, key):
            if not isinstance(batch, int) or batch > 0:
                eng.wait_ge(signal.sem, signal.at(batch - 1, key))

        def chunk_index(st, c):
            return c if st == 1 else CHUNKS[1] + c

        def chunk_before(st, c, n):
            i = chunk_index(st, c) - n
            if i < 0:
                i += len(chunks)
                return (chunks[i][1], chunks[i][2]), False
            return (chunks[i][1], chunks[i][2]), True

        def up_of(s):
            return bank_b(product_of(s)).rearrange("p (j w t) -> p j w t", j=2, w=2)[:, :, 0, :]

        def gate_of(s):
            return bank_b(product_of(s)).rearrange("p (j w t) -> p j w t", j=2, w=2)[:, :, 1, :]

        block = ctx.enter_context(nc.Block())

        def run(eng, step, feed_forward_weights):
            def iteration(it):
                for shift, s in ORDER:
                    if isinstance(it, int) and it < 0 and s in WEIGHTS_BEFORE:
                        feed_forward_weights(WEIGHTS_BEFORE.index(s))
                    if not isinstance(it, int) or 0 <= it + shift < NB:
                        step(it + shift, s)

            iteration(-1)
            iteration(0)
            with eng.Fori(1, NB - 1) as it:
                iteration(it)
            iteration(NB - 1)
            iteration(NB)

        @block.sync
        def _(sp):
            def load_xt(b):
                sp.dma_start(stage.rearrange("p (k t) -> p k t", k=KB), xT[b, :, :, :]).then_inc(xt_in.sem, 16)

            sp.dma_start(raw[0], wa).then_inc(s_w[0], 16)
            sp.dma_start(raw[1][:, 0:2048], wx).then_inc(s_w[0], 16)
            sp.dma_start(sub_sb, sub_w).then_inc(s_const, 16)
            load_xt(0)
            sp.dma_start(b_qk_sb, b_qk).then_inc(s_const, 16)
            sp.dma_start(b_o_sb, b_o).then_inc(s_const, 16)
            sp.dma_start(bv_row[:, :], b_v.partition_broadcast(P)).then_inc(s_const, 16)
            sp.dma_start(lam_sb[:, :], lam_in.partition_broadcast(P)).then_inc(s_const, 16)
            sp.dma_start(raw[2], w_ffn[2]).then_inc(s_w[3], 16)
            sp.wait_ge(s_set, 1)
            sp.dma_start(raw[0], w_ffn[0]).then_inc(s_w[1], 16)
            sp.wait_ge(s_set, 2)
            sp.dma_start(raw[1], w_ffn[1]).then_inc(s_w[2], 16)

            def feed_forward_weights(n):
                if n == 3:
                    sp.wait_ge(s_set, 6)

            def step(b, s):
                if s[0] == "XT":
                    if isinstance(b, int) and b == 0:
                        return
                    if not isinstance(b, int) or b >= 2:
                        sp.wait_ge(hid_lo.sem, hid_lo.at(b - 2, EB // 2 - 1))
                    else:
                        wait_last(sp, x_lo, b, ("CS",))
                    load_xt(b)
                elif s[0] == "XC":
                    sp.wait_ge(x_lo.sem, x_lo.at(b, ("XS",)))
                    sp.dma_start(stage.rearrange("p (k t) -> p k t", k=TB),
                                 ctx_in[b, :, :].rearrange("(k p) t -> p k t", p=P)).then_inc(ctx_loaded.sem, 16)
                elif s[0] == "LOADX":
                    wait_last(sp, norm_done, b, ("LN2",))
                    sp.dma_start(xr, x[b, :, :].rearrange("(k p) t -> p k t", p=P)).then_inc(x_in.sem, 16)
                elif s[0] == "QKD":
                    i = s[1]
                    if not isinstance(b, int) or b > 0:
                        wait_last(sp, scores_full, b, ("S", 2, (i + 1) * CHUNKS[2] // 2 - 1))
                    elif i == 0:
                        sp.wait_ge(s_set_pool, 7)
                    sp.wait_ge(qk_lo.sem, qk_lo.at(b, ("QK", 2 * i + 1)))
                    for which, op in ((0, q_op), (1, k_op)):
                        for r, half in enumerate((qk_h, qk_l, qk_h, qk_l) if which == 0 else (qk_h, qk_l, qk_l, qk_h)):
                            src = half[:, i * 1024:(i + 1) * 1024].rearrange("p (c w t) -> p c w t", c=2, w=2)
                            sp.dma_start(op[16 * r:16 * r + 16, i * 4096:(i + 1) * 4096], src[:, :, which, :])\
                                .then_inc(ops1_in[i].sem, 16)
                elif s[0] == "Q2":
                    for r, half in ((0, qk_h), (2, qk_h), (1, qk_l), (3, qk_l)):
                        if r == 0:
                            sp.wait_ge(hi_done.sem, hi_done.at(b, s))
                        elif r == 1:
                            sp.wait_ge(lo_done.sem, lo_done.at(b, s))
                        sp.dma_start(q_op[16 * r:16 * r + 16, :], half[:, 0:1024].rearrange("p (c t) -> p c t", c=2))\
                            .then_inc(ops2_in.sem, 16)
                elif s[0] == "AT":
                    sp.wait_ge(scores_full.sem, scores_full.at(b, ("S", 1, CHUNKS[1] - 1)))
                    sp.wait_ge(ctx_lo.sem, ctx_lo.at(b, ("K2", 1)))
                    for r, half in enumerate((qk_h, qk_l, qk_l, qk_h)):
                        sp.dma_start(k_op[16 * r:16 * r + 16, :], half[:, 1024:2048].rearrange("p (c t) -> p c t", c=2))\
                            .then_inc(ops2_in.sem, 16)
                elif s[0] == "T":
                    st, g = s[1], s[2]
                    sp.wait_ge(a_free.sem, a_free.at(b, s))
                    sp.dma_start(q_op[96:98, g * GCOLS:(g + 1) * GCOLS], mrow[:, g % NG, :])\
                        .then_inc(max_in[g % NG].sem, 16)
                elif s[0] == "FN":
                    tb = s[1]
                    sp.wait_ge(f_out.sem, f_out.at(b, tb))
                    sp.dma_start(out[b, tb * P:(tb + 1) * P, :], x2[:, tb, :]).then_inc(stored.sem, 16)

            run(sp, step, feed_forward_weights)
            sp.wait_ge(stored.sem, stored.at(NB - 1, 1))

        @block.tensor
        def _(pe):
            pe.wait_ge(s_set_pool, 3)
            def feed_forward_weights(n):
                if n < 3:
                    pe.wait_ge(s_asum, n + 1)
                    pe.matmul(ps_a[:, 0, n:n + 1], ones, asum[:, WEIGHTS[n]:WEIGHTS[n] + 1], start=True, stop=True)\
                        .then_inc(s_set_pe, 1)

            def product(dst, lhs, rhs, blocks, n):
                for k in blocks:
                    (lh, ll), (rh, rl) = lhs(k), rhs(k)
                    for j, (a, c) in enumerate(((lh, rh), (lh, rl), (ll, rh))):
                        last = pe.matmul(dst, a, c, start=k == 0 and j == 0, stop=k == n - 1 and j == 2)
                return last

            def b_slot(b, s):
                before = item_before(RING_B, SLOT_B, b - SHIFT[s], item_of(s))
                if before:
                    signal, key = b_release(before[0])
                    pe.wait_ge(signal.sem, signal.at(before[1], key))

            def f_slot(b, s):
                before = item_before(RING_F, None, b - SHIFT[s], s)
                if before:
                    signal, key = f_release(before[0])
                    pe.wait_ge(signal.sem, signal.at(before[1], key))

            def a_slot(b, s):
                n = RING_A.index(s)
                if n >= 2:
                    pe.wait_ge(a_free.sem, a_free.at(b, RING_A[n - 2]))
                else:
                    wait_last(pe, a_free, b, RING_A[n - 2])

            def take_wait(dst):
                pe.matmul(dst, ident16[:, :], ident16[:, 0:1], start=True, stop=True)

            def step(b, s):
                kind = s[0]
                if kind in B_PRODUCTS or kind == "S":
                    dst = bank_b(s)
                    if s[2:] != (1,) or kind == "S":
                        b_slot(b, s)
                if kind == "QKP":
                    j, w = s[1], s[2]
                    if w == 0:
                        f_slot(b, s)
                        if j == 0:
                            pe.wait_ge(x_lo.sem, x_lo.at(b, ("XS",)))
                    last = product(ps_f[:, w * T:(w + 1) * T],
                                   lambda k: (wa_h[:, w, k, j * P:(j + 1) * P], wa_l[:, w, k, j * P:(j + 1) * P]),
                                   lambda k: (fx_h[:, k * T:(k + 1) * T], fx_l[:, k * T:(k + 1) * T]), range(KB), KB)
                    if w == 1:
                        last.then_inc(proj_full.sem, 1)
                elif kind == "VVP":
                    tb, part = s[1], s[2]
                    if part == 0:
                        f_slot(b, s)
                    last = product(ps_f[:, :],
                                   lambda k: (fx_h[:, k * T + tb * P:k * T + tb * P + P], fx_l[:, k * T + tb * P:k * T + tb * P + P]),
                                   lambda k: (wa_h[:, 2, k, :], wa_l[:, 2, k, :]), range(2 * part, 2 * part + 2), KB)
                    if part == 1:
                        last.then_inc(proj_full.sem, 1)
                elif kind == "V2P":
                    f_slot(b, s)
                    if s[1] == 0:
                        pe.wait_ge(x_lo.sem, x_lo.at(b, ("CS",)))
                    for i in range(2):
                        tb = 2 * s[1] + i
                        last = product(ps_f[:, i * 256:(i + 1) * 256],
                                       lambda k: (ctx_h[:, k * D + tb * P:k * D + tb * P + P], ctx_l[:, k * D + tb * P:k * D + tb * P + P]),
                                       lambda k: (wx_h[:, 2, k, :], wx_l[:, 2, k, :]), range(TB), TB)
                    last.then_inc(ctx_full.sem, 1)
                elif kind == "K2P":
                    f_slot(b, s)
                    ob = s[1]
                    last = product(ps_f[:, :],
                                   lambda k: (wx_h[:, 1, k, ob * P:(ob + 1) * P], wx_l[:, 1, k, ob * P:(ob + 1) * P]),
                                   lambda k: (ctx_h[:, k * D:(k + 1) * D], ctx_l[:, k * D:(k + 1) * D]), range(TB), TB)
                    last.then_inc(ctx_full.sem, 1)
                elif kind in ("Q2P", "OP2P"):
                    w, src = (0, ("X1",)) if kind == "Q2P" else (3, ("OT",))
                    if kind == "Q2P" or s[2] == 0:
                        pe.wait_ge(lo_done.sem, lo_done.at(b, src))
                        pe.wait_ge(hi_done.sem, hi_done.at(b, src))
                    for ob in range(TB) if kind == "Q2P" else (s[2],):
                        last = product(dst[:, ob * 512:(ob + 1) * 512],
                                       lambda k: (wx_h[:, w, k, ob * P:(ob + 1) * P], wx_l[:, w, k, ob * P:(ob + 1) * P]),
                                       lambda k: (act_h[:, k * D:(k + 1) * D], act_l[:, k * D:(k + 1) * D]), range(TB), TB)
                    if kind == "Q2P" or s[2] == 1:
                        last.then_inc(b_full.sem, 1)
                elif kind == "A":
                    st, i = s[1], s[2]
                    a_slot(b, s)
                    if st == 1 and i % 16 == 0:
                        pe.wait_ge(ops1_in[i // 16].sem, ops1_in[i // 16].at(b, "x"))
                    if st == 2 and i == 0:
                        pe.wait_ge(ops2_in.sem, ops2_in.at(b, "x"))
                    bank = bank_a(s)
                    if st == 1:
                        for tb in range(TB):
                            last = pe.matmul(bank[:, tb * T:(tb + 1) * T],
                                             q_op[0:ROWS_A, i * T + tb * P:i * T + tb * P + P],
                                             k_op[0:ROWS_A, i * T:(i + 1) * T], start=True, stop=True)
                    else:
                        h = i // KB
                        last = pe.matmul(bank, q_op[0:ROWS_A, i * P:(i + 1) * P],
                                         k_op[0:ROWS_A, h * D:(h + 1) * D], start=True, stop=True)
                    last.then_inc(a_full.sem, 1)
                elif kind == "T":
                    st, g = s[1], s[2]
                    a_slot(b, s)
                    pe.wait_ge(max_split.sem, max_split.at(b, ("TM", st, g)))
                    pe.transpose(bank_a(s).bitcast(f16)[0:16, 0:P], mhl[:, g % NG, :], ident16[:, :])\
                        .then_inc(a_full.sem, 1)
                elif kind == "S":
                    st, c = s[1], s[2]
                    g = c // PER_GROUP[st]
                    if c % PER_GROUP[st] == 0:
                        pe.wait_ge(max_in[g % NG].sem, max_in[g % NG].at(b, (st, g)))
                    for j in range(2):
                        if st == 1:
                            m = 2 * c + j
                            for kb in range(TB):
                                last = pe.matmul(dst[:, j * 512 + kb * T:j * 512 + (kb + 1) * T],
                                                 k_op[0:ROWS_B, m * T + kb * P:m * T + kb * P + P],
                                                 q_op[0:ROWS_B, m * T:(m + 1) * T], start=True, stop=True)
                        else:
                            h, kb = c // 2, 2 * (c % 2) + j
                            last = pe.matmul(dst[:, j * 512:(j + 1) * 512],
                                             k_op[0:ROWS_B, h * D + kb * P:h * D + kb * P + P],
                                             q_op[0:ROWS_B, h * D:(h + 1) * D], start=True, stop=True)
                    last.then_inc(scores_full.sem, 1)
                elif kind == "AV":
                    st, c = s[1], s[2]
                    first = st == 1 or c % 4 == 0
                    if first:
                        n = AV_RING.index(("AVE", st, c if st == 1 else c // 4))
                        if n >= 1:
                            pe.wait_ge(av_free.sem, av_free.at(b, AV_RING[n - 1]))
                        else:
                            wait_last(pe, av_free, b, AV_RING[-1])
                    if c == 0:
                        signal, key = (vv_lo, ("VV", TB - 1)) if st == 1 else (ctx_lo, ("V2", 1))
                        pe.wait_ge(signal.sem, signal.at(b, key))
                    signal, key = cast_of(st, c)
                    pe.wait_ge(signal.sem, signal.at(b, key))
                    signal, key = sub_of(st, c)
                    pe.wait_ge(signal.sem, signal.at(b, key))
                    buf = chunk_index(st, c) % NPH
                    start = first
                    for j in range(2):
                        for tb in range(TB if st == 1 else KB):
                            for kb in range(TB if st == 1 else 1):
                                for part in (prob_hi, prob_lo):
                                    if st == 1:
                                        col, r = j * 512 + kb * T + tb * P, j * TB + tb
                                        rhs, width = v1[:, kb * HEADS + c, :], 65
                                    else:
                                        col, r = j * 512 + tb * P, ((c // 2) % 2) * KB + tb
                                        rhs, width = v2[:, (2 * (c % 2) + j) * HEADS + c // 2, :], 33
                                    last = pe.matmul(ps_v[:, r * width:(r + 1) * width], part[buf][:, col:col + P],
                                                     rhs, start=start, stop=True, skip_group_check=True)
                                    start = False
                    last.then_inc(av_full.sem, 1)
                elif kind == "ATP":
                    pe.wait_ge(attn_done.sem, attn_done.at(b, ("R1N", 3)))
                    for cb in range(KB):
                        for tb in range(TB):
                            last = pe.transpose(dst[:, cb * T + tb * P:cb * T + tb * P + P],
                                                attn[:, tb * D + cb * P:tb * D + cb * P + P], ident[:, :])
                    last.then_inc(b_full.sem, 1)
                elif kind == "OPP":
                    pe.wait_ge(lo_done.sem, lo_done.at(b, ("AT",)))
                    pe.wait_ge(hi_done.sem, hi_done.at(b, ("AT",)))
                    for tb in range(TB):
                        last = product(dst[:, tb * 512:(tb + 1) * 512],
                                       lambda k: (act_h[:, k * T + tb * P:k * T + tb * P + P], act_l[:, k * T + tb * P:k * T + tb * P + P]),
                                       lambda k: (wa_h[:, 3, k, :], wa_l[:, 3, k, :]), range(KB), KB)
                    last.then_inc(b_full.sem, 1)
                elif kind == "OTP":
                    pe.wait_ge(attn_done.sem, attn_done.at(b, ("R2", 1)))
                    for cb in range(TB):
                        for tb in range(KB):
                            last = pe.transpose(dst[:, cb * D + tb * P:cb * D + tb * P + P],
                                                attn[:, tb * CH + cb * P:tb * CH + cb * P + P], ident[:, :])
                    last.then_inc(b_full.sem, 1)

                elif kind == "FTP":
                    pe.wait_ge(norm_done.sem, norm_done.at(b, ("LN2",)))
                    for k in range(KB):
                        for tb in range(TB):
                            last = pe.transpose(dst[:, k * T + tb * P:k * T + tb * P + P],
                                                x2[:, tb, k * P:(k + 1) * P], ident[:, :])
                    last.then_inc(f_full.sem, 1)
                elif kind == "UGP":
                    if s[1:] == (0, 0):
                        pe.wait_ge(fx_lo.sem, fx_lo.at(b, ("FT",)))
                        pe.wait_ge(fx_hi.sem, fx_hi.at(b, ("FT",)))
                    j = s[2]
                    if j == 0:
                        take_wait(dst[:, 0:1])
                    e = 2 * s[1] + j
                    for w in range(2):
                        for k in range(KB):
                            for half in (fx_h, fx_l):
                                last = pe.matmul(dst[:, (2 * j + w) * T:(2 * j + w + 1) * T],
                                                 w8[:, w, k * E + e * P:k * E + e * P + P],
                                                 half[:, k * T:(k + 1) * T],
                                                 start=k == 0 and half is fx_h, stop=k == KB - 1 and half is fx_l)
                    if j == 1:
                        last.then_inc(f_full.sem, 1)
                elif kind == "DN":
                    tb, p = s[1], s[2]
                    n = EB // D_PARTS
                    if p == 0:
                        f_slot(b, s)
                        if tb == 0:
                            pe.wait_ge(hid_hi.sem, hid_hi.at(b, EB // 2 - 1))
                            pe.wait_ge(hid_lo.sem, hid_lo.at(b, EB // 2 - 1))
                        take_wait(ps_f[:, 0:1])
                    for e in range(p * n, (p + 1) * n):
                        for half in (hid_h, hid_l):
                            last = pe.matmul(ps_f[:, :], half[:, e * T + tb * P:e * T + tb * P + P],
                                             w8[:, 2, e * D:(e + 1) * D], start=e == 0 and half is hid_h,
                                             stop=e == EB - 1 and half is hid_l)
                    if p == D_PARTS - 1:
                        last.then_inc(down_full.sem, 1)

            run(pe, step, feed_forward_weights)

        @block.scalar
        def _(act):
            act.wait_ge(s_w[0], 32)
            act.wait_ge(s_const, 80)
            for w in range(4):
                src = raw[0][:, w * 2048:(w + 1) * 2048]
                dst = wa_h[:, w, :, :].rearrange("p k n -> p (k n)")
                if w == 3:
                    act.wait_ge(s_set_pool, 4)
                act.activation(dst, src, ACT.Copy, scale=sub_s if w == 3 else W_UP)
            act.activation(wx_h[:, :, :, :].rearrange("p w k n -> p (w k n)"), raw[1][:, 0:2048], ACT.Copy, scale=W_UP)\
                .then_inc(s_set_act, 1)
            act.wait_ge(s_set, 3)
            act.activation(lam2, lam2, ACT.Exp).then_inc(s_set_act, 1)

            def feed_forward_weights(n):
                pass

            def cast_chunk(eng, b, st, c):
                eng.wait_ge(exp_done.sem, exp_done.at(b, ("S", st, c)))
                before, same = chunk_before(st, c, NPH)
                if same:
                    eng.wait_ge(av_full.sem, av_full.at(b, ("AV", *before)))
                else:
                    wait_last(eng, av_full, b, ("AV", *before))
                i = chunk_index(st, c)
                return eng.activation(prob_hi[i % NPH], prob32[i % N32], ACT.Copy)

            def step(b, s):
                kind = s[0]
                if kind in ("XS", "CS"):
                    signal, dst = (xt_in, fx_h) if kind == "XS" else (ctx_loaded, ctx_h)
                    act.wait_ge(signal.sem, signal.at(b, "x"))
                    act.activation(dst[:, :], stage, ACT.Copy).then_inc(x_hi.sem, 1)
                elif kind == "QK":
                    act.wait_ge(proj_full.sem, proj_full.at(b, product_of(s)))
                    if s[1] == 0:
                        wait_last(act, ops2_in, b, "x")
                    act.activation(qk_h[:, s[1] * 512:(s[1] + 1) * 512], ps_f[:, :], ACT.Copy, scale=1 / W_UP)\
                        .then_inc(x_hi.sem, 1)
                elif kind == "VV":
                    act.wait_ge(proj_full.sem, proj_full.at(b, product_of(s)))
                    act.activation(v1[:, s[1] * HEADS:(s[1] + 1) * HEADS, 32:64], ps_f[:, :].rearrange("p (h e) -> p h e", e=32),
                                   ACT.Copy, scale=1 / W_UP).then_inc(x_hi.sem, 1)
                elif kind in ("V2", "K2"):
                    j = s[1]
                    act.wait_ge(ctx_value.sem, ctx_value.at(b, s))
                    if s == ("K2", 0):
                        act.wait_ge(ops1_in[1].sem, ops1_in[1].at(b, "x"))
                    src = work[:, j * 512:(j + 1) * 512]
                    if kind == "V2":
                        dst, src = v2[:, j * 32:(j + 1) * 32, 16:32], src.rearrange("p (h e) -> p h e", e=16)
                    else:
                        dst = qk_h[:, 1024 + j * 512:1536 + j * 512]
                    act.activation(dst, src, ACT.Copy).then_inc(ctx_hi.sem, 1)
                elif kind == "Q2":
                    act.wait_ge(full_done.sem, full_done.at(b, s))
                    act.activation(qk_h[:, 0:1024], work, ACT.Copy).then_inc(hi_done.sem, 1)
                elif kind in ("AT", "OT"):
                    act.wait_ge(b_full.sem, b_full.at(b, product_of(s)))
                    act.activation(act_h[:, :], bank_b(product_of(s)), ACT.Copy).then_inc(hi_done.sem, 1)
                elif kind == "X1":
                    act.wait_ge(norm_done.sem, norm_done.at(b, ("LN1",)))
                    act.activation(act_h[:, :], xr.rearrange("p b n -> p (b n)"), ACT.Copy).then_inc(hi_done.sem, 1)
                elif kind == "S":
                    st, c = s[1], s[2]
                    act.wait_ge(scores_full.sem, scores_full.at(b, s))
                    before, same = chunk_before(st, c, N32)
                    signal, key = sub_of(*before)
                    if same:
                        act.wait_ge(signal.sem, signal.at(b, key))
                    else:
                        wait_last(act, signal, b, key)
                    act.activation(prob32[chunk_index(st, c) % N32], bank_b(s), ACT.Exp, scale=SCALE)\
                        .then_inc(exp_done.sem, 1)
                elif kind == "CAST" and cast_on_act(*s[1:]):
                    st, c = s[1], s[2]
                    cast_chunk(act, b, st, c).then_inc(cast_act.sem, 1)
                elif kind == "AVE":
                    st, i = s[1], s[2]
                    act.wait_ge(av_full.sem, av_full.at(b, ("AV", st, i if st == 1 else 4 * i + 3)))
                    n = SUMS.index(sums_item(s))
                    if i % 4 == 0:
                        if n >= 2:
                            act.wait_ge(sums_read.sem, sums_read.at(b, SUMS[n - 2]))
                        else:
                            wait_last(act, sums_read, b, SUMS[n - 2])
                    width = 260 if st == 1 else 264
                    act.activation(sums[:, n % 2, (i % 4) * width:(i % 4 + 1) * width], ps_v[:, 0:width],
                                   ACT.Copy).then_inc(av_free.sem, 1)
                elif s[0] == "FT":
                    act.wait_ge(f_full.sem, f_full.at(b, product_of(s)))
                    act.activation(fx_h[:, :], bank_b(product_of(s)), ACT.Copy).then_inc(fx_hi.sem, 1)
                elif s[0] == "UG":
                    e = s[1]
                    act.wait_ge(f_full.sem, f_full.at(b, product_of(s)))
                    if e >= 1:
                        act.wait_ge(hid_done.sem, hid_done.at(b, e - 1))
                    act.activation(tanh_b[:, :, :], up_of(s), ACT.Tanh, scale=half_sc[:, 0:1]).then_inc(tanh_done.sem, 1)
                elif s[0] == "UL":
                    e = s[1]
                    act.wait_ge(hid_done.sem, hid_done.at(b, e))
                    act.activation(hid_h[:, e * 512:(e + 1) * 512], hid32[:, e % 2, :, :].rearrange("p j t -> p (j t)"),
                                   ACT.Copy).then_inc(hid_hi.sem, 1)

            run(act, step, feed_forward_weights)

        @block.gpsimd
        def _(pool):
            pool.memset(small[:, 0:8], -0.5)
            pool.memset(ones, 1.0)
            pool.memset(v1[:, :, 64:65], 1.0).then_inc(stored.sem, 16)
            pool.memset(v2[:, :, 32:33], 1.0)
            pool.memset(ident[:, :], 0.0)
            pool.memset(ident16[:, :], 0.0).then_inc(s_set_pool, 1)
            pool.wait_ge(s_set_pool, 1)
            for m in (ident, ident16):
                pool.affine_select(out=m[:, :], in_=m[:, :], compare_op=ALU.not_equal, fill=1.0, base=0,
                                   pattern=[[-1, P]], channel_multiplier=1).then_inc(s_set_pool, 1)
            pool.wait_ge(s_const, 80)
            pool.tensor_scalar(sub_s, sub_sb, W_UP * (1.0 - LAMBDA_INIT), None, ALU.mult).then_inc(s_set_pool, 1)
            def feed_forward_weights(n):
                if n == 2:
                    pool.wait_ge(s_set, 4)
                    pool.memset(q_op[64:96, :], 0.0).then_inc(s_set_pool, 1)
                    pool.memset(k_op[64:96, :], 0.0).then_inc(s_set_pool, 1)
                    pool.memset(k_op[96:98, :], -1.0).then_inc(s_set_pool, 1)

            def step(b, s):
                if s[0] == "SUB" and sub_on_pool(*s[1:]):
                    st, c = s[1], s[2]
                    signal, key = cast_of(st, c)
                    pool.wait_ge(signal.sem, signal.at(b, key))
                    i = chunk_index(st, c)
                    pool.tensor_tensor(prob_lo[i % NPH], prob32[i % N32], prob_hi[i % NPH], ALU.subtract)\
                        .then_inc(sub_pool.sem, 1)
                elif s[0] == "R1":
                    pool.wait_ge(ms_done.sem, ms_done.at(b, s))
                    pool.tensor_tensor(rrms[:, s[1] % 2, :], msq[:, :], neg_half, ALU.pow).then_inc(rms_done.sem, 1)
                elif s[0] in ("LN1", "LN2"):
                    pool.wait_ge(var_done.sem, var_done.at(b, s))
                    pool.tensor_tensor(rstd[:, 0, :], var[:, 0, :], neg_half[:, 0:2], ALU.pow).then_inc(rstd_done.sem, 1)
                elif s[0] == "FV":
                    tb = s[1]
                    pool.wait_ge(fvar_done.sem, fvar_done.at(b, tb))
                    pool.tensor_tensor(rstd[:, 1, tb:tb + 1], var[:, 1, tb:tb + 1], neg_half[:, 0:1], ALU.pow)\
                        .then_inc(frstd_done.sem, 1)

            run(pool, step, feed_forward_weights)

        @block.vector
        def _(dve):
            steps = [0]

            def setup_step(ins):
                steps[0] += 1
                ins.then_inc(s_set, 1)
                dve.wait_ge(s_set, steps[0])

            dve.wait_ge(s_set_act, 1)
            for w in range(4):
                src = raw[0][:, w * 2048:(w + 1) * 2048]
                hi = wa_h[:, w, :, :].rearrange("p k n -> p (k n)")
                lo = wa_l[:, w, :, :].rearrange("p k n -> p (k n)")
                last = dve.scalar_tensor_tensor(out=lo, in0=src, scalar=sub_s if w == 3 else W_UP, in1=hi,
                                                op0=ALU.mult, op1=ALU.subtract)
            setup_step(last)
            setup_step(dve.scalar_tensor_tensor(
                out=wx_l[:, :, :, :].rearrange("p w k n -> p (w k n)"), in0=raw[1][:, 0:2048], scalar=W_UP,
                in1=wx_h[:, :, :, :].rearrange("p w k n -> p (w k n)"), op0=ALU.mult, op1=ALU.subtract))
            dve.wait_ge(s_const, 80)
            lam = lam_sb[:, :].rearrange("p (s b d) -> p s b d", s=2, b=2)
            chain = [0]

            def chained(ins):
                chain[0] += 1
                ins.then_inc(s_chain, 1)
                dve.wait_ge(s_chain, chain[0])

            chained(dve.tensor_tensor(lam[:, 0, :, :], lam[:, 0, :, :], lam[:, 1, :, :], ALU.mult))
            setup_step(dve.tensor_reduce(lam2, lam[:, 0, :, :], AX.X, ALU.add))
            dve.wait_ge(s_set_act, 2)
            chained(dve.tensor_scalar(nlam, lam2[:, 1:2], LAMBDA_INIT, None, ALU.subtract))
            chained(dve.tensor_tensor(nlam, nlam, lam2[:, 0:1], ALU.subtract))
            def feed_forward_weights(n):
                if n < 3:
                    w = WEIGHTS[n]
                    dve.wait_ge(s_w[1 + w], 16)
                    dve.tensor_reduce(asum[:, w:w + 1], raw[w], AX.X, ALU.add, apply_absolute_value=True)\
                        .then_inc(s_asum, 1)
                    dve.wait_ge(s_set_pe, 1 + n)
                    chained(dve.tensor_scalar(w_sc[:, w:w + 1], ps_a[:, 0, n:n + 1], 1.0 / (D * E), Q_EPS, ALU.mult, ALU.add))
                    chained(dve.tensor_scalar(half_sc[:, w:w + 1], w_sc[:, w:w + 1], 0.5, None, ALU.mult))
                    chained(dve.tensor_scalar(nhalf_sc[:, w:w + 1], w_sc[:, w:w + 1], -0.5, None, ALU.mult))
                    chained(dve.tensor_scalar(w8[:, w, :], raw[w], nhalf_sc[:, w:w + 1], None, ALU.is_lt, saturate=False))
                    last = dve.scalar_tensor_tensor(out=w8[:, w, :], in0=raw[w], scalar=half_sc[:, w:w + 1],
                                                    in1=w8[:, w, :], op0=ALU.is_gt, op1=ALU.subtract, saturate=False)
                    if n == 1:
                        setup_step(last)
                    else:
                        chained(last)
                else:
                    chained(dve.tensor_tensor(down_sc, w_sc[:, 0:1], w_sc[:, 1:2], ALU.mult))
                    chained(dve.tensor_tensor(down_sc, down_sc, w_sc[:, 2:3], ALU.mult))
                    setup_step(dve.tensor_scalar(down_sc, down_sc, 8.0, None, ALU.mult))
                    setup_step(dve.memset(msq[:, :], 1.0))

            def linked(b, s, k, ins, signal=None):
                signal = signal or link
                ins.then_inc(signal.sem, 1)
                dve.wait_ge(signal.sem, signal.at(b, (s, k)))

            def layer_norm(b, s, k0, src, part, blocks, signal, ready):
                for tb in blocks:
                    last = dve.bn_stats(stats[:, part, tb, :], src[:, tb, :])
                linked(b, s, k0, last, signal)
                dve.memset(wait_col[:, part:part + 1], 0.0)
                for tb in blocks:
                    last = dve.bn_aggr(mv[:, part, tb, :], stats[:, part, tb, :])
                linked(b, s, k0 + 1, last, signal)
                dve.tensor_scalar(var[:, part, blocks[0]:blocks[-1] + 1], mv[:, part, blocks[0]:blocks[-1] + 1, 1],
                                  EPS, None, ALU.add).then_inc(ready.sem, 1)

            def block_norm(b, s):
                item = ("OPP",) if s[0] == "LN1" else ("OP2P", 0, 1)
                dve.wait_ge(b_full.sem, b_full.at(b, item))
                for tb in range(TB):
                    last = dve.scalar_tensor_tensor(out=xr[:, tb, :], in0=bank_b(item)[:, tb * 512:(tb + 1) * 512],
                                                    scalar=1 / W_UP, in1=xr[:, tb, :], op0=ALU.mult, op1=ALU.add)
                last.then_inc(y_done.sem, 1)

            def block_stats(b, s):
                s = (s[0][:-1],)
                dve.wait_ge(y_done.sem, y_done.at(b, s))
                layer_norm(b, s, 0, xr, 0, (0, 1), norm_link, var_done)

            def block_scale(b, s):
                dve.wait_ge(rstd_done.sem, rstd_done.at(b, (s[0][:-1],)))
                if s[0] == "LN2N":
                    wait_last(dve, stored, b, 1)
                dst = xr if s[0] == "LN1N" else x2
                for tb in range(TB):
                    last = dve.tensor_scalar(dst[:, tb, :], xr[:, tb, :], mv[:, 0, tb, 0:1], rstd[:, 0, tb:tb + 1],
                                             ALU.subtract, ALU.mult)
                last.then_inc(norm_done.sem, 1)

            def attn_heads(q):
                return attn.rearrange("p (t h e) -> p t h e", t=TB, h=HEADS)[:, :, 4 * q:4 * q + 4, :]

            def step(b, s):
                kind = s[0]
                low = kind in LOW
                if low:
                    kind, s = kind[:-1], (kind[:-1], *s[1:])
                if kind in ("XS", "CS", "QK", "VV") and low:
                    dve.wait_ge(x_hi.sem, x_hi.at(b, s))
                    if kind == "XS":
                        ins = dve.tensor_tensor(fx_l[:, :], stage, fx_h[:, :], ALU.subtract)
                    elif kind == "CS":
                        ins = dve.tensor_tensor(ctx_l[:, :], stage, ctx_h[:, :], ALU.subtract)
                    elif kind == "QK":
                        cols = slice(s[1] * 512, (s[1] + 1) * 512)
                        ins = dve.scalar_tensor_tensor(out=qk_l[:, cols], in0=ps_f[:, :], scalar=1 / W_UP,
                                                       in1=qk_h[:, cols], op0=ALU.mult, op1=ALU.subtract)
                    else:
                        rows = slice(s[1] * HEADS, (s[1] + 1) * HEADS)
                        ins = dve.scalar_tensor_tensor(out=v1[:, rows, 0:32], in0=ps_f[:, :].rearrange("p (h e) -> p h e", e=32),
                                                       scalar=1 / W_UP, in1=v1[:, rows, 32:64], op0=ALU.mult, op1=ALU.subtract)
                    ins.then_inc({"QK": qk_lo, "VV": vv_lo}.get(kind, x_lo).sem, 1)
                elif kind in ("V2", "K2"):
                    j = s[1]
                    value = work[:, j * 512:(j + 1) * 512]
                    if not low:
                        if kind == "V2":
                            wait_last(dve, attn_done, b, ("R2", 1))
                        else:
                            dve.wait_ge(ctx_lo.sem, ctx_lo.at(b, ("V2", j)))
                        dve.wait_ge(ctx_full.sem, ctx_full.at(b, product_of(s)))
                        if kind == "V2":
                            ins = dve.scalar_tensor_tensor(
                                out=value.rearrange("p (k n) -> p k n", k=2), in0=ps_f[:, :].rearrange("p (k n) -> p k n", k=2),
                                scalar=1 / W_UP, in1=bv_row[:, :].unsqueeze(1).to_broadcast([P, 2, CH]),
                                op0=ALU.mult, op1=ALU.add)
                        else:
                            ins = dve.tensor_scalar(value, ps_f[:, :], 1 / W_UP, b_qk_sb[:, TB + j:TB + j + 1], ALU.mult, ALU.add)
                        ins.then_inc(ctx_value.sem, 1)
                    else:
                        dve.wait_ge(ctx_hi.sem, ctx_hi.at(b, s))
                        if kind == "V2":
                            rows = slice(j * 32, (j + 1) * 32)
                            ins = dve.tensor_tensor(v2[:, rows, 0:16], value.rearrange("p (h e) -> p h e", e=16),
                                                    v2[:, rows, 16:32], ALU.subtract)
                        else:
                            cols = slice(1024 + j * 512, 1536 + j * 512)
                            ins = dve.tensor_tensor(qk_l[:, cols], value, qk_h[:, cols], ALU.subtract)
                        ins.then_inc(ctx_lo.sem, 1)
                elif kind == "Q2" and not low:
                    dve.wait_ge(b_full.sem, b_full.at(b, product_of(s)))
                    for ob in range(TB):
                        last = dve.tensor_scalar(work[:, ob * 512:(ob + 1) * 512],
                                                 bank_b(product_of(s))[:, ob * 512:(ob + 1) * 512],
                                                 1 / W_UP, b_qk_sb[:, ob:ob + 1], ALU.mult, ALU.add)
                    last.then_inc(full_done.sem, 1)
                elif kind in ("AT", "OT", "X1", "Q2") and low:
                    dve.wait_ge(hi_done.sem, hi_done.at(b, s))
                    if kind == "Q2":
                        ins = dve.tensor_tensor(qk_l[:, 0:1024], work, qk_h[:, 0:1024], ALU.subtract)
                    elif kind in ("AT", "OT"):
                        ins = dve.tensor_tensor(act_l[:, :], bank_b(product_of(s)), act_h[:, :], ALU.subtract)
                    else:
                        ins = dve.tensor_tensor(act_l[:, :], xr.rearrange("p b n -> p (b n)"), act_h[:, :], ALU.subtract)
                    ins.then_inc(lo_done.sem, 1)
                    if kind == "X1":
                        dve.wait_ge(lo_done.sem, lo_done.at(b, s))
                        for tb in range(TB):
                            dve.tensor_scalar(xr[:, tb, :], xr[:, tb, :], b_o_sb[:, tb:tb + 1], None, ALU.add)
                elif kind == "A":
                    st, i = s[1], s[2]
                    g, n = divmod(i, A_ITEMS[st])
                    dve.wait_ge(a_full.sem, a_full.at(b, s))
                    if st == 1:
                        dve.tensor_reduce(mcol[:, g % NG, 2 * n:2 * n + 2], bank_a(s).rearrange("p (t k) -> p t k", t=TB),
                                          AX.X, ALU.max).then_inc(a_free.sem, 1)
                    else:
                        dve.tensor_reduce(mcol[:, g % NG, n:n + 1], bank_a(s), AX.X, ALU.max).then_inc(a_free.sem, 1)
                elif kind == "TM":
                    st, g = s[1], s[2]
                    dve.wait_ge(a_free.sem, a_free.at(b, ("A", st, (g + 1) * A_ITEMS[st] - 1)))
                    linked(b, s, 0, dve.tensor_scalar(mhl[:, g % NG, 0:8], mcol[:, g % NG, :], -P_SHIFT, None, ALU.add), split_link)
                    dve.scalar_tensor_tensor(out=mhl[:, g % NG, 8:16], in0=mcol[:, g % NG, :], scalar=-P_SHIFT,
                                             in1=mhl[:, g % NG, 0:8], op0=ALU.add, op1=ALU.subtract)\
                        .then_inc(max_split.sem, 1)
                elif kind == "T":
                    st, g = s[1], s[2]
                    dve.wait_ge(a_full.sem, a_full.at(b, s))
                    dve.tensor_copy(mrow[:, g % NG, :], bank_a(s).bitcast(f16)[0:16, 0:P]).then_inc(a_free.sem, 1)
                elif kind == "CAST" and not cast_on_act(*s[1:]):
                    st, c = s[1], s[2]
                    dve.wait_ge(exp_done.sem, exp_done.at(b, ("S", st, c)))
                    before, same = chunk_before(st, c, NPH)
                    if same:
                        dve.wait_ge(av_full.sem, av_full.at(b, ("AV", *before)))
                    else:
                        wait_last(dve, av_full, b, ("AV", *before))
                    i = chunk_index(st, c)
                    dve.tensor_copy(prob_hi[i % NPH], prob32[i % N32]).then_inc(cast_dve.sem, 1)
                elif kind == "SUB" and not sub_on_pool(*s[1:]):
                    st, c = s[1], s[2]
                    signal, key = cast_of(st, c)
                    dve.wait_ge(signal.sem, signal.at(b, key))
                    i = chunk_index(st, c)
                    dve.tensor_tensor(prob_lo[i % NPH], prob32[i % N32], prob_hi[i % NPH], ALU.subtract)\
                        .then_inc(sub_dve.sem, 1)
                elif kind == "R1":
                    q = s[1]
                    if q in (0, 2):
                        dve.wait_ge(ctx_lo.sem, ctx_lo.at(b, ("K2" if q else "V2", 1)))
                    dve.wait_ge(av_free.sem, av_free.at(b, ("AVE", 1, 4 * q + 3)))
                    src = sums[:, SUMS.index(s) % 2, 0:1040].rearrange("p (r e) -> p r e", e=65)
                    r = rec[:, 0:16]
                    odd = r.rearrange("p (h two t) -> p h two t", h=4, two=2)[:, :, 1, :]
                    avr = av.rearrange("p (r e) -> p r e", e=32)
                    linked(b, s, 0, dve.reciprocal(r, src[:, :, 64]))
                    linked(b, s, 1, dve.tensor_scalar(odd, odd, nlam, None, ALU.mult))
                    dve.tensor_tensor(avr, src[:, :, 0:32], src[:, :, 32:64], ALU.add).then_inc(sums_read.sem, 1)
                    dve.wait_ge(sums_read.sem, sums_read.at(b, s))
                    linked(b, s, 2, dve.tensor_tensor(avr, avr, r.unsqueeze(2).to_broadcast([P, 16, 32]), ALU.mult))
                elif kind == "R1B":
                    q, s = s[1], ("R1", s[1])
                    pair = av.rearrange("p (h two t e) -> p t h two e", h=4, two=2, t=TB)
                    dst = attn_heads(q)
                    linked(b, s, 3, dve.tensor_tensor(dst, pair[:, :, :, 0, :], pair[:, :, :, 1, :], ALU.add))
                    sq = work[:, 0:256].rearrange("p (t h e) -> p t h e", t=TB, h=4)
                    linked(b, s, 4, dve.tensor_tensor(sq, dst, dst, ALU.mult))
                    linked(b, s, 5, dve.tensor_reduce(msq[:, :].rearrange("p (t h) -> p t h", t=TB), sq, AX.X, ALU.add))
                    dve.tensor_scalar(msq[:, :], msq[:, :], 1.0 / 32, EPS, ALU.mult, ALU.add).then_inc(ms_done.sem, 1)
                elif kind == "R1N":
                    q = s[1]
                    dve.wait_ge(rms_done.sem, rms_done.at(b, ("R1", q)))
                    dst = attn_heads(q)
                    dve.tensor_tensor(dst, dst, rrms[:, q % 2, :].rearrange("p (t h) -> p t h", t=TB).unsqueeze(3)
                                      .to_broadcast([P, TB, 4, 32]), ALU.mult).then_inc(attn_done.sem, 1)
                elif kind == "R2":
                    half = s[1]
                    if half == 0:
                        dve.wait_ge(lo_done.sem, lo_done.at(b, ("Q2",)))
                    else:
                        dve.wait_ge(attn_done.sem, attn_done.at(b, ("R2", 0)))
                    dve.wait_ge(av_free.sem, av_free.at(b, ("AVE", 2, 4 * half + 3)))
                    src = sums[:, SUMS.index(s) % 2, :].rearrange("p (r e) -> p r e", e=33)
                    r = rec[:, :]
                    linked(b, s, 0, dve.reciprocal(r, src[:, :, 32]))
                    dve.tensor_tensor(av.rearrange("p (r e) -> p r e", e=16), src[:, :, 0:16], src[:, :, 16:32], ALU.add)\
                        .then_inc(sums_read.sem, 1)
                    dve.wait_ge(sums_read.sem, sums_read.at(b, s))
                    dst = attn.rearrange("p (t h e) -> p t h e", t=KB, h=HEADS)[:, :, 8 * half:8 * half + 8, :]
                    dve.tensor_tensor(dst, av.rearrange("p (h t e) -> p t h e", h=8, t=KB),
                                      r.rearrange("p (h t) -> p t h", h=8).unsqueeze(3).to_broadcast([P, KB, 8, 16]),
                                      ALU.mult).then_inc(attn_done.sem, 1)
                elif kind in ("LN1", "LN2"):
                    if kind == "LN1":
                        dve.wait_ge(x_in.sem, x_in.at(b, "x"))
                    block_norm(b, s)
                elif kind in ("LN1S", "LN2S"):
                    block_stats(b, s)
                elif kind in ("LN1N", "LN2N"):
                    block_scale(b, s)
                elif kind == "FT" and low:
                    dve.wait_ge(fx_hi.sem, fx_hi.at(b, s))
                    dve.tensor_tensor(fx_l[:, :], bank_b(product_of(s)), fx_h[:, :], ALU.subtract).then_inc(fx_lo.sem, 1)
                elif kind == "UG":
                    e = s[1]
                    dve.wait_ge(tanh_done.sem, tanh_done.at(b, e))
                    if e >= 2:
                        dve.wait_ge(hid_lo.sem, hid_lo.at(b, e - 2))
                    elif not isinstance(b, int) or b < NB - 1:
                        dve.wait_ge(x_lo.sem, x_lo.at(b + 1, ("CS",)))
                    linked(b, s, 0, dve.scalar_tensor_tensor(out=hid32[:, e % 2, :, :], in0=tanh_b[:, :, :], scalar=1.0,
                                                             in1=up_of(s), op0=ALU.add, op1=ALU.mult), flink)
                    dve.scalar_tensor_tensor(out=hid32[:, e % 2, :, :], in0=gate_of(s), scalar=1.0 / 16,
                                             in1=hid32[:, e % 2, :, :], op0=ALU.mult, op1=ALU.mult)\
                        .then_inc(hid_done.sem, 1)
                elif kind == "UL":
                    e = s[1]
                    dve.wait_ge(hid_hi.sem, hid_hi.at(b, e))
                    dve.tensor_tensor(hid_l[:, e * 512:(e + 1) * 512], hid32[:, e % 2, :, :].rearrange("p j t -> p (j t)"),
                                      hid_h[:, e * 512:(e + 1) * 512], ALU.subtract).then_inc(hid_lo.sem, 1)
                elif kind == "FV":
                    tb = s[1]
                    dve.wait_ge(down_full.sem, down_full.at(b, tb))
                    dve.scalar_tensor_tensor(out=x2[:, tb, :], in0=ps_f[:, :], scalar=down_sc, in1=x2[:, tb, :],
                                             op0=ALU.mult, op1=ALU.add).then_inc(fy_done.sem, 1)
                    dve.wait_ge(fy_done.sem, fy_done.at(b, tb))
                    layer_norm(b, s, 0, x2, 1, (tb,), flink, fvar_done)
                elif kind == "FN":
                    tb = s[1]
                    dve.wait_ge(frstd_done.sem, frstd_done.at(b, tb))
                    dve.tensor_scalar(x2[:, tb, :], x2[:, tb, :], mv[:, 1, tb, 0:1], rstd[:, 1, tb:tb + 1],
                                      ALU.subtract, ALU.mult).then_inc(f_out.sem, 1)

            run(dve, step, feed_forward_weights)


def kernel(**inputs):
    import numpy as np
    import concourse.bacc as bacc
    from concourse.bass_utils import run_bass_kernel_spmd

    a = {k: np.asarray(v) for k, v in inputs.items()}

    def rows_first(w):
        wt = w.T
        n = wt.shape[0] // P
        return np.ascontiguousarray(wt.reshape(n, P, wt.shape[1]).transpose(1, 0, 2)).reshape(P, -1)

    def channel_order(matrices):
        order = np.empty((matrices // 8, HD, 8), np.int64)
        for cb in range(matrices // 8):
            for j in range(8):
                m = (cb // 2) * 16 + j * 2 + cb % 2
                order[cb, :, j] = m * HD + np.arange(HD)
        return order.reshape(-1)

    c1, c2 = channel_order(NM), channel_order(HEADS)
    L, X = "L0_attn_", "L0_xattn_"
    arrays = {
        "xT": np.ascontiguousarray(a["x"].transpose(0, 2, 1).reshape(NB, KB, P, T).transpose(0, 2, 1, 3)),
        "x": a["x"],
        "ctx_in": a["ctx_2048"],
        "wa": np.concatenate([rows_first(a[L + "Wq"][c1]), rows_first(a[L + "Wk"][c1]), rows_first(a[L + "Wv"]),
                              rows_first(a[L + "Wo"])], axis=1),
        "wx": np.concatenate([rows_first(a[X + "Wq"][c2]), rows_first(a[X + "Wk"][c2]), rows_first(a[X + "Wv"]),
                              rows_first(a[X + "Wo"])], axis=1),
        "w_ffn": np.stack([rows_first(a["L0_ffn_W_up"]), rows_first(a["L0_ffn_W_gate"]),
                           rows_first(a["L0_ffn_W_down"])]),
        "sub_w": np.tile(a[L + "subln_weight"], P // 32).reshape(P, 1),
        "lam_in": np.concatenate([a[L + "lambda_q1"], a[L + "lambda_q2"], a[L + "lambda_k1"], a[L + "lambda_k2"]]),
        "b_qk": np.ascontiguousarray(np.concatenate([a[X + "bq"][c2].reshape(TB, P).T, a[X + "bk"][c2].reshape(TB, P).T], axis=1)),
        "b_v": a[X + "bv"],
        "b_o": np.ascontiguousarray(a[X + "bo"].reshape(TB, P).T),
    }
    nc = bacc.Bacc("TRN2", target_bir_lowering=False, num_devices=1)
    args = [nc.dram_tensor(f"in_{k}", v.shape, f32, kind="ExternalInput").ap() for k, v in arrays.items()]
    args.append(nc.dram_tensor("out_0", (NB, T, D), f32, kind="ExternalOutput").ap())
    decoder_kernel(nc, *args)
    r = run_bass_kernel_spmd(nc, [{f"in_{k}": v for k, v in arrays.items()}], core_ids=[0])
    return r.results[0]["out_0"]
```
